# Optimizing a Trainium2 kernel written in Bass

```python
import numpy as np
import jax
import jax.numpy as jnp

def _softmax(x, axis=-1):
    return jax.nn.softmax(x, axis=axis)

def _gelu(x):
    return jax.nn.gelu(x, approximate=True)

def _silu(x):
    return jax.nn.silu(x)

def _sigmoid(x):
    return jax.nn.sigmoid(x)

def _layernorm(x, axis=-1, eps=1e-05):
    m = jnp.mean(x, axis=axis, keepdims=True)
    v = jnp.var(x, axis=axis, keepdims=True)
    return (x - m) / jnp.sqrt(v + eps)

def _scatter_add(tgt, idx, src, axis=0):
    return tgt.at[idx].add(src)

def _segment_sum(src, seg, n):
    return jax.ops.segment_sum(src, seg, n)
kernel_name = 'mk_adaln_attn_ffn_d1_seqx_r8_3fd736'

def setup_inputs(seed: int=0):
    np.random.seed(seed)
    _w = jnp.asarray

    def _rec_inputs():
        import jax
        import jax.numpy as jnp
        _rk = jax.random.key(seed)
        x = -1.394e-06 + 0.9999 * jax.random.normal(jax.random.fold_in(_rk, 1), (4, 256, 256), jnp.float32)
        _lenS = 256 - jax.random.randint(jax.random.fold_in(_rk, 7), (4,), 0, max(1, 256 // 4) + 1, jnp.int32)
        _lenS2 = 256 - jax.random.randint(jax.random.fold_in(_rk, 8), (4,), 0, max(1, 256 // 4) + 1, jnp.int32)
        cond_2048 = -0.00499425 + 1.0058 * jax.random.normal(jax.random.fold_in(_rk, 11), (4, 256), jnp.float32)
        return (x, cond_2048)
    x, cond_2048 = _rec_inputs()

    def _L0_cond_setup():
        import jax, jax.numpy as jnp
        import numpy as np
        B, T, D = (16, 128, 256)
        key = jax.random.key(seed)
        k0, k1, k2, k3 = jax.random.split(key, 4)
        scale = 1.0 / np.sqrt(D)
        return {'initial_state': jax.random.normal(k0, (B, D), jnp.float32), 'inputs': jax.random.normal(k1, (B, T, D), jnp.float32), 'W_ih': jax.random.normal(k2, (D, 3 * D), jnp.float32) * scale, 'W_hh': jax.random.normal(k3, (D, 3 * D), jnp.float32) * scale, 'b_ih': jnp.zeros((3 * D,), jnp.float32), 'b_hh': jnp.zeros((3 * D,), jnp.float32)}
    _L0_cond_all = _L0_cond_setup()
    _L0_cond_in = {k: v for k, v in _L0_cond_all.items() if k in ('W_ih', 'W_hh', 'b_ih', 'b_hh')}
    del _L0_cond_all

    def _L0_attn_setup():
        import jax, jax.numpy as jnp
        import numpy as np
        N_HEADS = 16
        D_HEAD = 128
        D_MODEL = 256
        MAXLEN = 256
        key = jax.random.key(seed)
        ks = jax.random.split(key, 9)
        b, t = (2, 256)
        hd = N_HEADS * D_HEAD
        init = 0.02
        return {'x': jax.random.normal(ks[0], (b, t, D_MODEL), dtype=jnp.float32), 'Wq': jax.random.normal(ks[1], (D_MODEL, hd), dtype=jnp.float32) * init, 'bq': jnp.zeros((hd,), dtype=jnp.float32), 'Wk': jax.random.normal(ks[2], (D_MODEL, hd), dtype=jnp.float32) * init, 'bk': jnp.zeros((hd,), dtype=jnp.float32), 'Wv': jax.random.normal(ks[3], (D_MODEL, hd), dtype=jnp.float32) * init, 'bv': jnp.zeros((hd,), dtype=jnp.float32), 'Wo': jax.random.normal(ks[4], (hd, D_MODEL), dtype=jnp.float32) * init, 'bo': jnp.zeros((D_MODEL,), dtype=jnp.float32)}
    _L0_attn_all = _L0_attn_setup()
    _L0_attn_in = {k: v for k, v in _L0_attn_all.items() if k in ('Wq', 'bq', 'Wk', 'bk', 'Wv', 'bv', 'Wo', 'bo')}
    del _L0_attn_all

    def _L0_cond2_setup():
        import jax, jax.numpy as jnp
        import numpy as np
        HEADS = 16
        EPS = 1e-06

        def _rms_norm(x, g):
            xf = x.astype(jnp.float32)
            y = xf * jax.lax.rsqrt(jnp.mean(xf * xf, axis=-1, keepdims=True) + EPS)
            return y.astype(x.dtype) * g
        key = jax.random.key(seed)
        ks = jax.random.split(key, 6)
        b, n, dim, emb_dim = (4, 256, 256, 256)
        d_head = dim // HEADS
        return {'x': jax.random.normal(ks[0], (b, n, dim), jnp.float32), 'emb': jax.random.normal(ks[1], (b, 1, emb_dim), jnp.float32), 'W_emb': jax.random.normal(ks[2], (emb_dim, 2 * dim), jnp.float32) * emb_dim ** (-0.5), 'b_emb': jnp.zeros((2 * dim,), jnp.float32), 'g_norm': jnp.ones((dim,), jnp.float32), 'W_qkv': jax.random.normal(ks[3], (dim, 3 * dim), jnp.float32) * dim ** (-0.5), 'g_q': jnp.ones((d_head,), jnp.float32), 'g_k': jnp.ones((d_head,), jnp.float32), 'W_out': jax.random.normal(ks[4], (dim, dim), jnp.float32) * dim ** (-0.5)}
    _L0_cond2_all = _L0_cond2_setup()
    _L0_cond2_in = {k: v for k, v in _L0_cond2_all.items() if k in ('W_emb', 'b_emb', 'g_norm', 'W_qkv', 'g_q', 'g_k', 'W_out')}
    del _L0_cond2_all

    def _L0_ffn_setup():
        import jax, jax.numpy as jnp
        import numpy as np
        B, S, H = (4, 128, 256)
        E, K, I, SI = (16, 4, 176, 704)

        def _silu_mul(gu, inter):
            return jax.nn.silu(gu[:, :inter]) * gu[:, inter:]
        key = jax.random.key(seed)
        ks = jax.random.split(key, 7)
        s = 0.02
        return {'hidden_states': jax.random.normal(ks[0], (B, S, H), jnp.float32), 'gate_w': jax.random.normal(ks[1], (E, H), jnp.float32) * s, 'expert_gate_up': jax.random.normal(ks[2], (E, 2 * I, H), jnp.float32) * s, 'expert_down': jax.random.normal(ks[3], (E, H, I), jnp.float32) * s, 'shared_gate_up': jax.random.normal(ks[4], (2 * SI, H), jnp.float32) * s, 'shared_down': jax.random.normal(ks[5], (H, SI), jnp.float32) * s, 'shared_gate_vec': jax.random.normal(ks[6], (1, H), jnp.float32) * s}
    _L0_ffn_all = _L0_ffn_setup()
    _L0_ffn_in = {k: v for k, v in _L0_ffn_all.items() if k in ('gate_w', 'expert_gate_up', 'expert_down', 'shared_gate_up', 'shared_down', 'shared_gate_vec')}
    del _L0_ffn_all
    return {'x': x, 'cond_2048': cond_2048, 'L0_cond_W_ih': _L0_cond_in['W_ih'], 'L0_cond_W_hh': _L0_cond_in['W_hh'], 'L0_cond_b_ih': _L0_cond_in['b_ih'], 'L0_cond_b_hh': _L0_cond_in['b_hh'], 'L0_attn_Wq': _L0_attn_in['Wq'], 'L0_attn_bq': _L0_attn_in['bq'], 'L0_attn_Wk': _L0_attn_in['Wk'], 'L0_attn_bk': _L0_attn_in['bk'], 'L0_attn_Wv': _L0_attn_in['Wv'], 'L0_attn_bv': _L0_attn_in['bv'], 'L0_attn_Wo': _L0_attn_in['Wo'], 'L0_attn_bo': _L0_attn_in['bo'], 'L0_cond2_W_emb': _L0_cond2_in['W_emb'], 'L0_cond2_b_emb': _L0_cond2_in['b_emb'], 'L0_cond2_g_norm': _L0_cond2_in['g_norm'], 'L0_cond2_W_qkv': _L0_cond2_in['W_qkv'], 'L0_cond2_g_q': _L0_cond2_in['g_q'], 'L0_cond2_g_k': _L0_cond2_in['g_k'], 'L0_cond2_W_out': _L0_cond2_in['W_out'], 'L0_ffn_gate_w': _L0_ffn_in['gate_w'], 'L0_ffn_expert_gate_up': _L0_ffn_in['expert_gate_up'], 'L0_ffn_expert_down': _L0_ffn_in['expert_down'], 'L0_ffn_shared_gate_up': _L0_ffn_in['shared_gate_up'], 'L0_ffn_shared_down': _L0_ffn_in['shared_down'], 'L0_ffn_shared_gate_vec': _L0_ffn_in['shared_gate_vec']}

def reference(x, cond_2048, L0_cond_W_ih, L0_cond_W_hh, L0_cond_b_ih, L0_cond_b_hh, L0_attn_Wq, L0_attn_bq, L0_attn_Wk, L0_attn_bk, L0_attn_Wv, L0_attn_bv, L0_attn_Wo, L0_attn_bo, L0_cond2_W_emb, L0_cond2_b_emb, L0_cond2_g_norm, L0_cond2_W_qkv, L0_cond2_g_q, L0_cond2_g_k, L0_cond2_W_out, L0_ffn_gate_w, L0_ffn_expert_gate_up, L0_ffn_expert_down, L0_ffn_shared_gate_up, L0_ffn_shared_down, L0_ffn_shared_gate_vec):
    import jax
    import jax.numpy as jnp

    def _L0_cond_ref(initial_state, inputs, W_ih, W_hh, b_ih, b_hh):
        import jax, jax.numpy as jnp
        import numpy as np
        B, T, D = (16, 128, 256)
        "ScanOverTime(GRU cell): sequential per-timestep module call with\n            dict-state passing; merge_dict_trees stacks the per-step\n            'state_predicted' tensors along axis=1 -> [B, T, D]."

        def cell(h, x):
            gi = x @ W_ih + b_ih
            gh = h @ W_hh + b_hh
            i_r, i_z, i_n = jnp.split(gi, 3, axis=-1)
            h_r, h_z, h_n = jnp.split(gh, 3, axis=-1)
            r = jax.nn.sigmoid(i_r + h_r)
            z = jax.nn.sigmoid(i_z + h_z)
            n = jnp.tanh(i_n + r * h_n)
            h_new = (1.0 - z) * n + z * h
            return (h_new, h_new)
        xs = jnp.swapaxes(inputs, 0, 1)
        _, hs = jax.lax.scan(cell, initial_state, xs)
        return jnp.swapaxes(hs, 0, 1)

    def _L0_attn_ref(x, Wq, bq, Wk, bk, Wv, bv, Wo, bo):
        import jax, jax.numpy as jnp
        import numpy as np
        N_HEADS = 16
        D_HEAD = 128
        D_MODEL = 256
        MAXLEN = 256
        b, t, _ = x.shape
        h, dh = (N_HEADS, D_HEAD)
        scale = 1.0 / np.sqrt(dh).astype(np.float32)
        q = (x @ Wq + bq).reshape(b, h, t, dh)
        k = (x @ Wk + bk).reshape(b, t, h, dh).transpose(0, 2, 3, 1)
        v = (x @ Wv + bv).reshape(b, t, h, dh).transpose(0, 2, 1, 3)
        logits = jnp.einsum('bhtd,bhds->bhts', q, k) * scale
        mask = jnp.triu(jnp.full((t, t), -jnp.inf, dtype=x.dtype), k=1)
        weights = jax.nn.softmax(logits + mask, axis=-1)
        out = jnp.einsum('bhts,bhsd->bhtd', weights, v)
        out = out.transpose(0, 2, 1, 3).reshape(b, t, h * dh)
        return out @ Wo + bo

    def _L0_cond2_ref(x, emb, W_emb, b_emb, g_norm, W_qkv, g_q, g_k, W_out):
        import jax, jax.numpy as jnp
        import numpy as np
        HEADS = 16
        EPS = 1e-06

        def _rms_norm(x, g):
            xf = x.astype(jnp.float32)
            y = xf * jax.lax.rsqrt(jnp.mean(xf * xf, axis=-1, keepdims=True) + EPS)
            return y.astype(x.dtype) * g
        b, n, dim = x.shape
        h = HEADS
        d = dim // h
        scale_shift = emb @ W_emb + b_emb
        scale, shift = jnp.split(scale_shift, 2, axis=-1)
        xn = _rms_norm(x, g_norm) * (1.0 + scale) + shift
        qkv = xn @ W_qkv
        qkv = qkv.reshape(b, n, 3, h, d)
        q, k, v = jnp.moveaxis(qkv, 2, 0)
        q = jnp.swapaxes(q, 1, 2)
        k = jnp.swapaxes(k, 1, 2)
        v = jnp.swapaxes(v, 1, 2)
        q = _rms_norm(q, g_q)
        k = _rms_norm(k, g_k)
        logits = jnp.einsum('bhqd,bhkd->bhqk', q, k) * d ** (-0.5)
        attn = jax.nn.softmax(logits, axis=-1)
        o = jnp.einsum('bhqk,bhkd->bhqd', attn, v)
        o = jnp.swapaxes(o, 1, 2).reshape(b, n, dim)
        return o + o @ W_out

    def _L0_ffn_ref(hidden_states, gate_w, expert_gate_up, expert_down, shared_gate_up, shared_down, shared_gate_vec):
        import jax, jax.numpy as jnp
        import numpy as np
        B, S, H = (4, 128, 256)
        E, K, I, SI = (16, 4, 176, 704)

        def _silu_mul(gu, inter):
            return jax.nn.silu(gu[:, :inter]) * gu[:, inter:]
        orig_shape = hidden_states.shape
        x = hidden_states.reshape(-1, H)
        router_logits = x @ gate_w.T
        routing_probs = jax.nn.softmax(router_logits.astype(jnp.float32), axis=-1)
        topk_w, topk_idx = jax.lax.top_k(routing_probs, K)
        topk_w = topk_w / topk_w.sum(axis=-1, keepdims=True)
        topk_w = topk_w.astype(x.dtype)
        combine = (jax.nn.one_hot(topk_idx, E, dtype=x.dtype) * topk_w[..., None]).sum(1)
        shared = _silu_mul(x @ shared_gate_up.T, SI) @ shared_down.T
        shared = shared * jax.nn.sigmoid(x @ shared_gate_vec.T)

        def step(acc, ew):
            w_gu, w_d, cw = ew
            h = _silu_mul(x @ w_gu.T, I)
            return (acc + h @ w_d.T * cw[:, None], None)
        acc0 = jnp.zeros_like(x)
        sparse, _ = jax.lax.scan(step, acc0, (expert_gate_up, expert_down, combine.T))
        return (shared + sparse).reshape(orig_shape)
    x = x + _L0_attn_ref(_L0_cond_ref(cond_2048, x, L0_cond_W_ih, L0_cond_W_hh, L0_cond_b_ih, L0_cond_b_hh), L0_attn_Wq, L0_attn_bq, L0_attn_Wk, L0_attn_bk, L0_attn_Wv, L0_attn_bv, L0_attn_Wo, L0_attn_bo)
    x = x + _L0_ffn_ref(_L0_cond2_ref(x, cond_2048[:, None, :], L0_cond2_W_emb, L0_cond2_b_emb, L0_cond2_g_norm, L0_cond2_W_qkv, L0_cond2_g_q, L0_cond2_g_k, L0_cond2_W_out), L0_ffn_gate_w, L0_ffn_expert_gate_up, L0_ffn_expert_down, L0_ffn_shared_gate_up, L0_ffn_shared_down, L0_ffn_shared_gate_vec)
    return x

_drawn_inputs = setup_inputs


def setup_inputs(seed=0):
    import zlib

    import numpy as np

    out = dict(_drawn_inputs(seed))
    spreads = {'L0_cond_b_ih': (0.0, 0.484),
     'L0_cond_b_hh': (0.0, 0.8),
     'L0_attn_bq': (0.0, 0.8),
     'L0_attn_bk': (0.0, 0.8),
     'L0_attn_bv': (0.0, 0.1),
     'L0_attn_bo': (0.0, 0.1),
     'L0_cond2_b_emb': (0.0, 0.8),
     'L0_cond2_g_norm': (1.0, 0.6),
     'L0_cond2_g_q': (1.0, 0.6),
     'L0_cond2_g_k': (1.0, 0.6)}
    factors = {'L0_cond_W_hh': 3.571,
     'L0_attn_Wq': 8.0,
     'L0_attn_Wk': 8.0,
     'L0_ffn_gate_w': 4.284,
     'L0_ffn_expert_gate_up': 3.33,
     'L0_ffn_expert_down': 3.35,
     'L0_ffn_shared_gate_vec': 4.927}
    for name, (base, spread) in spreads.items():
        noise = np.random.default_rng([zlib.crc32(name.encode()), seed]).standard_normal(out[name].shape)
        drawn = base * np.exp(spread * noise) if base else spread * noise
        out[name] = jnp.asarray(drawn.astype(out[name].dtype))
    for name, factor in factors.items():
        out[name] = (out[name] * factor).astype(out[name].dtype)
    return out
```

```python
from contextlib import ExitStack

import numpy as np

import concourse.bass as bass
from concourse import mybir

P = 128
F32 = mybir.dt.float32
BF16 = mybir.dt.bfloat16
ACT = mybir.ActivationFunctionType
ALU = mybir.AluOpType
AX = mybir.AxisListType

B, T, D = 4, 256, 256
J = D // P
NT = B * T
TILES = NT // P
HALF = 512
H1, DH1 = 16, 128
H2, DH2 = 16, 16
TC = T // P
E, TOPK, INTER, SHARED = 16, 4, 176, 704
HID = E * INTER + SHARED
NCH = -(-HID // P)
U = 8


class Count:

    def __init__(self, sem):
        self.sem, self.n = sem, 0

    def inc(self, instruction, by=1):
        instruction.then_inc(self.sem, by)
        self.n += by
        return self.n


def gru_block(nc, dram, gruT):
    with ExitStack() as ctx:
        def sb(name, shape, dt=F32):
            return ctx.enter_context(nc.sbuf_tensor(name, shape, dt))

        def sem(name):
            return ctx.enter_context(nc.semaphore(name))

        xT = sb("xT", [P, J, NT])
        wih = sb("wih", [P, J, 3 * D])
        whh = sb("whh", [P, J, 3 * D])
        whh_rest = sb("whh_rest", [P, 2, J, 3 * D])
        whh_part = sb("whh_part", [P, 3, J, 3 * D], BF16)
        bias_ih = sb("bias_ih", [P, 6])
        bias_hh = sb("bias_hh", [P, 6])
        bias_g = sb("bias_g", [P, 4])
        ident = sb("ident_f", [P, P])
        identb = sb("ident_b", [P, P], BF16)
        condT = sb("condT", [P, J, B])
        gates = [sb(f"gates{q}", [P, T, 24]) for q in range(3)]
        bhn = sb("bhn", [P, 3, 8])
        hs = sb("hs", [P, 2, 3, 16])
        r_scan = sb("r_scan", [P, 32])
        t_scan = sb("t_scan", [P, 32])
        u_scan = sb("u_scan", [P, 16])
        nv_scan = sb("nv_scan", [P, 16])
        r_sum = sb("r_sum", [P, 8])
        z_sum = sb("z_sum", [P, 8])
        z_gate = sb("z_gate", [P, 8])
        bank = [ctx.enter_context(nc.psum_tensor(f"gb{i}", [P, HALF], F32)) for i in range(7)]
        R, Z, N = bank[4:7]

        loaded = {n: sem(f"ld_{n}") for n in ("x", "wih", "whh", "small")}
        gi_psum, gi_sbuf, bias_ready = sem("gi_psum"), sem("gi_sbuf"), sem("bias_ready")
        split_dve, split_pool = sem("split_dve"), sem("split_pool")
        r_psum, z_psum, scan_in = sem("r_psum"), sem("z_psum"), sem("scan_in")
        r_sum_ready, z_sum_ready, z_ready = sem("r_sum_ready"), sem("z_sum_ready"), sem("z_ready")
        npre_ready, hin_ready = sem("npre_ready"), sem("hin_ready")
        h_new, h_rest, h_ready, h_stored = sem("h_new"), sem("h_rest"), sem("h_ready"), sem("h_stored")

        def high(ap):
            return ap.bitcast(BF16)[:, 1::2]

        def part(par, q):
            return hs[:, par, q, 1::2]

        def part_high(par, q):
            return hs[:, par, q, :].bitcast(BF16)[:, 3::4]

        block = ctx.enter_context(nc.Block())

        @block.sync
        def _(sp):
            sp.dma_start(xT[:], dram["xT"]).then_inc(loaded["x"], 16)
            sp.dma_start(wih[:], dram["wih"]).then_inc(loaded["wih"], 16)
            sp.dma_start(whh[:], dram["whh"]).then_inc(loaded["whh"], 16)
            for dst, name in ((bias_ih, "bias_ih"), (bias_hh, "bias_hh"), (condT, "condT"),
                              (ident, "ident")):
                sp.dma_start(dst[:], dram[name]).then_inc(loaded["small"], 16)

        @block.tensor
        def _(pe):
            pe.wait_ge(loaded["x"], 16)
            pe.wait_ge(loaded["wih"], 16)
            for n in range(12):
                m, half = n // 2, n % 2
                if n >= 4:
                    pe.wait_ge(gi_sbuf, n - 3)
                for j in range(J):
                    mm = pe.matmul(bank[n % 4][:], wih[:, j, m * P:(m + 1) * P],
                                   xT[:, j, half * HALF:(half + 1) * HALF],
                                   start=(j == 0), stop=(j == J - 1))
                mm.then_inc(gi_psum, 1)
            pe.wait_ge(split_dve, 1)
            pe.wait_ge(split_pool, 1)
            with pe.Fori(0, T // U) as i:
                for k in range(U):
                    t, cur = i * U + k, k % 2
                    pe.wait_ge(z_sum_ready, t + 1)
                    for q in range(3):
                        for dst, c0 in ((R, 0), (Z, 8)):
                            g = gates[q][:, bass.ds(t, 1), c0:c0 + 8].rearrange("p a b -> p (a b)")
                            pe.matmul(dst[:, 0:24:3], identb[:], high(g), start=(q == 0),
                                      stop=False, skip_group_check=True)
                    pe.wait_ge(npre_ready, t + 1)
                    for q in range(3):
                        g = gates[q][:, bass.ds(t, 1), 16:24].rearrange("p a b -> p (a b)")
                        pe.matmul(N[:, 3:32:4], identb[:], high(g), start=(q == 0), stop=False,
                                  skip_group_check=True)
                        pe.matmul(N[:, 0:32:4], identb[:], high(bhn[:, q, :]), start=False,
                                  stop=False, skip_group_check=True)
                    pe.wait_ge(h_ready, t + 1)
                    for dst, width, m0, done in ((R, 3, 0, r_psum), (Z, 3, 2, z_psum),
                                                 (N, 4, 4, scan_in)):
                        for mi in range(J):
                            out = dst[:, mi * B * width:(mi + 1) * B * width] \
                                .rearrange("p (b q) -> p b q", q=width)[:, :, 0:3]
                            for q in range(3):
                                for j in range(J):
                                    w = whh_part[:, q, j, (m0 + mi) * P:(m0 + mi + 1) * P]
                                    h = hs[:, cur, :, 8 * j:8 * j + 8].bitcast(BF16)[:, :, 3::4] \
                                        .rearrange("p q b -> p b q")
                                    mm = pe.matmul(out, w, h, start=False, stop=False,
                                                   skip_group_check=True)
                        mm.then_inc(done, 1)

        @block.scalar
        def _(act):
            act.wait_ge(bias_ready, 1)
            for n in range(12):
                m, half = n // 2, n % 2
                gate, mi = m // 2, m % 2
                act.wait_ge(gi_psum, n + 1)
                c0 = gate * 8 + mi * B + half * 2
                out = gates[0][:, :, c0:c0 + 2].rearrange("p t b -> p b t")
                bias = bias_g[:, m:m + 1] if gate < 2 else bias_ih[:, m:m + 1]
                nc.scalar.activation(out, bank[n % 4][:].rearrange("p (b t) -> p b t", b=2),
                                     ACT.Identity, bias=bias).then_inc(gi_sbuf, 1)
            with act.Fori(0, T // U) as i:
                for k in range(U):
                    t = i * U + k
                    act.wait_ge(r_sum_ready, t + 1)
                    nc.scalar.activation(r_scan[:, 3::4], r_sum[:], ACT.Sigmoid).then_inc(scan_in, 1)
                    act.wait_ge(z_sum_ready, t + 2)
                    nc.scalar.activation(z_gate[:], z_sum[:], ACT.Sigmoid).then_inc(z_ready, 1)
                    nc.scalar.activation(u_scan[:, 1::2], z_sum[:], ACT.Sigmoid, scale=-1.0)
                    act.wait_ge(npre_ready, t + 2)
                    nc.scalar.activation(nv_scan[:, 0::2], t_scan[:, 3::4],
                                         ACT.Tanh).then_inc(hin_ready, 1)

        @block.vector
        def _(dve):
            dve.wait_ge(loaded["small"], 64)
            nc.vector.tensor_tensor(bias_g[:], bias_ih[:, 0:4], bias_hh[:, 0:4],
                                    ALU.add).then_inc(bias_ready, 1)
            nc.vector.memset(r_scan[:], 0.0).then_inc(bias_ready, 1)
            nc.vector.memset(u_scan[:], 0.0).then_inc(bias_ready, 1)
            nc.vector.memset(hs[:], 0.0).then_inc(bias_ready, 1)
            dve.wait_ge(bias_ready, 4)
            nc.vector.memset(r_scan[:, 1::4], 1.0).then_inc(bias_ready, 1)
            nc.vector.memset(r_scan[:, 2::4], 1.0).then_inc(bias_ready, 1)
            nc.vector.tensor_copy(identb[:], ident[:]).then_inc(bias_ready, 1)
            nc.vector.memset(bhn[:], 0.0).then_inc(bias_ready, 1)
            dve.wait_ge(bias_ready, 8)
            for mi in range(J):
                nc.vector.tensor_scalar(bhn[:, 0, mi * B:(mi + 1) * B], bhn[:, 0, mi * B:(mi + 1) * B],
                                        bias_hh[:, 4 + mi:5 + mi], None,
                                        ALU.add).then_inc(bias_ready, 1)
            nc.vector.tensor_copy(part(0, 0), condT[:].rearrange("p j b -> p (j b)")) \
                .then_inc(bias_ready, 1)
            dve.wait_ge(bias_ready, 11)
            dve.wait_ge(loaded["whh"], 16)
            src = whh[:].rearrange("p j n -> p (j n)")
            for q in range(3):
                if q < 2:
                    rest = whh_rest[:, q].rearrange("p j n -> p (j n)")
                    nc.vector.tensor_tensor(rest, src, high(src), ALU.subtract).then_inc(bias_ready, 1)
                    nc.vector.tensor_tensor(bhn[:, q + 1, :], bhn[:, q, :], high(bhn[:, q, :]),
                                            ALU.subtract).then_inc(bias_ready, 1)
                    nc.vector.tensor_tensor(part(0, q + 1), part(0, q), part_high(0, q),
                                            ALU.subtract).then_inc(bias_ready, 1)
                nc.vector.tensor_copy(whh_part[:, q].rearrange("p j n -> p (j n)"),
                                      high(src)).then_inc(bias_ready, 1)
                if q < 2:
                    dve.wait_ge(bias_ready, 15 + 4 * q)
                    src = rest
            dve.wait_ge(gi_sbuf, 12)
            for q in range(2):
                a = gates[q][:, 0:T // 2, :].rearrange("p t c -> p (t c)")
                o = gates[q + 1][:, 0:T // 2, :].rearrange("p t c -> p (t c)")
                nc.vector.tensor_tensor(o, a, high(a), ALU.subtract).then_inc(bias_ready, 1)
                dve.wait_ge(bias_ready, 21 + q)
            nc.vector.memset(t_scan[:], 0.0).then_inc(npre_ready, 1)
            nc.vector.memset(r_sum[:], 0.0).then_inc(z_sum_ready, 1)
            nc.vector.memset(z_sum[:], 0.0).then_inc(h_ready, 1)
            nc.vector.memset(nv_scan[:], 0.0).then_inc(split_dve, 1)
            with dve.Fori(0, T // U) as i:
                for k in range(U):
                    t, cur = i * U + k, k % 2
                    nxt = 1 - cur
                    dve.wait_ge(r_psum, t + 1)
                    nc.vector.tensor_reduce(r_sum[:], R[:, 0:24].rearrange("p (m q) -> p m q", q=3),
                                            AX.X, ALU.add).then_inc(r_sum_ready, 1)
                    dve.wait_ge(z_psum, t + 1)
                    nc.vector.tensor_reduce(z_sum[:], Z[:, 0:24].rearrange("p (m q) -> p m q", q=3),
                                            AX.X, ALU.add).then_inc(z_sum_ready, 1)
                    dve.wait_ge(scan_in, 2 * t + 2)
                    nc.vector.tensor_tensor_scan(t_scan[:], r_scan[:], N[:, 0:32], 0.0, ALU.mult,
                                                 ALU.add).then_inc(npre_ready, 1)
                    dve.wait_ge(z_ready, t + 1)
                    nc.vector.tensor_tensor(nv_scan[:, 1::2], z_gate[:], part(cur, 0),
                                            ALU.mult).then_inc(hin_ready, 1)
                    dve.wait_ge(h_stored, t + 1)
                    dve.wait_ge(hin_ready, 2 * t + 2)
                    nc.vector.tensor_tensor_scan(hs[:, nxt, 0, :], u_scan[:], nv_scan[:], 0.0,
                                                 ALU.mult, ALU.add).then_inc(h_new, 1)
                    dve.wait_ge(h_new, t + 1)
                    nc.vector.tensor_tensor(part(nxt, 1), part(nxt, 0), part_high(nxt, 0),
                                            ALU.subtract).then_inc(h_rest, 1)
                    dve.wait_ge(h_rest, t + 1)
                    nc.vector.tensor_tensor(part(nxt, 2), part(nxt, 1), part_high(nxt, 1),
                                            ALU.subtract).then_inc(h_ready, 1)

        @block.gpsimd
        def _(pool):
            pool.wait_ge(gi_sbuf, 12)
            for q in range(2):
                a = gates[q][:, T // 2:T, :].rearrange("p t c -> p (t c)")
                o = gates[q + 1][:, T // 2:T, :].rearrange("p t c -> p (t c)")
                (nc.gpsimd.tensor_tensor(o, a, high(a), ALU.subtract)
                 .then_inc(split_pool if q else h_stored, 1))
                if q == 0:
                    pool.wait_ge(h_stored, 1)
            with pool.Fori(0, T // U) as i:
                for k in range(U):
                    t, nxt = i * U + k, 1 - k % 2
                    pool.wait_ge(h_new, t + 1)
                    nc.gpsimd.tensor_copy(
                        gruT[:, :, :, bass.ds(t, 1)].rearrange("p j b o -> p (j b o)"),
                        part(nxt, 0)).then_inc(h_stored, 1)


def attention_block(nc, dram, gruT, x1):
    scale = float(DH1) ** -0.5
    units = H1 * B
    with ExitStack() as ctx:
        def sb(name, shape, dt=F32):
            return ctx.enter_context(nc.sbuf_tensor(name, shape, dt))

        def sem(name):
            return ctx.enter_context(nc.semaphore(name))

        QT = sb("QT", [P, B, T, H1])
        wq = sb("wq", [P, 2, J * P + 1])
        wkv = sb("wkv", [P, 2, 2 * J * P + 1])
        wo = sb("wo", [P, 2, D + 1])
        qh = sb("qh", [P, 2, B, T])
        kh = sb("kh", [P, 2, B, T])
        vh = sb("vh", [P, 2, B, TC * DH1])
        logits = sb("logits", [P, 2, 3 * P])
        probs = sb("probs", [P, 2, 3 * P])
        probsT = sb("probsT", [P, 3 * P])
        oT = sb("oT", [P, T])
        mask = sb("mask", [P, 3 * P])
        ident = sb("ident_a", [P, P])
        ones = sb("ones", [1, P])
        bo = sb("bo", [1, D])
        xr = sb("xr", [P, TILES, D])
        waiter = sb("waiter", [P, 1])
        rmax = sb("rmax", [P, 2, TC])
        nmax = sb("nmax", [P, 2, TC])
        rsum = sb("rsum", [P, 2, TC])
        rinv = sb("rinv", [P, 2, TC])
        acc = [ctx.enter_context(nc.psum_tensor(f"acc{i}", [P, HALF], F32)) for i in range(B)]
        S = [ctx.enter_context(nc.psum_tensor(f"S{i}", [P, HALF], F32)) for i in range(2)]
        TB = ctx.enter_context(nc.psum_tensor("TB", [P, HALF], F32))
        OB = ctx.enter_context(nc.psum_tensor("OB", [P, HALF], F32))
        qbank = [S[0], S[1], TB, OB]

        const_in, x_in = sem("const_in"), sem("x_in")
        wq_in, wkv_in, wo_in = ([sem(f"{n}{par}") for par in range(2)]
                                for n in ("wq_in", "wkv_in", "wo_in"))
        ones_ready, q_psum, q_act, q_dve = (sem(n) for n in (
            "ones_ready", "q_psum", "q_act", "q_dve"))
        qh_ready, s_psum, k_psum, v_psum, t_psum, o_psum, op_done = (sem(n) for n in (
            "qh_ready", "s_psum", "k_psum", "v_psum", "t_psum", "o_psum", "op_done"))
        k_ready, v_ready, pT_ready, oT_ready = (sem(n) for n in (
            "k_ready", "v_ready", "pT_ready", "oT_ready"))
        max_ready, nmax_ready, exp_done, rinv_ready, p_ready, x1_ready = (sem(n) for n in (
            "max_ready", "nmax_ready", "exp_done", "rinv_ready", "p_ready", "x1_ready"))

        block = ctx.enter_context(nc.Block())

        def heads(eng, head):
            with eng.Fori(0, H1 // 2 - 1) as i:
                for hh in range(2):
                    head(i, i * 2 + hh, hh, False)
            head(H1 // 2 - 1, H1 - 2, 0, False)
            head(H1 // 2 - 1, H1 - 1, 1, True)

        @block.sync
        def _(sp):
            for dst, name in ((mask, "mask"), (ident, "ident"), (bo, "bo")):
                sp.dma_start(dst[:], dram[name]).then_inc(const_in, 16)
            sp.dma_start(wq[:, 0], dram["wq"][0]).then_inc(wq_in[0], 16)
            sp.dma_start(wq[:, 1], dram["wq"][1]).then_inc(wq_in[1], 16)
            sp.dma_start(wkv[:, 0], dram["wkv"][0]).then_inc(wkv_in[0], 16)
            sp.dma_start(wo[:, 0], dram["wo"][0]).then_inc(wo_in[0], 16)
            sp.dma_start(wkv[:, 1], dram["wkv"][1]).then_inc(wkv_in[1], 16)
            sp.dma_start(xr[:], dram["xr"]).then_inc(x_in, 16)
            with sp.Fori(0, H1 // 2 - 1) as i:
                for par in range(2):
                    c = i * 2 + par
                    sp.wait_ge(q_act, c + 3)
                    sp.wait_ge(q_dve, c + 3)
                    sp.dma_start(wq[:, par], dram["wq"][bass.ds(c + 2, 1)]
                                 .rearrange("o p n -> (o p) n")).then_inc(wq_in[par], 16)

            def loads(i, h, par, last):
                if last:
                    return
                sp.wait_ge(op_done, 4 * h + 1)
                sp.dma_start(wo[:, 1 - par], dram["wo"][bass.ds(h + 1, 1)]
                             .rearrange("o p n -> (o p) n")).then_inc(wo_in[1 - par], 16)
                if isinstance(h, int) and h + 2 >= H1:
                    return
                sp.wait_ge(k_ready, 4 * h + 4)
                sp.wait_ge(v_psum, 4 * h + 4)
                sp.dma_start(wkv[:, par], dram["wkv"][bass.ds(h + 2, 1)]
                             .rearrange("o p n -> (o p) n")).then_inc(wkv_in[par], 16)
            heads(sp, loads)

        @block.tensor
        def _(pe):
            with pe.Fori(0, H1 // 2) as i:
                for par in range(2):
                    c = i * 2 + par
                    pe.wait_ge(wq_in[par], 16 * i + 16)
                    pe.wait_ge(q_act, c + 1)
                    pe.wait_ge(q_dve, c + 1)
                    for half in range(2):
                        for j in range(J):
                            mm = pe.matmul(qbank[2 * par + half][:], wq[:, par, j * P:(j + 1) * P],
                                           gruT[:, j, 2 * half:2 * half + 2, :]
                                           .rearrange("p b t -> p (b t)"),
                                           start=(j == 0), stop=(j == J - 1))
                        mm.then_inc(q_psum, 1)

            def k_unit(par, b, bank):
                for j in range(J):
                    mm = pe.matmul(bank[:, 0:T], wkv[:, par, j * P:(j + 1) * P], gruT[:, j, b, :],
                                   start=(j == 0), stop=(j == J - 1))
                mm.then_inc(k_psum, 1)

            def v_unit(par, b, bank):
                for sc in range(TC):
                    for j in range(J):
                        mm = pe.matmul(bank[:, sc * DH1:(sc + 1) * DH1],
                                       gruT[:, j, b, sc * P:(sc + 1) * P],
                                       wkv[:, par, (J + j) * P:(J + j + 1) * P],
                                       start=(j == 0), stop=(j == J - 1))
                mm.then_inc(v_psum, 1)

            def score_unit(par, b, bank):
                for tc in range(TC):
                    mm = pe.matmul(bank[:, tc * P:(2 * tc + 1) * P],
                                   qh[:, par, b, tc * P:(tc + 1) * P],
                                   kh[:, par, b, 0:(tc + 1) * P], start=True, stop=True)
                mm.then_inc(s_psum, 1)

            pe.wait_ge(const_in, 48)
            pe.wait_ge(ones_ready, 1)
            for b in range(B):
                for tc in range(TC):
                    mm = pe.matmul(acc[b][:, tc * D:(tc + 1) * D], ones[:], bo[:], start=(tc == 0),
                                   stop=False, skip_group_check=True)
            mm.then_inc(op_done, 1)
            pe.wait_ge(wkv_in[0], 16)
            pe.wait_ge(q_act, H1 + 2)
            pe.wait_ge(q_dve, H1 + 2)
            for b in range(B):
                if b >= 1:
                    pe.wait_ge(k_ready, b)
                k_unit(0, b, OB)
                if b >= 1:
                    pe.wait_ge(v_ready, b)
                v_unit(0, b, TB)
            pe.wait_ge(k_ready, 4)
            pe.wait_ge(qh_ready, 1)
            score_unit(0, 0, S[0])

            def head(i, h, par, last):
                for b in range(B):
                    u = h * 4 + b
                    if not (last and b == B - 1):
                        if last:
                            pe.wait_ge(k_ready, units)
                            pe.wait_ge(exp_done, u)
                        else:
                            pe.wait_ge(k_ready, u + 4)
                        if b == B - 1:
                            pe.wait_ge(qh_ready, h + 2)
                        score_unit(par if b < B - 1 else 1 - par, (b + 1) % B, S[(b + 1) % 2])
                    pe.wait_ge(p_ready, u + 1)
                    pe.wait_ge(v_ready, units if last else u + 4)
                    for n in range(3):
                        mm = pe.transpose(TB[:, n * P:(n + 1) * P],
                                          probs[:, b % 2, n * P:(n + 1) * P], ident[:])
                    mm.then_inc(t_psum, 1)
                    if not last:
                        if b == 0:
                            pe.wait_ge(wkv_in[1 - par], 16 * (i + par) + 16)
                        k_unit(1 - par, b, S[b % 2])
                    pe.wait_ge(pT_ready, u + 1)
                    pe.matmul(OB[:, 0:P], vh[:, par, b, 0:DH1], probsT[:, 0:P],
                              start=True, stop=False, skip_group_check=True)
                    pe.matmul(OB[:, P:T], vh[:, par, b, 0:DH1], probsT[:, P:2 * P],
                              start=False, stop=False, skip_group_check=True)
                    pe.matmul(OB[:, P:T], vh[:, par, b, DH1:2 * DH1], probsT[:, 2 * P:3 * P],
                              start=False, stop=True, skip_group_check=True).then_inc(o_psum, 1)
                    if not last:
                        v_unit(1 - par, b, TB)
                    if b == 0:
                        pe.wait_ge(wo_in[par], 16 * i + 16)
                    pe.wait_ge(oT_ready, u + 1)
                    for tc in range(TC):
                        mm = pe.matmul(acc[b][:, tc * D:(tc + 1) * D], oT[:, tc * P:(tc + 1) * P],
                                       wo[:, par, 0:D], start=False, stop=False,
                                       skip_group_check=True)
                    mm.then_inc(op_done, 1)
            heads(pe, head)

        @block.scalar
        def _(act):
            with act.Fori(0, H1 // 2) as i:
                for par in range(2):
                    c = i * 2 + par
                    act.wait_ge(q_psum, 2 * c + 1)
                    nc.scalar.activation(QT[:, 0:2, :, bass.ds(c, 1)].rearrange("p b t o -> p b (t o)"),
                                         qbank[2 * par][:].rearrange("p (b t) -> p b t", b=2),
                                         ACT.Identity, bias=wq[:, par, J * P:J * P + 1]) \
                        .then_inc(q_act, 1)

            def key(par, b, bank, n):
                act.wait_ge(k_psum, n + 1)
                nc.scalar.activation(kh[:, par, b, :], bank[:, 0:T], ACT.Identity,
                                     bias=wkv[:, par, 2 * J * P:2 * J * P + 1]).then_inc(k_ready, 1)

            def exps(n, par):
                act.wait_ge(nmax_ready, n + 1)
                for tc in range(TC):
                    c = slice(tc * P, (2 * tc + 1) * P)
                    a = nc.scalar.activation(probs[:, par, c], logits[:, par, c], ACT.Exp,
                                             bias=nmax[:, par, tc:tc + 1],
                                             accum_out=rsum[:, par, tc:tc + 1])
                a.then_inc(exp_done, 1)

            for b in range(B):
                key(0, b, OB, b)
            exps(0, 0)

            def head(i, h, par, last):
                for b in range(B):
                    u = h * 4 + b
                    if not (last and b == B - 1):
                        if isinstance(h, int) or b > 0:
                            act.wait_ge(t_psum, u)
                        exps(u + 1, (b + 1) % 2)
                    if not last:
                        key(1 - par, b, S[b % 2], u + 4)
                    if b == 0:
                        act.wait_ge(wo_in[par], 16 * i + 16)
                    act.wait_ge(op_done, u + 1)
                    act.wait_ge(o_psum, u + 1)
                    nc.scalar.activation(oT[:], OB[:, 0:T], ACT.Identity,
                                         bias=wo[:, par, D:D + 1]).then_inc(oT_ready, 1)
            heads(act, head)

        @block.vector
        def _(dve):
            nc.vector.memset(ones[:], 1.0).then_inc(ones_ready, 1)
            nc.vector.memset(rmax[:], 0.0).then_inc(q_act, 2)
            nc.vector.memset(nmax[:], 0.0).then_inc(q_dve, 2)
            with dve.Fori(0, H1 // 2) as i:
                for par in range(2):
                    c = i * 2 + par
                    dve.wait_ge(q_psum, 2 * c + 2)
                    nc.vector.tensor_scalar(QT[:, 2:4, :, bass.ds(c, 1)].rearrange("p b t o -> p b (t o)"),
                                            qbank[2 * par + 1][:].rearrange("p (b t) -> p b t", b=2),
                                            wq[:, par, J * P:J * P + 1], None,
                                            ALU.add).then_inc(q_dve, 1)

            def value(par, b, n):
                dve.wait_ge(v_psum, n + 1)
                nc.vector.tensor_copy(vh[:, par, b, :], TB[:, 0:TC * DH1]).then_inc(v_ready, 1)

            def maxima(n, par, bank):
                dve.wait_ge(s_psum, n + 1)
                nc.vector.memset(waiter[:], 0.0)
                for tc in range(TC):
                    c = slice(tc * P, (2 * tc + 1) * P)
                    a = nc.vector.tensor_tensor_reduce(
                        out=logits[:, par, c], in0=bank[:, c], in1=mask[:, c], scale=scale,
                        scalar=-3.0e38, op0=ALU.add, op1=ALU.max, accum_out=rmax[:, par, tc:tc + 1])
                a.then_inc(max_ready, 1)
                dve.wait_ge(max_ready, n + 1)
                nc.vector.tensor_scalar(nmax[:, par, :], rmax[:, par, :], -1.0, None,
                                        ALU.mult).then_inc(nmax_ready, 1)

            def inverse(n, par):
                dve.wait_ge(exp_done, n + 1)
                nc.vector.reciprocal(rinv[:, par, :], rsum[:, par, :]).then_inc(rinv_ready, 1)

            for b in range(B):
                value(0, b, b)
            maxima(0, 0, S[0])
            inverse(0, 0)

            def head(i, h, par, last):
                for b in range(B):
                    u = h * 4 + b
                    nxt = (b + 1) % 2
                    if not (last and b == B - 1):
                        maxima(u + 1, nxt, S[nxt])
                    dve.wait_ge(t_psum, u + 1)
                    nc.vector.tensor_copy(probsT[:], TB[:, 0:3 * P]).then_inc(pT_ready, 1)
                    if not (last and b == B - 1):
                        inverse(u + 1, nxt)
                    if not last:
                        value(1 - par, b, u + 4)
            heads(dve, head)
            dve.wait_ge(x_in, 16)
            dve.wait_ge(op_done, units + 1)
            for b in range(B):
                nc.vector.tensor_tensor(x1[:, 2 * b:2 * b + 2, :].rearrange("p a d -> p (a d)"),
                                        acc[b][:], xr[:, 2 * b:2 * b + 2, :]
                                        .rearrange("p a d -> p (a d)"), ALU.add).then_inc(x1_ready, 1)

        @block.gpsimd
        def _(pool):
            pool.wait_ge(q_act, H1 + 2)
            pool.wait_ge(q_dve, H1 + 2)

            def query(h, par):
                if isinstance(h, int):
                    src = QT[:, :, 16 * h:16 * h + 16, :]
                else:
                    src = QT[:, :, bass.ds(h * 16, 16), :]
                nc.gpsimd.tensor_copy(qh[:, par], src.rearrange("p b r c -> p b (r c)")) \
                    .then_inc(qh_ready, 1)

            def weights(n, par):
                pool.wait_ge(rinv_ready, n + 1)
                for tc in range(TC):
                    c = slice(tc * P, (2 * tc + 1) * P)
                    a = nc.gpsimd.tensor_tensor(
                        probs[:, par, c], probs[:, par, c],
                        rinv[:, par, tc:tc + 1].to_broadcast([P, (tc + 1) * P]), ALU.mult)
                a.then_inc(p_ready, 1)
            query(0, 0)
            weights(0, 0)

            def head(i, h, par, last):
                for b in range(B):
                    u = h * 4 + b
                    if b == 0 and not last:
                        pool.wait_ge(s_psum, u + 1)
                        query(h + 1, 1 - par)
                    if not (last and b == B - 1):
                        weights(u + 1, (b + 1) % 2)
            heads(pool, head)


def adaln_block(nc, dram, x1, yT):
    eps, scale = 1e-6, float(DH2) ** -0.5
    GROUPS = TILES * J
    PAIRS = 4 * GROUPS
    with ExitStack() as ctx:
        def sb(name, shape, dt=F32):
            return ctx.enter_context(nc.sbuf_tensor(name, shape, dt))

        def sem(name):
            return ctx.enter_context(nc.semaphore(name))

        wemb = sb("wemb", [P, J, 2 * D])
        bemb = sb("bemb", [P, 4])
        gnorm = sb("gnorm", [P, J])
        condT = sb("condT2", [P, J, B])
        wqkv = sb("wqkv", [P, J, 3 * D])
        gqk = sb("gqk", [P, 2 * D])
        wout = sb("wout", [P, J, D])
        ident = sb("ident_c", [P, P])
        parity = sb("parity", [P, 2])
        emb = sb("emb", [P, 4, B])
        gain = sb("gain", [P, J, B])
        epst = sb("epst", [P, 1])
        ss = sb("ss", [P, TILES])
        rms = sb("rms", [P, TILES])
        rstd = sb("rstd", [P, TILES])
        junk = sb("junk", [P, D])
        xn = sb("xn", [P, TILES, D])
        xnT = sb("xnT", [P, J, NT])
        qk = sb("qk", [P, TILES, 2 * D])
        sq = sb("sq", [P, 2, 2 * D])
        ss2 = sb("ss2", [P, TILES, 32])
        rms2 = sb("rms2", [P, TILES, 32])
        rstd2 = sb("rstd2", [P, TILES, 32])
        v = sb("v", [P, TILES, D])
        qT = sb("qT", [P, J, NT])
        kT = sb("kT", [P, J, B, 2, T])
        mx = sb("mx", [P, 2, 8])
        nmx = sb("nmx", [P, 2, 8])
        rsum = sb("rsum2", [P, TILES, H2])
        rinv = sb("rinv2", [P, TILES, H2])
        probs = sb("probs2", [P, 2, 8, T])
        pT = sb("pT", [P, 4, HALF])
        o = sb("o", [P, TILES, D])
        oT = sb("oT2", [P, J, NT])
        bk = [ctx.enter_context(nc.psum_tensor(f"cb{i}", [P, HALF], F32)) for i in range(8)]

        w_in, emb_psum, emb_act, gain_ready = (sem(n) for n in (
            "w_in", "emb_psum", "emb_act", "gain_ready"))
        ss_ready, rms_ready, rstd_ready, xn_ready = (sem(n) for n in (
            "ss_ready", "rms_ready", "rstd_ready", "xn_ready"))
        xt_psum, xt_done, qk_psum, qk_done, v_psum, v_done = (sem(n) for n in (
            "xt_psum", "xt_done", "qk_psum2", "qk_done", "v_psum2", "v_done"))
        sq_ready, ss2_ready, rms2_ready, rstd2_ready, qn_dve, qn_pool, qn_part = (sem(n) for n in (
            "sq_ready", "ss2_ready", "rms2_ready", "rstd2_ready", "qn_dve", "qn_pool", "qn_part"))
        t_psum, tq_done, tk_done = sem("t_psum2"), sem("tq_done"), sem("tk_done")
        sc_psum, mx_ready, nmx_ready, exp_done = (sem(n) for n in (
            "sc_psum", "mx_ready", "nmx_ready", "exp_done2"))
        tr_psum, pt_dve, pt_act, pv_done = (sem(n) for n in (
            "tr_psum", "pt_dve", "pt_act", "pv_done"))
        rinv_ready, o_done, ot_psum, ot_done, y_psum, y_done = (sem(n) for n in (
            "rinv_ready2", "o_done", "ot_psum", "ot_done", "y_psum", "y_done"))
        block = ctx.enter_context(nc.Block())

        def tile_cols(i):
            return slice(i * P, (i + 1) * P)

        @block.sync
        def _(sp):
            for dst, name in ((wemb, "wemb"), (bemb, "bemb"), (gnorm, "gnorm"), (condT, "condT"),
                              (wqkv, "wqkv"), (gqk, "gqk"), (wout, "wout"), (ident, "ident"),
                              (parity, "parity")):
                sp.dma_start(dst[:], dram[name]).then_inc(w_in, 16)

        @block.tensor
        def _(pe):
            pe.wait_ge(w_in, 144)
            for m in range(4):
                for j in range(J):
                    mm = pe.matmul(bk[7][:, m * B:(m + 1) * B], wemb[:, j, m * P:(m + 1) * P],
                                   condT[:, j, :], start=(j == 0), stop=(j == J - 1))
            mm.then_inc(emb_psum, 1)
            for n in range(B * J):
                b, j = n // J, n % J
                if n >= 4:
                    pe.wait_ge(xt_done, n - 3)
                for tc in range(TC):
                    i = b * TC + tc
                    pe.wait_ge(xn_ready, i + 1)
                    mm = pe.transpose(bk[n % 4][:, tile_cols(tc)], xn[:, i, j * P:(j + 1) * P],
                                      ident[:])
                mm.then_inc(xt_psum, 1)
            pe.wait_ge(emb_act, 4)
            for i in range(TILES):
                pe.wait_ge(xt_done, J * (i // TC + 1))
                if i >= 2:
                    pe.wait_ge(qk_done, i - 1)
                    pe.wait_ge(v_done, i - 1)
                for j in range(J):
                    mm = pe.matmul(bk[4 + i % 2][:], xnT[:, j, tile_cols(i)], wqkv[:, j, 0:2 * D],
                                   start=(j == 0), stop=(j == J - 1))
                mm.then_inc(qk_psum, 1)
                for j in range(J):
                    mm = pe.matmul(bk[6 + i % 2][:, 0:D], xnT[:, j, tile_cols(i)],
                                   wqkv[:, j, 2 * D:3 * D], start=(j == 0), stop=(j == J - 1))
                mm.then_inc(v_psum, 1)
            for b in range(B):
                pe.wait_ge(qn_dve, b + 1)
                pe.wait_ge(qn_pool, b + 1)
                for n in range(2 * J):
                    which, j = n // J, n % J
                    if b >= 1:
                        pe.wait_ge((tq_done, tk_done)[which], J * (b - 1) + j + 1)
                    for tc in range(TC):
                        mm = pe.transpose(bk[n][:, tile_cols(tc)],
                                          qk[:, b * TC + tc, which * D + j * P:which * D + (j + 1) * P],
                                          ident[:])
                    mm.then_inc(t_psum, 1)
            pe.wait_ge(tq_done, J * B)
            pe.wait_ge(tk_done, J * B)

            def score_group(g):
                i, j = g // J, g % J
                for p in range(4):
                    rows = slice(32 * p, 32 * p + 32)
                    mm = pe.matmul(bk[p][:], qT[rows, j, tile_cols(i)],
                                   kT[rows, j, i // TC].rearrange("p e t -> p (e t)"),
                                   start=True, stop=True, tile_position=(32 * p, 0))
                mm.then_inc(sc_psum, 1)

            def pv_pair(n):
                g, p = n // 4, n % 4
                i, j = g // J, g % J
                pe.wait_ge((pt_dve, pt_act)[n % 2], n // 2 + 1)
                if n % 8 == 0 and i >= 2:
                    pe.wait_ge(o_done, i - 1)
                for e in range(2):
                    h = j * 8 + p * 2 + e
                    for sc in range(TC):
                        mm = pe.matmul(bk[6 + i % 2][:, h * DH2:(h + 1) * DH2],
                                       pT[:, n % 4, (2 * e + sc) * P:(2 * e + sc + 1) * P],
                                       v[:, (i // TC) * TC + sc, h * DH2:(h + 1) * DH2],
                                       start=(sc == 0), stop=(sc == TC - 1))
                mm.then_inc(pv_done, 1)

            score_group(0)
            pe.wait_ge(v_done, TILES)
            for g in range(GROUPS):
                for p in range(4):
                    n = 4 * g + p
                    pe.wait_ge(exp_done, n + 1)
                    if n >= 2:
                        pe.wait_ge((pt_dve, pt_act)[n % 2], n // 2)
                    for e in range(2):
                        for sc in range(TC):
                            mm = pe.transpose(bk[4 + n % 2][:, (2 * e + sc) * P:(2 * e + sc + 1) * P],
                                              probs[:, g % 2, 2 * p + e, sc * P:(sc + 1) * P],
                                              ident[:])
                    mm.then_inc(tr_psum, 1)
                    if p == 3 and g + 1 < GROUPS:
                        score_group(g + 1)
                    if n >= 1:
                        pv_pair(n - 1)
            pv_pair(PAIRS - 1)
            for n in range(B * J):
                b, j = n // J, n % J
                pe.wait_ge(o_done, TC * (b + 1))
                if n >= 4:
                    pe.wait_ge(ot_done, n - 3)
                for tc in range(TC):
                    mm = pe.transpose(bk[n % 4][:, tile_cols(tc)],
                                      o[:, b * TC + tc, j * P:(j + 1) * P], ident[:])
                mm.then_inc(ot_psum, 1)
            for n in range(4):
                m, half = n % 2, n // 2
                pe.wait_ge(ot_done, 4 * (half + 1))
                for j in range(J):
                    mm = pe.matmul(bk[4 + n][:], wout[:, j, m * P:(m + 1) * P],
                                   oT[:, j, half * HALF:(half + 1) * HALF],
                                   start=(j == 0), stop=(j == J - 1))
                mm.then_inc(y_psum, 1)

        def transposed(eng, n):
            eng.wait_ge(tr_psum, n + 1)
            if n >= 4:
                eng.wait_ge(pv_done, n - 3)
            if n % 2:
                nc.scalar.activation(pT[:, n % 4, :], bk[4 + n % 2][:], ACT.Copy).then_inc(pt_act, 1)
            else:
                nc.vector.tensor_copy(pT[:, n % 4, :], bk[4 + n % 2][:]).then_inc(pt_dve, 1)

        @block.scalar
        def _(act):
            act.wait_ge(emb_psum, 1)
            for m in range(4):
                nc.scalar.activation(emb[:, m, :], bk[7][:, m * B:(m + 1) * B], ACT.Identity,
                                     bias=bemb[:, m:m + 1]).then_inc(emb_act, 1)
            act.wait_ge(ss_ready, TILES + 1)
            nc.scalar.activation(rms[:], ss[:], ACT.Sqrt, bias=epst[:],
                                 scale=1.0 / D).then_inc(rms_ready, 1)
            act.wait_ge(gain_ready, 2)
            for n in range(B * J):
                b, j = n // J, n % J
                act.wait_ge(xt_psum, n + 1)
                nc.scalar.activation(xnT[:, j, b * T:(b + 1) * T], bk[n % 4][:, 0:T], ACT.Identity,
                                     bias=emb[:, J + j, b:b + 1],
                                     scale=gain[:, j, b:b + 1]).then_inc(xt_done, 1)
            for i in range(TILES):
                act.wait_ge(qk_psum, i + 1)
                nc.scalar.activation(qk[:, i, :], bk[4 + i % 2][:], ACT.Copy).then_inc(qk_done, 1)
            act.wait_ge(ss2_ready, TILES)
            nc.scalar.activation(rms2[:].rearrange("p i h -> p (i h)"),
                                 ss2[:].rearrange("p i h -> p (i h)"), ACT.Sqrt, bias=epst[:],
                                 scale=1.0 / DH2).then_inc(rms2_ready, 1)
            for b in range(B):
                for j in range(J):
                    act.wait_ge(t_psum, 2 * J * b + j + 1)
                    nc.scalar.activation(qT[:, j, b * T:(b + 1) * T], bk[j][:, 0:T],
                                         ACT.Copy).then_inc(tq_done, 1)
            for g in range(GROUPS):
                i, j = g // J, g % J
                act.wait_ge(nmx_ready, g + 1)
                if g >= 2:
                    act.wait_ge(tr_psum, 4 * (g - 1))
                for p in range(4):
                    n = 4 * g + p
                    for e in range(2):
                        h = j * 8 + p * 2 + e
                        a = nc.scalar.activation(probs[:, g % 2, 2 * p + e, :],
                                                 bk[p][:, e * T:(e + 1) * T], ACT.Exp,
                                                 bias=nmx[:, g % 2, 2 * p + e:2 * p + e + 1],
                                                 scale=scale, accum_out=rsum[:, i, h:h + 1])
                    a.then_inc(exp_done, 1)
                    if n % 2 == 1 and n >= 3:
                        transposed(act, n - 2)
                if g == GROUPS - 1:
                    transposed(act, PAIRS - 1)
            for n in range(B * J):
                b, j = n // J, n % J
                act.wait_ge(ot_psum, n + 1)
                nc.scalar.activation(oT[:, j, b * T:(b + 1) * T], bk[n % 4][:, 0:T],
                                     ACT.Copy).then_inc(ot_done, 1)

        @block.vector
        def _(dve):
            nc.vector.memset(epst[:], eps).then_inc(ss_ready, 1)
            for i in range(TILES):
                nc.vector.tensor_tensor_reduce(out=junk[:], in0=x1[:, i, :], in1=x1[:, i, :],
                                               scale=1.0, scalar=0.0, op0=ALU.mult, op1=ALU.add,
                                               accum_out=ss[:, i:i + 1]).then_inc(ss_ready, 1)
                dve.wait_ge(ss_ready, i + 2)
            dve.wait_ge(emb_act, 4)
            nc.vector.tensor_scalar(gain[:].rearrange("p j b -> p (j b)"),
                                    emb[:, 0:J, :].rearrange("p j b -> p (j b)"), 1.0, None,
                                    ALU.add).then_inc(gain_ready, 1)
            dve.wait_ge(gain_ready, 1)
            for j in range(J):
                a = nc.vector.tensor_scalar(gain[:, j, :], gain[:, j, :], gnorm[:, j:j + 1], None,
                                            ALU.mult)
            a.then_inc(gain_ready, 1)
            dve.wait_ge(rms_ready, 1)
            nc.vector.reciprocal(rstd[:], rms[:]).then_inc(rstd_ready, 1)
            dve.wait_ge(rstd_ready, 1)
            for i in range(TILES):
                nc.vector.tensor_scalar(xn[:, i, :], x1[:, i, :], rstd[:, i:i + 1], None,
                                        ALU.mult).then_inc(xn_ready, 1)
            for i in range(TILES):
                dve.wait_ge(v_psum, i + 1)
                nc.vector.tensor_copy(v[:, i, :], bk[6 + i % 2][:, 0:D]).then_inc(v_done, 1)
                dve.wait_ge(sq_ready, i + 1)
                nc.vector.tensor_reduce(ss2[:, i, :], sq[:, i % 2].rearrange("p (h d) -> p h d", d=DH2),
                                        AX.X, ALU.add).then_inc(ss2_ready, 1)
            dve.wait_ge(rms2_ready, 1)
            nc.vector.reciprocal(rstd2[:].rearrange("p i h -> p (i h)"),
                                 rms2[:].rearrange("p i h -> p (i h)")).then_inc(rstd2_ready, 1)
            dve.wait_ge(rstd2_ready, 1)
            for b in range(B):
                i = b * TC
                q3 = qk[:, i].rearrange("p (h d) -> p h d", d=DH2)
                nc.vector.tensor_tensor(q3, q3, rstd2[:, i, :].unsqueeze(2).to_broadcast([P, 32, DH2]),
                                        ALU.mult).then_inc(qn_part, 1)
                dve.wait_ge(qn_part, b + 1)
                nc.vector.tensor_tensor(qk[:, i], qk[:, i], gqk[:], ALU.mult).then_inc(qn_dve, 1)
                for j in range(J):
                    dve.wait_ge(t_psum, 2 * J * b + J + j + 1)
                    for e in range(2):
                        a = nc.vector.tensor_scalar(kT[:, j, b, e, :], bk[J + j][:, 0:T],
                                                    parity[:, e:e + 1], None, ALU.mult)
                    a.then_inc(tk_done, 1)

            def maxima(g):
                dve.wait_ge(sc_psum, g + 1)
                for p in range(4):
                    a = nc.vector.tensor_reduce(mx[:, g % 2, 2 * p:2 * p + 2],
                                                bk[p][:].rearrange("p (e t) -> p e t", e=2),
                                                AX.X, ALU.max)
                a.then_inc(mx_ready, 1)
                dve.wait_ge(mx_ready, g + 1)
                if g >= 2:
                    dve.wait_ge(exp_done, 4 * (g - 1))
                nc.vector.tensor_scalar(nmx[:, g % 2, :], mx[:, g % 2, :], -scale, None,
                                        ALU.mult).then_inc(nmx_ready, 1)

            def normalise(i):
                dve.wait_ge(exp_done, 8 * (i + 1))
                nc.vector.reciprocal(rinv[:, i, :], rsum[:, i, :]).then_inc(rinv_ready, 1)
                dve.wait_ge(rinv_ready, i + 1)
                dve.wait_ge(pv_done, 8 * (i + 1))
                nc.vector.tensor_tensor(o[:, i, :].rearrange("p (h d) -> p h d", d=DH2),
                                        bk[6 + i % 2][:, 0:D].rearrange("p (h d) -> p h d", d=DH2),
                                        rinv[:, i, :].unsqueeze(2).to_broadcast([P, H2, DH2]),
                                        ALU.mult).then_inc(o_done, 1)

            maxima(0)
            for g in range(GROUPS):
                transposed(dve, 4 * g)
                if g % 2 == 0 and g >= 2:
                    normalise(g // 2 - 1)
                transposed(dve, 4 * g + 2)
                if g + 1 < GROUPS:
                    maxima(g + 1)
            normalise(TILES - 1)
            for n in range(4):
                m, half = n % 2, n // 2
                dve.wait_ge(y_psum, n + 1)
                nc.vector.tensor_tensor(yT[:, m, half * HALF:(half + 1) * HALF], bk[4 + n][:],
                                        oT[:, m, half * HALF:(half + 1) * HALF],
                                        ALU.add).then_inc(y_done, 1)

        @block.gpsimd
        def _(pool):
            for i in range(TILES):
                pool.wait_ge(qk_done, i + 1)
                if i >= 2:
                    pool.wait_ge(ss2_ready, i - 1)
                nc.gpsimd.tensor_tensor(sq[:, i % 2], qk[:, i], qk[:, i], ALU.mult).then_inc(sq_ready, 1)
            pool.wait_ge(rstd2_ready, 1)
            for b in range(B):
                i = b * TC + 1
                q3 = qk[:, i].rearrange("p (h d) -> p h d", d=DH2)
                nc.gpsimd.tensor_tensor(q3, q3, rstd2[:, i, :].unsqueeze(2).to_broadcast([P, 32, DH2]),
                                        ALU.mult).then_inc(sq_ready, 1)
                pool.wait_ge(sq_ready, TILES + b + 1)
                nc.gpsimd.tensor_tensor(qk[:, i], qk[:, i], gqk[:], ALU.mult).then_inc(qn_pool, 1)


def ffn_block(nc, dram, x1, yT, out):
    R17 = E + 1
    PAD = 4
    with ExitStack() as ctx:
        def sb(name, shape, dt=F32):
            return ctx.enter_context(nc.sbuf_tensor(name, shape, dt))

        def sem(name):
            return ctx.enter_context(nc.semaphore(name))

        gw = sb("gw", [P, J, R17])
        ident = sb("ident_d", [P, P])
        wf = sb("wf", [P, 2, 7 * P])
        lg = sb("lg", [P, TILES, R17])
        mx = sb("mxr", [P, TILES])
        ex = sb("ex", [P, TILES, E])
        pr = sb("pr", [P, TILES, E + PAD])
        den = sb("den", [P, TILES])
        rden = sb("rden", [P, TILES])
        top = sb("top", [P, TILES, 8])
        rep = sb("rep", [P, TILES, E + PAD])
        cw = sb("cw", [P, TILES, R17])
        es = sb("es", [P, TILES])
        cwT = sb("cwT", [R17, NT])
        act_g = sb("act_g", [P, 2, HALF])
        prod = sb("prod", [P, 2, HALF])
        hT = sb("hT", [P, 2, HALF])
        fin = sb("fin", [P, TILES, D])
        acc = [ctx.enter_context(nc.psum_tensor(f"fa{i}", [P, HALF], F32)) for i in range(4)]
        GB, UB, CB, XB = [ctx.enter_context(nc.psum_tensor(f"fb{i}", [P, HALF], F32))
                          for i in range(4)]
        w_in = sem("w_in3")
        wf_in = [sem(f"wf_in{par}") for par in range(2)]
        lg_psum, chain, exps, cw_ready, ct_psum, ct_done, es_done = (sem(n) for n in (
            "lg_psum", "chain", "exps", "cw_ready", "ct_psum", "ct_done", "es_done"))
        g_psum, u_psum, c_psum, d_done = (sem(n) for n in ("g_psum", "u_psum", "c_psum", "d_done"))
        g_act, prod_ready, h_ready, fin_ready, stored = (sem(n) for n in (
            "g_act", "prod_ready", "hid_ready", "fin_ready", "stored"))
        block = ctx.enter_context(nc.Block())

        @block.sync
        def _(sp):
            sp.dma_start(gw[:], dram["gw"]).then_inc(w_in, 16)
            sp.dma_start(ident[:], dram["ident"]).then_inc(w_in, 16)
            sp.dma_start(wf[:, 0], dram["wf"][0]).then_inc(wf_in[0], 16)
            sp.dma_start(wf[:, 1], dram["wf"][1]).then_inc(wf_in[1], 16)
            with sp.Fori(0, NCH // 2 - 1) as i:
                for par in range(2):
                    sp.wait_ge(d_done, i * 4 + 2 * par + 2)
                    sp.dma_start(wf[:, par], dram["wf"][bass.ds(i * 2 + 2 + par, 1)]
                                 .rearrange("o p n -> (o p) n")).then_inc(wf_in[par], 16)
            out_rows = out.rearrange("(i p) d -> p i d", p=P)
            for a in range(4):
                sp.wait_ge(fin_ready, a + 1)
                sp.dma_start(out_rows[:, 2 * a:2 * a + 2, :],
                             fin[:, 2 * a:2 * a + 2, :]).then_inc(stored, 16)
            sp.wait_ge(stored, 64)

        @block.tensor
        def _(pe):
            pe.wait_ge(w_in, 32)
            for i in range(TILES):
                for j in range(J):
                    mm = pe.matmul(XB[:, i * R17:(i + 1) * R17], yT[:, j, i * P:(i + 1) * P],
                                   gw[:, j, :], start=(j == 0), stop=(j == J - 1))
            mm.then_inc(lg_psum, 1)
            for i in range(TILES):
                pe.matmul(acc[i // 2][:, (i % 2) * D:(i % 2 + 1) * D], ident[:], x1[:, i, :],
                          start=(i % 2 == 0), stop=False, skip_group_check=True)
            pe.wait_ge(cw_ready, 2)
            for i in range(TILES):
                mm = pe.matmul((GB, UB)[i // 4][0:R17, (i % 4) * P:(i % 4 + 1) * P], cw[:, i, :],
                               ident[:], start=True, stop=True)
            mm.then_inc(ct_psum, 1)
            pe.wait_ge(ct_done, 2)
            with pe.Fori(0, NCH // 2) as i:
                for par in range(2):
                    c2 = i * 4 + par * 2
                    pe.wait_ge(wf_in[par], 16 * i + 16)
                    for hf in range(2):
                        u = c2 + hf
                        cols = slice(hf * HALF, (hf + 1) * HALF)
                        pe.wait_ge(g_act, u + 1)
                        for j in range(J):
                            mm = pe.matmul(GB[:], wf[:, par, j * P:(j + 1) * P], yT[:, j, cols],
                                           start=(j == 0), stop=(j == J - 1))
                        mm.then_inc(g_psum, 1)
                        pe.wait_ge(prod_ready, u + 1)
                        for j in range(J):
                            mm = pe.matmul(UB[:], wf[:, par, (J + j) * P:(J + j + 1) * P],
                                           yT[:, j, cols], start=(j == 0), stop=(j == J - 1))
                        mm.then_inc(u_psum, 1)
                        pe.wait_ge(h_ready, u + 1)
                        pe.matmul(CB[:], wf[0:R17, par, 6 * P:7 * P], cwT[:, cols],
                                  start=True, stop=True).then_inc(c_psum, 1)
                    for hf in range(2):
                        pe.wait_ge(h_ready, c2 + hf + 2)
                        for t4 in range(4):
                            i8 = hf * 4 + t4
                            mm = pe.matmul(acc[i8 // 2][:, (i8 % 2) * D:(i8 % 2 + 1) * D],
                                           hT[:, hf, t4 * P:(t4 + 1) * P],
                                           wf[:, par, 4 * P:4 * P + D], start=False, stop=False,
                                           skip_group_check=True)
                        mm.then_inc(d_done, 1)

        @block.scalar
        def _(act):
            act.wait_ge(chain, 3)
            nc.scalar.activation(ex[:].rearrange("p i e -> p (i e)"),
                                 ex[:].rearrange("p i e -> p (i e)"), ACT.Exp).then_inc(exps, 1)
            nc.scalar.activation(es[:], lg[:, :, E], ACT.Exp, scale=-1.0).then_inc(es_done, 1)
            with act.Fori(0, NCH // 2) as i:
                for k in range(4):
                    u = i * 4 + k
                    act.wait_ge(g_psum, u + 1)
                    act.wait_ge(prod_ready, u + 1)
                    nc.scalar.activation(act_g[:, k % 2, :], GB[:], ACT.Silu).then_inc(g_act, 1)

        @block.vector
        def _(dve):
            def link(a, n):
                a.then_inc(chain, 1)
                dve.wait_ge(chain, n)
            dve.wait_ge(lg_psum, 1)
            link(nc.vector.tensor_copy(lg[:].rearrange("p i e -> p (i e)"),
                                       XB[:, 0:TILES * R17]), 1)
            link(nc.vector.tensor_reduce(mx[:], lg[:, :, 0:E], AX.X, ALU.max), 2)
            link(nc.vector.tensor_tensor(ex[:], lg[:, :, 0:E],
                                         mx[:].unsqueeze(2).to_broadcast([P, TILES, E]),
                                         ALU.subtract), 3)
            link(nc.vector.memset(pr[:], -1.0), 4)
            dve.wait_ge(exps, 1)
            link(nc.vector.tensor_reduce(den[:], ex[:], AX.X, ALU.add), 5)
            link(nc.vector.reciprocal(rden[:], den[:]), 6)
            link(nc.vector.tensor_tensor(pr[:, :, 0:E], ex[:],
                                         rden[:].unsqueeze(2).to_broadcast([P, TILES, E]),
                                         ALU.mult), 7)
            for i in range(TILES):
                a = nc.vector.max(top[:, i, :], pr[:, i, 0:E])
            link(a, 8)
            link(nc.vector.memset(top[:, :, TOPK:8], -1.0), 9)
            for i in range(TILES):
                a = nc.vector.match_replace(rep[:, i, :], top[:, i, :], pr[:, i, :], -2.0)
            link(a, 10)
            link(nc.vector.tensor_reduce(den[:], top[:, :, 0:TOPK], AX.X, ALU.add), 11)
            link(nc.vector.reciprocal(rden[:], den[:]), 12)
            link(nc.vector.scalar_tensor_tensor(out=cw[:, :, 0:E], in0=rep[:, :, 0:E], scalar=0.0,
                                                in1=pr[:, :, 0:E], op0=ALU.is_lt, op1=ALU.mult), 13)
            nc.vector.tensor_tensor(cw[:, :, 0:E], cw[:, :, 0:E],
                                    rden[:].unsqueeze(2).to_broadcast([P, TILES, E]),
                                    ALU.mult).then_inc(cw_ready, 1)
            dve.wait_ge(es_done, 1)
            link(nc.vector.tensor_scalar(es[:], es[:], 1.0, None, ALU.add), 14)
            nc.vector.reciprocal(cw[:, :, E], es[:]).then_inc(cw_ready, 1)
            dve.wait_ge(ct_psum, 1)
            nc.vector.tensor_copy(cwT[:, 0:HALF], GB[0:R17, :]).then_inc(ct_done, 1)
            nc.vector.tensor_copy(cwT[:, HALF:NT], UB[0:R17, :]).then_inc(ct_done, 1)
            nc.vector.memset(act_g[:], 0.0).then_inc(g_act, 1)
            nc.vector.memset(prod[:], 0.0).then_inc(prod_ready, 1)
            nc.vector.memset(hT[:], 0.0).then_inc(h_ready, 1)
            with dve.Fori(0, NCH // 2) as i:
                for k in range(4):
                    u = i * 4 + k
                    dve.wait_ge(g_act, u + 2)
                    dve.wait_ge(u_psum, u + 1)
                    nc.vector.tensor_tensor(prod[:, k % 2, :], UB[:], act_g[:, k % 2, :],
                                            ALU.mult).then_inc(prod_ready, 1)
                    dve.wait_ge(prod_ready, u + 2)
                    dve.wait_ge(c_psum, u + 1)
                    nc.vector.tensor_tensor(hT[:, k % 2, :], CB[:], prod[:, k % 2, :],
                                            ALU.mult).then_inc(h_ready, 1)
            dve.wait_ge(d_done, 2 * NCH)
            for a in range(4):
                nc.vector.tensor_copy(fin[:, 2 * a:2 * a + 2, :].rearrange("p i d -> p (i d)"),
                                      acc[a][:]).then_inc(fin_ready, 1)


def program(nc, dram, out):
    with ExitStack() as ctx:
        def sb(name, shape):
            return ctx.enter_context(nc.sbuf_tensor(name, shape, F32))
        gruT = sb("gruT", [P, J, B, T])
        x1 = sb("x1", [P, TILES, D])
        yT = sb("yT", [P, J, NT])
        gru_block(nc, dram, gruT)
        attention_block(nc, dram, gruT, x1)
        adaln_block(nc, dram, x1, yT)
        ffn_block(nc, dram, x1, yT, out)


def laid_out(x, cond_2048, L0_cond_W_ih, L0_cond_W_hh, L0_cond_b_ih, L0_cond_b_hh, **w):
    def rows_in(a):
        return np.ascontiguousarray(a.reshape(J, P, -1).transpose(1, 0, 2))

    def cols(a):
        return np.ascontiguousarray(a.reshape(-1, P).T)

    def heads_of(w):
        return w.reshape(J, P, H1, DH1).transpose(2, 1, 0, 3).reshape(H1, P, J * DH1)

    tri = np.where(np.tri(P, dtype=bool), 0.0, -1e30).astype(np.float32)
    d = {
        "wq": np.concatenate([heads_of(w["L0_attn_Wq"]), w["L0_attn_bq"].reshape(H1, P, 1)], 2),
        "wkv": np.concatenate([heads_of(w["L0_attn_Wk"]), heads_of(w["L0_attn_Wv"]),
                               w["L0_attn_bk"].reshape(H1, P, 1)], 2),
        "wo": np.concatenate([w["L0_attn_Wo"].reshape(H1, P, D),
                              w["L0_attn_bv"].reshape(H1, P, 1)], 2),
        "bo": w["L0_attn_bo"].reshape(1, D),
        "mask": np.concatenate([tri, np.zeros((P, P), np.float32), tri], 1),
        "xr": np.ascontiguousarray(x.reshape(TILES, P, D).transpose(1, 0, 2)),
        "xT": rows_in(x.reshape(NT, D).T),
        "wih": rows_in(L0_cond_W_ih), "whh": rows_in(L0_cond_W_hh),
        "bias_ih": cols(L0_cond_b_ih), "bias_hh": cols(L0_cond_b_hh),
        "condT": rows_in(cond_2048.T), "ident": np.eye(P, dtype=np.float32),
    }
    def hidden(gu, shared):
        a = np.concatenate([gu.reshape(E * INTER, D), shared])
        return np.concatenate([a, np.zeros((NCH * P - HID, D), a.dtype)])

    def in_chunks(a):
        return a.reshape(NCH, P, J, P).transpose(0, 3, 2, 1).reshape(NCH, P, J * P)

    gu, sgu = w["L0_ffn_expert_gate_up"], w["L0_ffn_shared_gate_up"]
    down = hidden(w["L0_ffn_expert_down"].transpose(0, 2, 1), w["L0_ffn_shared_down"].T)
    owner = np.minimum(np.arange(NCH * P) // INTER, E)
    owner[HID:] = -1
    select = (owner[None, :] == np.arange(P)[:, None]).astype(np.float32)
    d.update({
        "wemb": rows_in(w["L0_cond2_W_emb"]), "bemb": cols(w["L0_cond2_b_emb"]),
        "gnorm": cols(w["L0_cond2_g_norm"]), "wqkv": rows_in(w["L0_cond2_W_qkv"]),
        "gqk": np.broadcast_to(np.concatenate([np.tile(w["L0_cond2_g_q"], H2),
                                               np.tile(w["L0_cond2_g_k"], H2)]), (P, 2 * D)),
        "wout": rows_in(w["L0_cond2_W_out"]),
        "parity": (np.arange(P)[:, None] // DH2 % 2 == np.arange(2)).astype(np.float32),
        "gw": rows_in(np.concatenate([w["L0_ffn_gate_w"], w["L0_ffn_shared_gate_vec"]]).T),
        "wf": np.concatenate([in_chunks(hidden(gu[:, :INTER], sgu[:SHARED])),
                              in_chunks(hidden(gu[:, INTER:], sgu[SHARED:])),
                              down.reshape(NCH, P, D),
                              select.reshape(P, NCH, P).transpose(1, 0, 2)], 2),
    })
    return {k: np.ascontiguousarray(a) for k, a in d.items()}


def kernel(**inputs):
    import concourse.bacc as bacc
    from concourse.bass_utils import run_bass_kernel_spmd

    arrays = laid_out(**{k: np.asarray(v) for k, v in inputs.items()})
    nc = bacc.Bacc("TRN2", target_bir_lowering=False, num_devices=1)
    dram = {n: nc.dram_tensor(f"in_{n}", a.shape, F32, kind="ExternalInput").ap()
            for n, a in arrays.items()}
    out = nc.dram_tensor("out", [NT, D], F32, kind="ExternalOutput").ap()
    program(nc, dram, out)
    result = run_bass_kernel_spmd(nc, [{f"in_{n}": a for n, a in arrays.items()}], core_ids=[0])
    return result.results[0]["out"].reshape(B, T, D)
```

```python
from contextlib import ExitStack

import numpy as np

import concourse.bass as bass
from concourse import mybir

P = 128
F32 = mybir.dt.float32
F32R = mybir.dt.float32r
BF16 = mybir.dt.bfloat16
ACT = mybir.ActivationFunctionType
ALU = mybir.AluOpType
AX = mybir.AxisListType

B, T, D = 4, 256, 256
J = D // P
NT = B * T
TILES = NT // P
HALF = 512
H1, DH1 = 16, 128
H2, DH2 = 16, 16
TC = T // P
E, TOPK, INTER, SHARED = 16, 4, 176, 704
HID = E * INTER + SHARED
NCH = -(-HID // P)
U = 8


class Count:

    def __init__(self, sem):
        self.sem, self.n = sem, 0

    def inc(self, instruction, by=1):
        instruction.then_inc(self.sem, by)
        self.n += by
        return self.n


def gru_block(nc, dram, gruT):
    with ExitStack() as ctx:
        def sb(name, shape, dt=F32):
            return ctx.enter_context(nc.sbuf_tensor(name, shape, dt))

        def sem(name):
            return ctx.enter_context(nc.semaphore(name))

        xT = sb("xT", [P, J, NT])
        wih = sb("wih", [P, J, 3 * D])
        whh = sb("whh", [P, J, 3 * D])
        whh_rest = sb("whh_rest", [P, 2, J, 3 * D])
        whh_part = sb("whh_part", [P, 3, J, 3 * D], BF16)
        bias_ih = sb("bias_ih", [P, 6])
        bias_hh = sb("bias_hh", [P, 6])
        bias_g = sb("bias_g", [P, 4])
        ident = sb("ident_f", [P, P])
        identb = sb("ident_b", [P, P], BF16)
        condT = sb("condT", [P, J, B])
        gates = [sb(f"gates{q}", [P, T, 24]) for q in range(3)]
        bhn = sb("bhn", [P, 3, 8])
        hs = sb("hs", [P, 2, 3, 16])
        r_scan = sb("r_scan", [P, 32])
        t_scan = sb("t_scan", [P, 32])
        u_scan = sb("u_scan", [P, 16])
        nv_scan = sb("nv_scan", [P, 16])
        r_sum = sb("r_sum", [P, 8])
        z_sum = sb("z_sum", [P, 8])
        z_gate = sb("z_gate", [P, 8])
        bank = [ctx.enter_context(nc.psum_tensor(f"gb{i}", [P, HALF], F32)) for i in range(7)]
        R, Z, N = bank[4:7]

        loaded = {n: sem(f"ld_{n}") for n in ("x", "wih", "whh", "small")}
        gi_psum, gi_sbuf, bias_ready = sem("gi_psum"), sem("gi_sbuf"), sem("bias_ready")
        split_dve, split_pool = sem("split_dve"), sem("split_pool")
        r_psum, z_psum, scan_in = sem("r_psum"), sem("z_psum"), sem("scan_in")
        r_sum_ready, z_sum_ready, z_ready = sem("r_sum_ready"), sem("z_sum_ready"), sem("z_ready")
        npre_ready, hin_ready = sem("npre_ready"), sem("hin_ready")
        h_new, h_rest, h_ready, h_stored = sem("h_new"), sem("h_rest"), sem("h_ready"), sem("h_stored")

        def high(ap):
            return ap.bitcast(BF16)[:, 1::2]

        def part(par, q):
            return hs[:, par, q, 1::2]

        def part_high(par, q):
            return hs[:, par, q, :].bitcast(BF16)[:, 3::4]

        block = ctx.enter_context(nc.Block())

        @block.sync
        def _(sp):
            sp.dma_start(xT[:], dram["xT"]).then_inc(loaded["x"], 16)
            sp.dma_start(wih[:], dram["wih"]).then_inc(loaded["wih"], 16)
            sp.dma_start(whh[:], dram["whh"]).then_inc(loaded["whh"], 16)
            for dst, name in ((bias_ih, "bias_ih"), (bias_hh, "bias_hh"), (condT, "condT"),
                              (ident, "ident")):
                sp.dma_start(dst[:], dram[name]).then_inc(loaded["small"], 16)

        @block.tensor
        def _(pe):
            pe.wait_ge(loaded["x"], 16)
            pe.wait_ge(loaded["wih"], 16)
            for n in range(12):
                m, half = n // 2, n % 2
                if n >= 4:
                    pe.wait_ge(gi_sbuf, n - 3)
                for j in range(J):
                    mm = pe.matmul(bank[n % 4][:], wih[:, j, m * P:(m + 1) * P],
                                   xT[:, j, half * HALF:(half + 1) * HALF],
                                   start=(j == 0), stop=(j == J - 1))
                mm.then_inc(gi_psum, 1)
            pe.wait_ge(split_dve, 1)
            pe.wait_ge(split_pool, 1)
            with pe.Fori(0, T // U) as i:
                for k in range(U):
                    t, cur = i * U + k, k % 2
                    pe.wait_ge(z_sum_ready, t + 1)
                    for q in range(3):
                        for dst, c0 in ((R, 0), (Z, 8)):
                            g = gates[q][:, bass.ds(t, 1), c0:c0 + 8].rearrange("p a b -> p (a b)")
                            pe.matmul(dst[:, 0:24:3], identb[:], high(g), start=(q == 0),
                                      stop=False, skip_group_check=True)
                    pe.wait_ge(npre_ready, t + 1)
                    for q in range(3):
                        g = gates[q][:, bass.ds(t, 1), 16:24].rearrange("p a b -> p (a b)")
                        pe.matmul(N[:, 3:32:4], identb[:], high(g), start=(q == 0), stop=False,
                                  skip_group_check=True)
                        pe.matmul(N[:, 0:32:4], identb[:], high(bhn[:, q, :]), start=False,
                                  stop=False, skip_group_check=True)
                    pe.wait_ge(h_ready, t + 1)
                    for dst, width, m0, done in ((R, 3, 0, r_psum), (Z, 3, 2, z_psum),
                                                 (N, 4, 4, scan_in)):
                        for mi in range(J):
                            out = dst[:, mi * B * width:(mi + 1) * B * width] \
                                .rearrange("p (b q) -> p b q", q=width)[:, :, 0:3]
                            for q in range(3):
                                for j in range(J):
                                    w = whh_part[:, q, j, (m0 + mi) * P:(m0 + mi + 1) * P]
                                    h = hs[:, cur, :, 8 * j:8 * j + 8].bitcast(BF16)[:, :, 3::4] \
                                        .rearrange("p q b -> p b q")
                                    mm = pe.matmul(out, w, h, start=False, stop=False,
                                                   skip_group_check=True)
                        mm.then_inc(done, 1)

        @block.scalar
        def _(act):
            act.wait_ge(bias_ready, 1)
            for n in range(12):
                m, half = n // 2, n % 2
                gate, mi = m // 2, m % 2
                act.wait_ge(gi_psum, n + 1)
                c0 = gate * 8 + mi * B + half * 2
                out = gates[0][:, :, c0:c0 + 2].rearrange("p t b -> p b t")
                bias = bias_g[:, m:m + 1] if gate < 2 else bias_ih[:, m:m + 1]
                nc.scalar.activation(out, bank[n % 4][:].rearrange("p (b t) -> p b t", b=2),
                                     ACT.Identity, bias=bias).then_inc(gi_sbuf, 1)
            with act.Fori(0, T // U) as i:
                for k in range(U):
                    t = i * U + k
                    act.wait_ge(r_sum_ready, t + 1)
                    nc.scalar.activation(r_scan[:, 3::4], r_sum[:], ACT.Sigmoid).then_inc(scan_in, 1)
                    act.wait_ge(z_sum_ready, t + 2)
                    nc.scalar.activation(z_gate[:], z_sum[:], ACT.Sigmoid).then_inc(z_ready, 1)
                    nc.scalar.activation(u_scan[:, 1::2], z_sum[:], ACT.Sigmoid, scale=-1.0)
                    act.wait_ge(npre_ready, t + 2)
                    nc.scalar.activation(nv_scan[:, 0::2], t_scan[:, 3::4],
                                         ACT.Tanh).then_inc(hin_ready, 1)

        @block.vector
        def _(dve):
            dve.wait_ge(loaded["small"], 64)
            nc.vector.tensor_tensor(bias_g[:], bias_ih[:, 0:4], bias_hh[:, 0:4],
                                    ALU.add).then_inc(bias_ready, 1)
            nc.vector.memset(r_scan[:], 0.0).then_inc(bias_ready, 1)
            nc.vector.memset(u_scan[:], 0.0).then_inc(bias_ready, 1)
            nc.vector.memset(hs[:], 0.0).then_inc(bias_ready, 1)
            dve.wait_ge(bias_ready, 4)
            nc.vector.memset(r_scan[:, 1::4], 1.0).then_inc(bias_ready, 1)
            nc.vector.memset(r_scan[:, 2::4], 1.0).then_inc(bias_ready, 1)
            nc.vector.tensor_copy(identb[:], ident[:]).then_inc(bias_ready, 1)
            nc.vector.memset(bhn[:], 0.0).then_inc(bias_ready, 1)
            dve.wait_ge(bias_ready, 8)
            for mi in range(J):
                nc.vector.tensor_scalar(bhn[:, 0, mi * B:(mi + 1) * B], bhn[:, 0, mi * B:(mi + 1) * B],
                                        bias_hh[:, 4 + mi:5 + mi], None,
                                        ALU.add).then_inc(bias_ready, 1)
            nc.vector.tensor_copy(part(0, 0), condT[:].rearrange("p j b -> p (j b)")) \
                .then_inc(bias_ready, 1)
            dve.wait_ge(bias_ready, 11)
            dve.wait_ge(loaded["whh"], 16)
            src = whh[:].rearrange("p j n -> p (j n)")
            for q in range(3):
                if q < 2:
                    rest = whh_rest[:, q].rearrange("p j n -> p (j n)")
                    nc.vector.tensor_tensor(rest, src, high(src), ALU.subtract).then_inc(bias_ready, 1)
                    nc.vector.tensor_tensor(bhn[:, q + 1, :], bhn[:, q, :], high(bhn[:, q, :]),
                                            ALU.subtract).then_inc(bias_ready, 1)
                    nc.vector.tensor_tensor(part(0, q + 1), part(0, q), part_high(0, q),
                                            ALU.subtract).then_inc(bias_ready, 1)
                nc.vector.tensor_copy(whh_part[:, q].rearrange("p j n -> p (j n)"),
                                      high(src)).then_inc(bias_ready, 1)
                if q < 2:
                    dve.wait_ge(bias_ready, 15 + 4 * q)
                    src = rest
            dve.wait_ge(gi_sbuf, 12)
            for q in range(2):
                a = gates[q][:, 0:T // 2, :].rearrange("p t c -> p (t c)")
                o = gates[q + 1][:, 0:T // 2, :].rearrange("p t c -> p (t c)")
                nc.vector.tensor_tensor(o, a, high(a), ALU.subtract).then_inc(bias_ready, 1)
                dve.wait_ge(bias_ready, 21 + q)
            nc.vector.memset(t_scan[:], 0.0).then_inc(npre_ready, 1)
            nc.vector.memset(r_sum[:], 0.0).then_inc(z_sum_ready, 1)
            nc.vector.memset(z_sum[:], 0.0).then_inc(h_ready, 1)
            nc.vector.memset(nv_scan[:], 0.0).then_inc(split_dve, 1)
            with dve.Fori(0, T // U) as i:
                for k in range(U):
                    t, cur = i * U + k, k % 2
                    nxt = 1 - cur
                    dve.wait_ge(r_psum, t + 1)
                    nc.vector.tensor_reduce(r_sum[:], R[:, 0:24].rearrange("p (m q) -> p m q", q=3),
                                            AX.X, ALU.add).then_inc(r_sum_ready, 1)
                    dve.wait_ge(z_psum, t + 1)
                    nc.vector.tensor_reduce(z_sum[:], Z[:, 0:24].rearrange("p (m q) -> p m q", q=3),
                                            AX.X, ALU.add).then_inc(z_sum_ready, 1)
                    dve.wait_ge(scan_in, 2 * t + 2)
                    nc.vector.tensor_tensor_scan(t_scan[:], r_scan[:], N[:, 0:32], 0.0, ALU.mult,
                                                 ALU.add).then_inc(npre_ready, 1)
                    dve.wait_ge(z_ready, t + 1)
                    nc.vector.tensor_tensor(nv_scan[:, 1::2], z_gate[:], part(cur, 0),
                                            ALU.mult).then_inc(hin_ready, 1)
                    dve.wait_ge(h_stored, t + 1)
                    dve.wait_ge(hin_ready, 2 * t + 2)
                    nc.vector.tensor_tensor_scan(hs[:, nxt, 0, :], u_scan[:], nv_scan[:], 0.0,
                                                 ALU.mult, ALU.add).then_inc(h_new, 1)
                    dve.wait_ge(h_new, t + 1)
                    nc.vector.tensor_tensor(part(nxt, 1), part(nxt, 0), part_high(nxt, 0),
                                            ALU.subtract).then_inc(h_rest, 1)
                    dve.wait_ge(h_rest, t + 1)
                    nc.vector.tensor_tensor(part(nxt, 2), part(nxt, 1), part_high(nxt, 1),
                                            ALU.subtract).then_inc(h_ready, 1)

        @block.gpsimd
        def _(pool):
            pool.wait_ge(gi_sbuf, 12)
            for q in range(2):
                a = gates[q][:, T // 2:T, :].rearrange("p t c -> p (t c)")
                o = gates[q + 1][:, T // 2:T, :].rearrange("p t c -> p (t c)")
                (nc.gpsimd.tensor_tensor(o, a, high(a), ALU.subtract)
                 .then_inc(split_pool if q else h_stored, 1))
                if q == 0:
                    pool.wait_ge(h_stored, 1)
            with pool.Fori(0, T // U) as i:
                for k in range(U):
                    t, nxt = i * U + k, 1 - k % 2
                    pool.wait_ge(h_new, t + 1)
                    nc.gpsimd.tensor_copy(
                        gruT[:, :, :, bass.ds(t, 1)].rearrange("p j b o -> p (j b o)"),
                        part(nxt, 0)).then_inc(h_stored, 1)


def attention_block(nc, dram, gruT, x1):
    scale = float(DH1) ** -0.5
    units = H1 * B
    with ExitStack() as ctx:
        def sb(name, shape, dt=F32):
            return ctx.enter_context(nc.sbuf_tensor(name, shape, dt))

        def sem(name):
            return ctx.enter_context(nc.semaphore(name))

        QT = sb("QT", [P, B, T, H1])
        wq = sb("wq", [P, 2, J * P + 1])
        wkv = sb("wkv", [P, 2, 2 * J * P + 1])
        wo = sb("wo", [P, 2, D + 1])
        qh = sb("qh", [P, 2, B, T])
        kh = sb("kh", [P, 2, B, T])
        vh = sb("vh", [P, 2, B, TC * DH1])
        logits = sb("logits", [P, 2, 3 * P])
        probs = sb("probs", [P, 2, 3 * P])
        probsT = sb("probsT", [P, 3 * P])
        oT = sb("oT", [P, T])
        mask = sb("mask", [P, 3 * P])
        ident = sb("ident_a", [P, P])
        ones = sb("ones", [1, P])
        bo = sb("bo", [1, D])
        xr = sb("xr", [P, TILES, D])
        waiter = sb("waiter", [P, 1])
        rmax = sb("rmax", [P, 2, TC])
        nmax = sb("nmax", [P, 2, TC])
        rsum = sb("rsum", [P, 2, TC])
        rinv = sb("rinv", [P, 2, TC])
        acc = [ctx.enter_context(nc.psum_tensor(f"acc{i}", [P, HALF], F32)) for i in range(B)]
        S = [ctx.enter_context(nc.psum_tensor(f"S{i}", [P, HALF], F32)) for i in range(2)]
        TB = ctx.enter_context(nc.psum_tensor("TB", [P, HALF], F32))
        OB = ctx.enter_context(nc.psum_tensor("OB", [P, HALF], F32))
        qbank = [S[0], S[1], TB, OB]

        const_in, x_in = sem("const_in"), sem("x_in")
        wq_in, wkv_in, wo_in = ([sem(f"{n}{par}") for par in range(2)]
                                for n in ("wq_in", "wkv_in", "wo_in"))
        ones_ready, q_psum, q_act, q_dve = (sem(n) for n in (
            "ones_ready", "q_psum", "q_act", "q_dve"))
        qh_ready, s_psum, k_psum, v_psum, t_psum, o_psum, op_done = (sem(n) for n in (
            "qh_ready", "s_psum", "k_psum", "v_psum", "t_psum", "o_psum", "op_done"))
        k_ready, v_ready, pT_ready, oT_ready = (sem(n) for n in (
            "k_ready", "v_ready", "pT_ready", "oT_ready"))
        max_ready, nmax_ready, exp_done, rinv_ready, p_ready, x1_ready = (sem(n) for n in (
            "max_ready", "nmax_ready", "exp_done", "rinv_ready", "p_ready", "x1_ready"))

        block = ctx.enter_context(nc.Block())

        def heads(eng, head):
            with eng.Fori(0, H1 // 2 - 1) as i:
                for hh in range(2):
                    head(i, i * 2 + hh, hh, False)
            head(H1 // 2 - 1, H1 - 2, 0, False)
            head(H1 // 2 - 1, H1 - 1, 1, True)

        @block.sync
        def _(sp):
            for dst, name in ((mask, "mask"), (ident, "ident"), (bo, "bo")):
                sp.dma_start(dst[:], dram[name]).then_inc(const_in, 16)
            sp.dma_start(wq[:, 0], dram["wq"][0]).then_inc(wq_in[0], 16)
            sp.dma_start(wq[:, 1], dram["wq"][1]).then_inc(wq_in[1], 16)
            sp.dma_start(wkv[:, 0], dram["wkv"][0]).then_inc(wkv_in[0], 16)
            sp.dma_start(wo[:, 0], dram["wo"][0]).then_inc(wo_in[0], 16)
            sp.dma_start(wkv[:, 1], dram["wkv"][1]).then_inc(wkv_in[1], 16)
            sp.dma_start(xr[:], dram["xr"]).then_inc(x_in, 16)
            with sp.Fori(0, H1 // 2 - 1) as i:
                for par in range(2):
                    c = i * 2 + par
                    sp.wait_ge(q_act, c + 3)
                    sp.wait_ge(q_dve, c + 3)
                    sp.dma_start(wq[:, par], dram["wq"][bass.ds(c + 2, 1)]
                                 .rearrange("o p n -> (o p) n")).then_inc(wq_in[par], 16)

            def loads(i, h, par, last):
                if last:
                    return
                sp.wait_ge(op_done, 4 * h + 1)
                sp.dma_start(wo[:, 1 - par], dram["wo"][bass.ds(h + 1, 1)]
                             .rearrange("o p n -> (o p) n")).then_inc(wo_in[1 - par], 16)
                if isinstance(h, int) and h + 2 >= H1:
                    return
                sp.wait_ge(k_ready, 4 * h + 4)
                sp.wait_ge(v_psum, 4 * h + 4)
                sp.dma_start(wkv[:, par], dram["wkv"][bass.ds(h + 2, 1)]
                             .rearrange("o p n -> (o p) n")).then_inc(wkv_in[par], 16)
            heads(sp, loads)

        @block.tensor
        def _(pe):
            with pe.Fori(0, H1 // 2) as i:
                for par in range(2):
                    c = i * 2 + par
                    pe.wait_ge(wq_in[par], 16 * i + 16)
                    pe.wait_ge(q_act, c + 1)
                    pe.wait_ge(q_dve, c + 1)
                    for half in range(2):
                        for j in range(J):
                            mm = pe.matmul(qbank[2 * par + half][:], wq[:, par, j * P:(j + 1) * P],
                                           gruT[:, j, 2 * half:2 * half + 2, :]
                                           .rearrange("p b t -> p (b t)"),
                                           start=(j == 0), stop=(j == J - 1))
                        mm.then_inc(q_psum, 1)

            def k_unit(par, b, bank):
                for j in range(J):
                    mm = pe.matmul(bank[:, 0:T], wkv[:, par, j * P:(j + 1) * P], gruT[:, j, b, :],
                                   start=(j == 0), stop=(j == J - 1))
                mm.then_inc(k_psum, 1)

            def v_unit(par, b, bank):
                for sc in range(TC):
                    for j in range(J):
                        mm = pe.matmul(bank[:, sc * DH1:(sc + 1) * DH1],
                                       gruT[:, j, b, sc * P:(sc + 1) * P],
                                       wkv[:, par, (J + j) * P:(J + j + 1) * P],
                                       start=(j == 0), stop=(j == J - 1))
                mm.then_inc(v_psum, 1)

            def score_unit(par, b, bank):
                for tc in range(TC):
                    mm = pe.matmul(bank[:, tc * P:(2 * tc + 1) * P],
                                   qh[:, par, b, tc * P:(tc + 1) * P],
                                   kh[:, par, b, 0:(tc + 1) * P], start=True, stop=True)
                mm.then_inc(s_psum, 1)

            pe.wait_ge(const_in, 48)
            pe.wait_ge(ones_ready, 1)
            for b in range(B):
                for tc in range(TC):
                    mm = pe.matmul(acc[b][:, tc * D:(tc + 1) * D], ones[:], bo[:], start=(tc == 0),
                                   stop=False, skip_group_check=True)
            mm.then_inc(op_done, 1)
            pe.wait_ge(wkv_in[0], 16)
            pe.wait_ge(q_act, H1 + 2)
            pe.wait_ge(q_dve, H1 + 2)
            for b in range(B):
                if b >= 1:
                    pe.wait_ge(k_ready, b)
                k_unit(0, b, OB)
                if b >= 1:
                    pe.wait_ge(v_ready, b)
                v_unit(0, b, TB)
            pe.wait_ge(k_ready, 4)
            pe.wait_ge(qh_ready, 1)
            score_unit(0, 0, S[0])

            def head(i, h, par, last):
                for b in range(B):
                    u = h * 4 + b
                    if not (last and b == B - 1):
                        if last:
                            pe.wait_ge(k_ready, units)
                            pe.wait_ge(exp_done, u)
                        else:
                            pe.wait_ge(k_ready, u + 4)
                        if b == B - 1:
                            pe.wait_ge(qh_ready, h + 2)
                        score_unit(par if b < B - 1 else 1 - par, (b + 1) % B, S[(b + 1) % 2])
                    pe.wait_ge(p_ready, u + 1)
                    pe.wait_ge(v_ready, units if last else u + 4)
                    for n in range(3):
                        mm = pe.transpose(TB[:, n * P:(n + 1) * P],
                                          probs[:, b % 2, n * P:(n + 1) * P], ident[:])
                    mm.then_inc(t_psum, 1)
                    if not last:
                        if b == 0:
                            pe.wait_ge(wkv_in[1 - par], 16 * (i + par) + 16)
                        k_unit(1 - par, b, S[b % 2])
                    pe.wait_ge(pT_ready, u + 1)
                    pe.matmul(OB[:, 0:P], vh[:, par, b, 0:DH1], probsT[:, 0:P],
                              start=True, stop=False, skip_group_check=True)
                    pe.matmul(OB[:, P:T], vh[:, par, b, 0:DH1], probsT[:, P:2 * P],
                              start=False, stop=False, skip_group_check=True)
                    pe.matmul(OB[:, P:T], vh[:, par, b, DH1:2 * DH1], probsT[:, 2 * P:3 * P],
                              start=False, stop=True, skip_group_check=True).then_inc(o_psum, 1)
                    if not last:
                        v_unit(1 - par, b, TB)
                    if b == 0:
                        pe.wait_ge(wo_in[par], 16 * i + 16)
                    pe.wait_ge(oT_ready, u + 1)
                    for tc in range(TC):
                        mm = pe.matmul(acc[b][:, tc * D:(tc + 1) * D], oT[:, tc * P:(tc + 1) * P],
                                       wo[:, par, 0:D], start=False, stop=False,
                                       skip_group_check=True)
                    mm.then_inc(op_done, 1)
            heads(pe, head)

        @block.scalar
        def _(act):
            with act.Fori(0, H1 // 2) as i:
                for par in range(2):
                    c = i * 2 + par
                    act.wait_ge(q_psum, 2 * c + 1)
                    nc.scalar.activation(QT[:, 0:2, :, bass.ds(c, 1)].rearrange("p b t o -> p b (t o)"),
                                         qbank[2 * par][:].rearrange("p (b t) -> p b t", b=2),
                                         ACT.Identity, bias=wq[:, par, J * P:J * P + 1]) \
                        .then_inc(q_act, 1)

            def key(par, b, bank, n):
                act.wait_ge(k_psum, n + 1)
                nc.scalar.activation(kh[:, par, b, :], bank[:, 0:T], ACT.Identity,
                                     bias=wkv[:, par, 2 * J * P:2 * J * P + 1]).then_inc(k_ready, 1)

            def exps(n, par):
                act.wait_ge(nmax_ready, n + 1)
                for tc in range(TC):
                    c = slice(tc * P, (2 * tc + 1) * P)
                    a = nc.scalar.activation(probs[:, par, c], logits[:, par, c], ACT.Exp,
                                             bias=nmax[:, par, tc:tc + 1],
                                             accum_out=rsum[:, par, tc:tc + 1])
                a.then_inc(exp_done, 1)

            for b in range(B):
                key(0, b, OB, b)
            exps(0, 0)

            def head(i, h, par, last):
                for b in range(B):
                    u = h * 4 + b
                    if not (last and b == B - 1):
                        if isinstance(h, int) or b > 0:
                            act.wait_ge(t_psum, u)
                        exps(u + 1, (b + 1) % 2)
                    if not last:
                        key(1 - par, b, S[b % 2], u + 4)
                    if b == 0:
                        act.wait_ge(wo_in[par], 16 * i + 16)
                    act.wait_ge(op_done, u + 1)
                    act.wait_ge(o_psum, u + 1)
                    nc.scalar.activation(oT[:], OB[:, 0:T], ACT.Identity,
                                         bias=wo[:, par, D:D + 1]).then_inc(oT_ready, 1)
            heads(act, head)

        @block.vector
        def _(dve):
            nc.vector.memset(ones[:], 1.0).then_inc(ones_ready, 1)
            nc.vector.memset(rmax[:], 0.0).then_inc(q_act, 2)
            nc.vector.memset(nmax[:], 0.0).then_inc(q_dve, 2)
            with dve.Fori(0, H1 // 2) as i:
                for par in range(2):
                    c = i * 2 + par
                    dve.wait_ge(q_psum, 2 * c + 2)
                    nc.vector.tensor_scalar(QT[:, 2:4, :, bass.ds(c, 1)].rearrange("p b t o -> p b (t o)"),
                                            qbank[2 * par + 1][:].rearrange("p (b t) -> p b t", b=2),
                                            wq[:, par, J * P:J * P + 1], None,
                                            ALU.add).then_inc(q_dve, 1)

            def value(par, b, n):
                dve.wait_ge(v_psum, n + 1)
                nc.vector.tensor_copy(vh[:, par, b, :], TB[:, 0:TC * DH1]).then_inc(v_ready, 1)

            def maxima(n, par, bank):
                dve.wait_ge(s_psum, n + 1)
                nc.vector.memset(waiter[:], 0.0)
                for tc in range(TC):
                    c = slice(tc * P, (2 * tc + 1) * P)
                    a = nc.vector.tensor_tensor_reduce(
                        out=logits[:, par, c], in0=bank[:, c], in1=mask[:, c], scale=scale,
                        scalar=-3.0e38, op0=ALU.add, op1=ALU.max, accum_out=rmax[:, par, tc:tc + 1])
                a.then_inc(max_ready, 1)
                dve.wait_ge(max_ready, n + 1)
                nc.vector.tensor_scalar(nmax[:, par, :], rmax[:, par, :], -1.0, None,
                                        ALU.mult).then_inc(nmax_ready, 1)

            def inverse(n, par):
                dve.wait_ge(exp_done, n + 1)
                nc.vector.reciprocal(rinv[:, par, :], rsum[:, par, :]).then_inc(rinv_ready, 1)

            for b in range(B):
                value(0, b, b)
            maxima(0, 0, S[0])
            inverse(0, 0)

            def head(i, h, par, last):
                for b in range(B):
                    u = h * 4 + b
                    nxt = (b + 1) % 2
                    if not (last and b == B - 1):
                        maxima(u + 1, nxt, S[nxt])
                    dve.wait_ge(t_psum, u + 1)
                    nc.vector.tensor_copy(probsT[:], TB[:, 0:3 * P]).then_inc(pT_ready, 1)
                    if not (last and b == B - 1):
                        inverse(u + 1, nxt)
                    if not last:
                        value(1 - par, b, u + 4)
            heads(dve, head)
            dve.wait_ge(x_in, 16)
            dve.wait_ge(op_done, units + 1)
            for b in range(B):
                nc.vector.tensor_tensor(x1[:, 2 * b:2 * b + 2, :].rearrange("p a d -> p (a d)"),
                                        acc[b][:], xr[:, 2 * b:2 * b + 2, :]
                                        .rearrange("p a d -> p (a d)"), ALU.add).then_inc(x1_ready, 1)

        @block.gpsimd
        def _(pool):
            pool.wait_ge(q_act, H1 + 2)
            pool.wait_ge(q_dve, H1 + 2)

            def query(h, par):
                if isinstance(h, int):
                    src = QT[:, :, 16 * h:16 * h + 16, :]
                else:
                    src = QT[:, :, bass.ds(h * 16, 16), :]
                nc.gpsimd.tensor_copy(qh[:, par], src.rearrange("p b r c -> p b (r c)")) \
                    .then_inc(qh_ready, 1)

            def weights(n, par):
                pool.wait_ge(rinv_ready, n + 1)
                for tc in range(TC):
                    c = slice(tc * P, (2 * tc + 1) * P)
                    a = nc.gpsimd.tensor_tensor(
                        probs[:, par, c], probs[:, par, c],
                        rinv[:, par, tc:tc + 1].to_broadcast([P, (tc + 1) * P]), ALU.mult)
                a.then_inc(p_ready, 1)
            query(0, 0)
            weights(0, 0)

            def head(i, h, par, last):
                for b in range(B):
                    u = h * 4 + b
                    if b == 0 and not last:
                        pool.wait_ge(s_psum, u + 1)
                        query(h + 1, 1 - par)
                    if not (last and b == B - 1):
                        weights(u + 1, (b + 1) % 2)
            heads(pool, head)


def adaln_block(nc, dram, x1, yT):
    eps, scale = 1e-6, float(DH2) ** -0.5
    PAIRS = TILES * H2 // 2
    LEAD, PPT = 3, H2 // 2
    with ExitStack() as ctx:
        def sb(name, shape, dt=F32):
            return ctx.enter_context(nc.sbuf_tensor(name, shape, dt))

        def sem(name):
            return ctx.enter_context(nc.semaphore(name))

        wemb = sb("wemb", [P, J, 2 * D])
        bemb = sb("bemb", [P, 4])
        gnorm = sb("gnorm", [P, J])
        condT = sb("condT2", [P, J, B])
        wqkv = sb("wqkv", [P, J, 3 * D])
        gqk = sb("gqk", [P, 2 * D])
        wout = sb("wout", [P, J, D])
        ident = sb("ident_c", [P, P])
        parity = sb("parity", [P, 2])
        emb = sb("emb", [P, 4, B])
        gain = sb("gain", [P, J, B])
        epst = sb("epst", [P, 1])
        ss = sb("ss", [P, TILES])
        rms = sb("rms", [P, TILES])
        rstd = sb("rstd", [P, TILES])
        junk = sb("junk", [P, D])
        xn = sb("xn", [P, TILES, D])
        xnT = sb("xnT", [P, J, NT])
        qk = sb("qk", [P, TILES, 2 * D])
        sq = sb("sq", [P, 2, 2 * D])
        ss2 = sb("ss2", [P, TILES, 32])
        rms2 = sb("rms2", [P, TILES, 32])
        rstd2 = sb("rstd2", [P, TILES, 32])
        v = sb("v", [P, TILES, H2 // 2, 2, 2, DH2])
        qT = sb("qT", [P, J, NT])
        kT = sb("kT", [P, J, B, 2, T])
        mx = sb("mx", [P, 4, 2])
        nmx = sb("nmx", [P, 4, 2])
        rsum = sb("rsum2", [P, TILES, H2])
        rinv = sb("rinv2", [P, TILES, H2])
        probs = sb("probs2", [P, 4, 2, T])
        pT = sb("pT", [P, 4, HALF])
        oT = sb("oT2", [P, J, NT])
        bk = [ctx.enter_context(nc.psum_tensor(f"cb{i}", [P, HALF], F32)) for i in range(8)]

        w_in, emb_psum, emb_act, gain_ready = (sem(n) for n in (
            "w_in", "emb_psum", "emb_act", "gain_ready"))
        ss_ready, rms_ready, rstd_ready, xn_ready = (sem(n) for n in (
            "ss_ready", "rms_ready", "rstd_ready", "xn_ready"))
        xt_psum, xt_done, qk_psum, qk_done, v_psum, v_done = (sem(n) for n in (
            "xt_psum", "xt_done", "qk_psum2", "qk_done", "v_psum2", "v_done"))
        sq_ready, ss2_ready, rms2_ready, rstd2_ready, qn_dve, qn_pool, qn_part = (sem(n) for n in (
            "sq_ready", "ss2_ready", "rms2_ready", "rstd2_ready", "qn_dve", "qn_pool", "qn_part"))
        t_psum, tq_done, tk_done = sem("t_psum2"), sem("tq_done"), sem("tk_done")
        sc_psum, mx_ready, nmx_ready, exp_done = (sem(n) for n in (
            "sc_psum", "mx_ready", "nmx_ready", "exp_done2"))
        tr_psum, pt_dve, pt_act, pv_done = (sem(n) for n in (
            "tr_psum", "pt_dve", "pt_act", "pv_done"))
        v_zero, rinv_ready, norm_done, ot_done, y_psum, y_done = (sem(n) for n in (
            "v_zero", "rinv_ready2", "norm_done", "ot_done2", "y_psum", "y_done"))
        block = ctx.enter_context(nc.Block())

        def tile_cols(i):
            return slice(i * P, (i + 1) * P)

        @block.sync
        def _(sp):
            for dst, name in ((wemb, "wemb"), (bemb, "bemb"), (gnorm, "gnorm"), (condT, "condT"),
                              (wqkv, "wqkv"), (gqk, "gqk"), (wout, "wout"), (ident, "ident"),
                              (parity, "parity")):
                sp.dma_start(dst[:], dram[name]).then_inc(w_in, 16)

        @block.tensor
        def _(pe):
            pe.wait_ge(w_in, 144)
            for m in range(4):
                for j in range(J):
                    mm = pe.matmul(bk[7][:, m * B:(m + 1) * B], wemb[:, j, m * P:(m + 1) * P],
                                   condT[:, j, :], start=(j == 0), stop=(j == J - 1))
            mm.then_inc(emb_psum, 1)
            for n in range(B * J):
                b, j = n // J, n % J
                if n >= 4:
                    pe.wait_ge(xt_done, n - 3)
                for tc in range(TC):
                    i = b * TC + tc
                    pe.wait_ge(xn_ready, i + 1)
                    mm = pe.transpose(bk[n % 4][:, tile_cols(tc)], xn[:, i, j * P:(j + 1) * P],
                                      ident[:])
                mm.then_inc(xt_psum, 1)
            pe.wait_ge(emb_act, 4)
            for i in range(TILES):
                pe.wait_ge(xt_done, J * (i // TC + 1))
                if i >= 2:
                    pe.wait_ge(qk_done, i - 1)
                    pe.wait_ge(v_done, i - 1)
                for j in range(J):
                    mm = pe.matmul(bk[4 + i % 2][:], xnT[:, j, tile_cols(i)], wqkv[:, j, 0:2 * D],
                                   start=(j == 0), stop=(j == J - 1))
                mm.then_inc(qk_psum, 1)
                for j in range(J):
                    mm = pe.matmul(bk[6 + i % 2][:, 0:D], xnT[:, j, tile_cols(i)],
                                   wqkv[:, j, 2 * D:3 * D], start=(j == 0), stop=(j == J - 1))
                mm.then_inc(v_psum, 1)
            for b in range(B):
                pe.wait_ge(qn_dve, b + 1)
                pe.wait_ge(qn_pool, b + 1)
                for n in range(2 * J):
                    which, j = n // J, n % J
                    if b >= 1:
                        pe.wait_ge((tq_done, tk_done)[which], J * (b - 1) + j + 1)
                    for tc in range(TC):
                        mm = pe.transpose(bk[n][:, tile_cols(tc)],
                                          qk[:, b * TC + tc, which * D + j * P:which * D + (j + 1) * P],
                                          ident[:])
                    mm.then_inc(t_psum, 1)
            pe.wait_ge(tq_done, J * B)
            pe.wait_ge(tk_done, J * B)

            def scores(n):
                i, j, p = n // PPT, n // 4 % J, n % 4
                rows = slice(32 * p, 32 * p + 32)
                if n >= 4:
                    pe.wait_ge(exp_done, n - 3)
                pe.matmul(bk[p][:], qT[rows, j, tile_cols(i)],
                          kT[rows, j, i // TC].rearrange("p e t -> p (e t)"), start=True,
                          stop=True, tile_position=(32 * p, 0)).then_inc(sc_psum, 1)

            def pv_pair(n):
                i, g, p = n // PPT, n // 4, n % 4
                pe.wait_ge((pt_dve, pt_act)[n % 2], n // 2 + 1)
                if p == 0 and g >= 2:
                    pe.wait_ge(ot_done, g - 1)
                for k in range(2 * TC):
                    e, sc = k // TC, k % TC
                    mm = pe.matmul(bk[6 + g % 2][32 * p:32 * p + 32, 0:P],
                                   v[:, (i // TC) * TC + sc, n % PPT, e].rearrange("p z d -> p (z d)"),
                                   pT[:, n % 4, k * P:(k + 1) * P], start=(k == 0),
                                   stop=(k == 2 * TC - 1), tile_position=(0, 32 * p))
                mm.then_inc(pv_done, 1)

            for n in range(LEAD):
                scores(n)
            pe.wait_ge(v_done, TILES)
            for n in range(PAIRS):
                if n + LEAD < PAIRS:
                    scores(n + LEAD)
                pe.wait_ge(norm_done, n + 1)
                if n >= 2:
                    pe.wait_ge((pt_dve, pt_act)[n % 2], n // 2)
                for k in range(2 * TC):
                    mm = pe.transpose(bk[4 + n % 2][:, k * P:(k + 1) * P],
                                      probs[:, n % 4, k // TC, k % TC * P:(k % TC + 1) * P], ident[:])
                mm.then_inc(tr_psum, 1)
                if n >= 2:
                    pv_pair(n - 2)
            pv_pair(PAIRS - 2)
            pv_pair(PAIRS - 1)
            for n in range(4):
                m, half = n % 2, n // 2
                pe.wait_ge(ot_done, PAIRS // 8 * (half + 1))
                for j in range(J):
                    mm = pe.matmul(bk[4 + n][:], wout[:, j, m * P:(m + 1) * P],
                                   oT[:, j, half * HALF:(half + 1) * HALF],
                                   start=(j == 0), stop=(j == J - 1))
                mm.then_inc(y_psum, 1)

        def transposed(eng, n):
            eng.wait_ge(tr_psum, n + 1)
            if n >= 4:
                eng.wait_ge(pv_done, n - 3)
            if n % 2:
                nc.scalar.activation(pT[:, n % 4, :], bk[4 + n % 2][:], ACT.Copy).then_inc(pt_act, 1)
            else:
                nc.vector.tensor_copy(pT[:, n % 4, :], bk[4 + n % 2][:]).then_inc(pt_dve, 1)

        @block.scalar
        def _(act):
            act.wait_ge(emb_psum, 1)
            for m in range(4):
                nc.scalar.activation(emb[:, m, :], bk[7][:, m * B:(m + 1) * B], ACT.Identity,
                                     bias=bemb[:, m:m + 1]).then_inc(emb_act, 1)
            act.wait_ge(ss_ready, TILES + 1)
            nc.scalar.activation(rms[:], ss[:], ACT.Sqrt, bias=epst[:],
                                 scale=1.0 / D).then_inc(rms_ready, 1)
            act.wait_ge(gain_ready, 2)
            for n in range(B * J):
                b, j = n // J, n % J
                act.wait_ge(xt_psum, n + 1)
                nc.scalar.activation(xnT[:, j, b * T:(b + 1) * T], bk[n % 4][:, 0:T], ACT.Identity,
                                     bias=emb[:, J + j, b:b + 1],
                                     scale=gain[:, j, b:b + 1]).then_inc(xt_done, 1)
            for i in range(TILES):
                act.wait_ge(qk_psum, i + 1)
                nc.scalar.activation(qk[:, i, :], bk[4 + i % 2][:], ACT.Copy).then_inc(qk_done, 1)
            act.wait_ge(ss2_ready, TILES)
            nc.scalar.activation(rms2[:].rearrange("p i h -> p (i h)"),
                                 ss2[:].rearrange("p i h -> p (i h)"), ACT.Sqrt, bias=epst[:],
                                 scale=1.0 / DH2).then_inc(rms2_ready, 1)
            for b in range(B):
                for j in range(J):
                    act.wait_ge(t_psum, 2 * J * b + j + 1)
                    nc.scalar.activation(qT[:, j, b * T:(b + 1) * T], bk[j][:, 0:T],
                                         ACT.Copy).then_inc(tq_done, 1)
            for n in range(PAIRS + LEAD):
                if n >= LEAD and (n - LEAD) % 2:
                    transposed(act, n - LEAD)
                if n >= PAIRS:
                    continue
                act.wait_ge(nmx_ready, n + 1)
                if n >= 4:
                    act.wait_ge(tr_psum, n - 3)
                for e in range(2):
                    h = n % PPT * 2 + e
                    a = nc.scalar.activation(probs[:, n % 4, e, :], bk[n % 4][:, e * T:(e + 1) * T],
                                             ACT.Exp, bias=nmx[:, n % 4, e:e + 1], scale=scale,
                                             accum_out=rsum[:, n // PPT, h:h + 1])
                a.then_inc(exp_done, 1)

        @block.vector
        def _(dve):
            nc.vector.memset(epst[:], eps).then_inc(ss_ready, 1)
            for i in range(TILES):
                nc.vector.tensor_tensor_reduce(out=junk[:], in0=x1[:, i, :], in1=x1[:, i, :],
                                               scale=1.0, scalar=0.0, op0=ALU.mult, op1=ALU.add,
                                               accum_out=ss[:, i:i + 1]).then_inc(ss_ready, 1)
                dve.wait_ge(ss_ready, i + 2)
            dve.wait_ge(emb_act, 4)
            nc.vector.tensor_scalar(gain[:].rearrange("p j b -> p (j b)"),
                                    emb[:, 0:J, :].rearrange("p j b -> p (j b)"), 1.0, None,
                                    ALU.add).then_inc(gain_ready, 1)
            dve.wait_ge(gain_ready, 1)
            for j in range(J):
                a = nc.vector.tensor_scalar(gain[:, j, :], gain[:, j, :], gnorm[:, j:j + 1], None,
                                            ALU.mult)
            a.then_inc(gain_ready, 1)
            dve.wait_ge(rms_ready, 1)
            nc.vector.reciprocal(rstd[:], rms[:]).then_inc(rstd_ready, 1)
            dve.wait_ge(rstd_ready, 1)
            for i in range(TILES):
                nc.vector.tensor_scalar(xn[:, i, :], x1[:, i, :], rstd[:, i:i + 1], None,
                                        ALU.mult).then_inc(xn_ready, 1)
            dve.wait_ge(v_zero, 1)
            for i in range(TILES):
                dve.wait_ge(v_psum, i + 1)
                for e in range(2):
                    a = nc.vector.tensor_copy(
                        v[:, i, :, e, e, :],
                        bk[6 + i % 2][:, 0:D].rearrange("p (n z d) -> p n z d", z=2, d=DH2)[:, :, e, :])
                a.then_inc(v_done, 1)
                dve.wait_ge(sq_ready, i + 1)
                nc.vector.tensor_reduce(ss2[:, i, :], sq[:, i % 2].rearrange("p (h d) -> p h d", d=DH2),
                                        AX.X, ALU.add).then_inc(ss2_ready, 1)
            dve.wait_ge(rms2_ready, 1)
            nc.vector.reciprocal(rstd2[:].rearrange("p i h -> p (i h)"),
                                 rms2[:].rearrange("p i h -> p (i h)")).then_inc(rstd2_ready, 1)
            dve.wait_ge(rstd2_ready, 1)
            for b in range(B):
                i = b * TC
                q3 = qk[:, i].rearrange("p (h d) -> p h d", d=DH2)
                nc.vector.tensor_tensor(q3, q3, rstd2[:, i, :].unsqueeze(2).to_broadcast([P, 32, DH2]),
                                        ALU.mult).then_inc(qn_part, 1)
                dve.wait_ge(qn_part, b + 1)
                nc.vector.tensor_tensor(qk[:, i], qk[:, i], gqk[:], ALU.mult).then_inc(qn_dve, 1)
                for j in range(J):
                    dve.wait_ge(t_psum, 2 * J * b + J + j + 1)
                    for e in range(2):
                        a = nc.vector.tensor_scalar(kT[:, j, b, e, :], bk[J + j][:, 0:T],
                                                    parity[:, e:e + 1], None, ALU.mult)
                    a.then_inc(tk_done, 1)

            def maxima(n):
                dve.wait_ge(sc_psum, n + 1)
                nc.vector.tensor_reduce(mx[:, n % 4, :], bk[n % 4][:].rearrange("p (e t) -> p e t", e=2),
                                        AX.X, ALU.max).then_inc(mx_ready, 1)
                dve.wait_ge(mx_ready, n + 1)
                nc.vector.tensor_scalar(nmx[:, n % 4, :], mx[:, n % 4, :], -scale, None,
                                        ALU.mult).then_inc(nmx_ready, 1)

            def out_rows(g):
                dve.wait_ge(pv_done, 4 * (g + 1))
                nc.vector.tensor_copy(oT[:, g % J, tile_cols(g // J)],
                                      bk[6 + g % 2][:, 0:P]).then_inc(ot_done, 1)

            def inverse(n):
                dve.wait_ge(exp_done, n + 1)
                heads = slice(n % PPT * 2, n % PPT * 2 + 2)
                nc.vector.reciprocal(rinv[:, n // PPT, heads],
                                     rsum[:, n // PPT, heads]).then_inc(rinv_ready, 1)

            for n in range(LEAD):
                maxima(n)
                if n:
                    inverse(n - 1)
            for n in range(PAIRS + 1):
                if n % 2 == 1:
                    transposed(dve, n - 1)
                if n + LEAD < PAIRS:
                    maxima(n + LEAD)
                if n + LEAD - 1 < PAIRS:
                    inverse(n + LEAD - 1)
                if n % 4 == 2 and n > 4:
                    out_rows(n // 4 - 1)
            out_rows(PAIRS // 4 - 1)
            for n in range(4):
                m, half = n % 2, n // 2
                dve.wait_ge(y_psum, n + 1)
                nc.vector.tensor_tensor(yT[:, m, half * HALF:(half + 1) * HALF], bk[4 + n][:],
                                        oT[:, m, half * HALF:(half + 1) * HALF],
                                        ALU.add).then_inc(y_done, 1)

        @block.gpsimd
        def _(pool):
            nc.gpsimd.memset(v[:], 0.0).then_inc(v_zero, 1)
            for i in range(TILES):
                pool.wait_ge(qk_done, i + 1)
                if i >= 2:
                    pool.wait_ge(ss2_ready, i - 1)
                nc.gpsimd.tensor_tensor(sq[:, i % 2], qk[:, i], qk[:, i], ALU.mult).then_inc(sq_ready, 1)
            pool.wait_ge(rstd2_ready, 1)
            for b in range(B):
                i = b * TC + 1
                q3 = qk[:, i].rearrange("p (h d) -> p h d", d=DH2)
                nc.gpsimd.tensor_tensor(q3, q3, rstd2[:, i, :].unsqueeze(2).to_broadcast([P, 32, DH2]),
                                        ALU.mult).then_inc(sq_ready, 1)
                pool.wait_ge(sq_ready, TILES + b + 1)
                nc.gpsimd.tensor_tensor(qk[:, i], qk[:, i], gqk[:], ALU.mult).then_inc(qn_pool, 1)
            for n in range(PAIRS):
                pool.wait_ge(rinv_ready, n + 1)
                heads = slice(n % PPT * 2, n % PPT * 2 + 2)
                nc.gpsimd.tensor_tensor(probs[:, n % 4], probs[:, n % 4],
                                        rinv[:, n // PPT, heads].unsqueeze(2).to_broadcast([P, 2, T]),
                                        ALU.mult).then_inc(norm_done, 1)


def ffn_block(nc, dram, x1, yT, out):
    R17 = E + 1
    PAD = 4
    LO = 32
    with ExitStack() as ctx:
        def sb(name, shape, dt=F32):
            return ctx.enter_context(nc.sbuf_tensor(name, shape, dt))

        def sem(name):
            return ctx.enter_context(nc.semaphore(name))

        gw = sb("gw", [P, J, R17])
        ident = sb("ident_d", [P, P])
        wf = sb("wf", [P, 2, 7 * P])
        w_hi = sb("w_hi", [P, 2, 6 * P], F32R)
        w_lo = sb("w_lo", [P, 2, 6 * P], F32R)
        select = sb("select", [2 * LO, 2, P], F32R)
        y_hi = sb("y_hi", [P, J, NT], F32R)
        y_lo = sb("y_lo", [P, J, NT], F32R)
        lg = sb("lg", [P, TILES, R17])
        mx = sb("mxr", [P, TILES])
        ex = sb("ex", [P, TILES, E])
        pr = sb("pr", [P, TILES, E + PAD])
        den = sb("den", [P, TILES])
        rden = sb("rden", [P, TILES])
        top = sb("top", [P, TILES, 8])
        rep = sb("rep", [P, TILES, E + PAD])
        cw = sb("cw", [P, TILES, R17])
        es = sb("es", [P, TILES])
        cw_hi = sb("cw_hi", [P, TILES, R17], F32R)
        cw_parts = sb("cw_parts", [P, TILES, 2 * LO])
        cwT = sb("cwT", [2 * LO, NT], F32R)
        act_g = sb("act_g", [P, 2, HALF])
        prod = sb("prod", [P, 2, HALF])
        hT = sb("hT", [P, 2, HALF])
        h_hi = sb("h_hi", [P, 2, HALF], F32R)
        h_lo = sb("h_lo", [P, 2, HALF], F32R)
        outT = sb("outT", [P, J, NT])
        waiter = sb("waiter_f", [1, 1])
        fin = sb("fin", [P, TILES, D])
        acc = [ctx.enter_context(nc.psum_tensor(f"fa{i}", [P, HALF], F32)) for i in range(4)]
        GB, UB, CB, XB = [ctx.enter_context(nc.psum_tensor(f"fb{i}", [P, HALF], F32))
                          for i in range(4)]
        w_in = sem("w_in3")
        wf_in = [sem(f"wf_in{par}") for par in range(2)]
        y_hi_ready, y_lo_ready = sem("y_hi_ready"), sem("y_lo_ready")
        lg_psum, chain, exps, cw_ready, ct_psum, ct_done, es_done = (sem(n) for n in (
            "lg_psum", "chain", "exps", "cw_ready", "ct_psum", "ct_done", "es_done"))
        gu_ready, zeros_ready, d_ready, d_done = (sem(n) for n in (
            "gu_ready", "zeros_ready", "d_ready", "d_done"))
        hi_written, d_hi_written = sem("hi_written"), sem("d_hi_written")
        g_psum, u_psum, c_psum = (sem(n) for n in ("g_psum", "u_psum", "c_psum"))
        g_act, prod_ready, h_made, hi_ready, lo_ready = (sem(n) for n in (
            "g_act", "prod_ready", "h_made", "hi_ready", "lo_ready"))
        out_read = [sem(f"out_read{hf}") for hf in range(2)]
        t_psum, fin_ready, stored = (sem(n) for n in (
            "t_psum3", "fin_ready", "stored"))
        block = ctx.enter_context(nc.Block())
        halves = [slice(0, HALF), slice(HALF, NT)]

        @block.sync
        def _(sp):
            sp.dma_start(gw[:], dram["gw"]).then_inc(w_in, 16)
            sp.dma_start(ident[:], dram["ident"]).then_inc(w_in, 16)
            sp.dma_start(wf[:, 0], dram["wf"][0]).then_inc(wf_in[0], 16)
            sp.dma_start(wf[:, 1], dram["wf"][1]).then_inc(wf_in[1], 16)
            with sp.Fori(0, NCH // 2 - 1) as i:
                for par in range(2):
                    sp.wait_ge(d_ready, i * 2 + par + 1)
                    sp.dma_start(wf[:, par], dram["wf"][bass.ds(i * 2 + 2 + par, 1)]
                                 .rearrange("o p n -> (o p) n")).then_inc(wf_in[par], 16)
            out_rows = out.rearrange("(i p) d -> p i d", p=P)
            for a in range(4):
                sp.wait_ge(fin_ready, a + 1)
                sp.dma_start(out_rows[:, 2 * a:2 * a + 2, :],
                             fin[:, 2 * a:2 * a + 2, :]).then_inc(stored, 16)
            sp.wait_ge(stored, 64)

        @block.tensor
        def _(pe):
            pe.wait_ge(w_in, 32)
            for i in range(TILES):
                for j in range(J):
                    mm = pe.matmul(XB[:, i * R17:(i + 1) * R17], yT[:, j, i * P:(i + 1) * P],
                                   gw[:, j, :], start=(j == 0), stop=(j == J - 1))
            mm.then_inc(lg_psum, 1)
            pe.wait_ge(cw_ready, 2)
            for i in range(TILES):
                mm = pe.matmul((GB, UB)[i // 4][0:2 * LO, (i % 4) * P:(i % 4 + 1) * P],
                               cw_parts[:, i, :], ident[:], start=True, stop=True)
            mm.then_inc(ct_psum, 1)
            pe.wait_ge(zeros_ready, 2)
            pe.wait_ge(lo_ready, 1)
            for a in range(4):
                mm = pe.matmul(acc[a][:], w_hi[:, 1, 4 * P:5 * P], h_hi[:, 1, :], start=True,
                               stop=False, skip_group_check=True)
            mm.then_inc(d_done, 1)
            pe.wait_ge(ct_done, 2)
            pe.wait_ge(y_lo_ready, 2)

            def product(dst, par, c0, hf, ready):
                n = 0
                for j in range(J):
                    cols = slice((c0 + j) * P, (c0 + j + 1) * P)
                    for w, y in ((w_hi, y_hi), (w_hi, y_lo), (w_lo, y_hi)):
                        mm = pe.matmul(dst[:], w[:, par, cols], y[:, j, halves[hf]],
                                       start=(n == 0), stop=(n == 3 * J - 1))
                        n += 1
                return mm.then_inc(ready, 1)

            def summed(par, hf):
                for m in range(J):
                    cols = slice((4 + m) * P, (5 + m) * P)
                    for w, h in ((w_hi, h_hi), (w_lo, h_hi), (w_hi, h_lo)):
                        mm = pe.matmul(acc[2 * m + hf][:], w[:, par, cols], h[:, hf, :],
                                       start=False, stop=False, skip_group_check=True)
                mm.then_inc(d_done, 1)

            with pe.Fori(0, NCH // 2) as i:
                for k in range(4):
                    par, hf, u = k // 2, k % 2, i * 4 + k
                    if hf == 0:
                        pe.wait_ge(gu_ready, i * 2 + par + 1)
                    pe.wait_ge(g_act, u + 1)
                    product(GB, par, 0, hf, g_psum)
                    pe.wait_ge(prod_ready, u + 1)
                    product(UB, par, J, hf, u_psum)
                    pe.wait_ge(h_made, u + 1)
                    pe.matmul(CB[:], select[:, par, :], cwT[:, halves[hf]],
                              start=True, stop=True).then_inc(c_psum, 1)
                    pe.wait_ge(lo_ready, u + 1)
                    if hf == 1:
                        pe.wait_ge(d_ready, i * 2 + par + 1)
                    summed((k - 1) % 4 // 2, (k - 1) % 2)
            pe.wait_ge(lo_ready, 2 * NCH + 1)
            summed(1, 1)
            for n in range(4):
                pe.wait_ge(out_read[n // 2], J)
                for k in range(4):
                    i, m = 2 * n + k // 2, k % 2
                    mm = pe.transpose((GB, UB, CB, XB)[n][:, k * P:(k + 1) * P],
                                      outT[:, m, i * P:(i + 1) * P], ident[:])
                mm.then_inc(t_psum, 1)

        @block.scalar
        def _(act):
            for hf in range(2):
                nc.scalar.activation(y_hi[:, :, halves[hf]], yT[:, :, halves[hf]],
                                     ACT.Copy).then_inc(y_hi_ready, 1)
            act.wait_ge(chain, 4)
            nc.scalar.activation(ex[:].rearrange("p i e -> p (i e)"),
                                 ex[:].rearrange("p i e -> p (i e)"), ACT.Exp).then_inc(exps, 1)
            nc.scalar.activation(es[:], lg[:, :, E], ACT.Exp, scale=-1.0).then_inc(es_done, 1)
            with act.Fori(0, NCH // 2) as i:
                for k in range(4):
                    u = i * 4 + k
                    act.wait_ge(g_psum, u + 1)
                    act.wait_ge(prod_ready, u + 1)
                    nc.scalar.activation(act_g[:, k % 2, :], GB[:], ACT.Silu).then_inc(g_act, 1)
                    act.wait_ge(h_made, u + 2)
                    act.wait_ge(d_done, u + 2)
                    nc.scalar.activation(h_hi[:, k % 2, :], hT[:, k % 2, :],
                                         ACT.Copy).then_inc(hi_ready, 1)
            act.wait_ge(d_done, 2 * NCH + 3)
            for m in range(J):
                nc.scalar.activation(outT[:, m, 0:HALF], acc[2 * m][:],
                                     ACT.Copy).then_inc(out_read[0], 1)

        @block.vector
        def _(dve):
            def link(a, n):
                a.then_inc(chain, 1)
                dve.wait_ge(chain, n)
            nc.vector.memset(hT[:], 0.0).then_inc(h_made, 1)
            dve.wait_ge(h_made, 1)
            nc.vector.tensor_copy(h_hi[:, 1, :], hT[:, 1, :]).then_inc(lo_ready, 1)
            nc.vector.tensor_copy(h_lo[:, 1, :], hT[:, 1, :]).then_inc(chain, 1)
            nc.vector.memset(cw_parts[:], 0.0).then_inc(g_act, 1)
            nc.vector.memset(prod[:], 0.0).then_inc(prod_ready, 1)
            nc.vector.memset(act_g[:], 0.0).then_inc(d_done, 1)
            dve.wait_ge(lg_psum, 1)
            link(nc.vector.tensor_copy(lg[:].rearrange("p i e -> p (i e)"),
                                       XB[:, 0:TILES * R17]), 2)
            link(nc.vector.tensor_reduce(mx[:], lg[:, :, 0:E], AX.X, ALU.max), 3)
            link(nc.vector.tensor_tensor(ex[:], lg[:, :, 0:E],
                                         mx[:].unsqueeze(2).to_broadcast([P, TILES, E]),
                                         ALU.subtract), 4)
            link(nc.vector.memset(pr[:], -1.0), 5)
            dve.wait_ge(exps, 1)
            link(nc.vector.tensor_reduce(den[:], ex[:], AX.X, ALU.add), 6)
            link(nc.vector.reciprocal(rden[:], den[:]), 7)
            link(nc.vector.tensor_tensor(pr[:, :, 0:E], ex[:],
                                         rden[:].unsqueeze(2).to_broadcast([P, TILES, E]),
                                         ALU.mult), 8)
            for i in range(TILES):
                a = nc.vector.max(top[:, i, :], pr[:, i, 0:E])
            link(a, 9)
            link(nc.vector.memset(top[:, :, TOPK:8], -1.0), 10)
            for i in range(TILES):
                a = nc.vector.match_replace(rep[:, i, :], top[:, i, :], pr[:, i, :], -2.0)
            link(a, 11)
            link(nc.vector.tensor_reduce(den[:], top[:, :, 0:TOPK], AX.X, ALU.add), 12)
            link(nc.vector.reciprocal(rden[:], den[:]), 13)
            link(nc.vector.scalar_tensor_tensor(out=cw[:, :, 0:E], in0=rep[:, :, 0:E], scalar=0.0,
                                                in1=pr[:, :, 0:E], op0=ALU.is_lt, op1=ALU.mult), 14)
            nc.vector.tensor_tensor(cw[:, :, 0:E], cw[:, :, 0:E],
                                    rden[:].unsqueeze(2).to_broadcast([P, TILES, E]),
                                    ALU.mult).then_inc(cw_ready, 1)
            dve.wait_ge(es_done, 1)
            link(nc.vector.tensor_scalar(es[:], es[:], 1.0, None, ALU.add), 15)
            link(nc.vector.reciprocal(cw[:, :, E], es[:]), 16)
            dve.wait_ge(cw_ready, 1)
            link(nc.vector.tensor_copy(cw_hi[:], cw[:]), 17)
            dve.wait_ge(g_act, 1)
            nc.vector.tensor_copy(cw_parts[:, :, 0:R17], cw_hi[:].bitcast(F32)).then_inc(chain, 1)
            nc.vector.tensor_tensor(cw_parts[:, :, LO:LO + R17], cw[:], cw_hi[:].bitcast(F32),
                                    ALU.subtract).then_inc(cw_ready, 1)
            for hf in range(2):
                dve.wait_ge(y_hi_ready, hf + 1)
                nc.vector.tensor_tensor(y_lo[:, :, halves[hf]], yT[:, :, halves[hf]],
                                        y_hi[:, :, halves[hf]].bitcast(F32),
                                        ALU.subtract).then_inc(y_lo_ready, 1)
            dve.wait_ge(ct_psum, 1)
            nc.vector.tensor_copy(cwT[:, 0:HALF], GB[0:2 * LO, :]).then_inc(ct_done, 1)
            nc.vector.tensor_copy(cwT[:, HALF:NT], UB[0:2 * LO, :]).then_inc(ct_done, 1)
            with dve.Fori(0, NCH // 2) as i:
                for k in range(4):
                    u = i * 4 + k
                    dve.wait_ge(g_act, u + 2)
                    dve.wait_ge(u_psum, u + 1)
                    nc.vector.tensor_tensor(prod[:, k % 2, :], UB[:], act_g[:, k % 2, :],
                                            ALU.mult).then_inc(prod_ready, 1)
                    dve.wait_ge(prod_ready, u + 2)
                    dve.wait_ge(c_psum, u + 1)
                    nc.vector.tensor_tensor(hT[:, k % 2, :], CB[:], prod[:, k % 2, :],
                                            ALU.mult).then_inc(h_made, 1)
                    dve.wait_ge(hi_ready, u + 1)
                    nc.vector.tensor_tensor(h_lo[:, k % 2, :], hT[:, k % 2, :],
                                            h_hi[:, k % 2, :].bitcast(F32),
                                            ALU.subtract).then_inc(lo_ready, 1)
            dve.wait_ge(d_done, 2 * NCH + 3)
            for m in range(J):
                nc.vector.tensor_copy(outT[:, m, HALF:NT], acc[2 * m + 1][:]).then_inc(out_read[1], 1)
            for n in range(4):
                dve.wait_ge(t_psum, n + 1)
                nc.vector.tensor_tensor(fin[:, 2 * n:2 * n + 2, :].rearrange("p i d -> p (i d)"),
                                        (GB, UB, CB, XB)[n][:],
                                        x1[:, 2 * n:2 * n + 2, :].rearrange("p i d -> p (i d)"),
                                        ALU.add).then_inc(fin_ready, 1)

        @block.gpsimd
        def _(pool):
            pool.wait_ge(h_made, 1)
            nc.gpsimd.tensor_copy(w_hi[:, 1, 4 * P:6 * P], hT[:, 1, 0:D]).then_inc(zeros_ready, 1)
            nc.gpsimd.tensor_copy(w_lo[:, 1, 4 * P:6 * P], hT[:, 1, 0:D]).then_inc(zeros_ready, 1)
            with pool.Fori(0, NCH // 2) as i:
                for par in range(2):
                    c = i * 2 + par
                    pool.wait_ge(wf_in[par], 16 * i + 16)
                    pool.wait_ge(d_done, c * 2 + 1)
                    nc.gpsimd.tensor_tensor(waiter[:], wf[0:1, par, 0:1], wf[0:1, par, 0:1], ALU.add)
                    for cols, written, ready in ((slice(0, 4 * P), hi_written, gu_ready),
                                                 (slice(4 * P, 6 * P), d_hi_written, d_ready)):
                        nc.gpsimd.tensor_copy(w_hi[:, par, cols], wf[:, par, cols]).then_inc(written, 1)
                        if ready is gu_ready:
                            nc.gpsimd.tensor_copy(select[:, par, :], wf[0:2 * LO, par, 6 * P:7 * P])
                        pool.wait_ge(written, c + 1)
                        nc.gpsimd.tensor_tensor(w_lo[:, par, cols], wf[:, par, cols],
                                                w_hi[:, par, cols].bitcast(F32),
                                                ALU.subtract).then_inc(ready, 1)


def program(nc, dram, out):
    with ExitStack() as ctx:
        def sb(name, shape):
            return ctx.enter_context(nc.sbuf_tensor(name, shape, F32))
        gruT = sb("gruT", [P, J, B, T])
        x1 = sb("x1", [P, TILES, D])
        yT = sb("yT", [P, J, NT])
        gru_block(nc, dram, gruT)
        attention_block(nc, dram, gruT, x1)
        adaln_block(nc, dram, x1, yT)
        ffn_block(nc, dram, x1, yT, out)


def laid_out(x, cond_2048, L0_cond_W_ih, L0_cond_W_hh, L0_cond_b_ih, L0_cond_b_hh, **w):
    def rows_in(a):
        return np.ascontiguousarray(a.reshape(J, P, -1).transpose(1, 0, 2))

    def cols(a):
        return np.ascontiguousarray(a.reshape(-1, P).T)

    def heads_of(w):
        return w.reshape(J, P, H1, DH1).transpose(2, 1, 0, 3).reshape(H1, P, J * DH1)

    tri = np.where(np.tri(P, dtype=bool), 0.0, -1e30).astype(np.float32)
    d = {
        "wq": np.concatenate([heads_of(w["L0_attn_Wq"]), w["L0_attn_bq"].reshape(H1, P, 1)], 2),
        "wkv": np.concatenate([heads_of(w["L0_attn_Wk"]), heads_of(w["L0_attn_Wv"]),
                               w["L0_attn_bk"].reshape(H1, P, 1)], 2),
        "wo": np.concatenate([w["L0_attn_Wo"].reshape(H1, P, D),
                              w["L0_attn_bv"].reshape(H1, P, 1)], 2),
        "bo": w["L0_attn_bo"].reshape(1, D),
        "mask": np.concatenate([tri, np.zeros((P, P), np.float32), tri], 1),
        "xr": np.ascontiguousarray(x.reshape(TILES, P, D).transpose(1, 0, 2)),
        "xT": rows_in(x.reshape(NT, D).T),
        "wih": rows_in(L0_cond_W_ih), "whh": rows_in(L0_cond_W_hh),
        "bias_ih": cols(L0_cond_b_ih), "bias_hh": cols(L0_cond_b_hh),
        "condT": rows_in(cond_2048.T), "ident": np.eye(P, dtype=np.float32),
    }
    def hidden(gu, shared):
        a = np.concatenate([gu.reshape(E * INTER, D), shared])
        return np.concatenate([a, np.zeros((NCH * P - HID, D), a.dtype)])

    def in_chunks(a):
        return a.reshape(NCH, P, J, P).transpose(0, 3, 2, 1).reshape(NCH, P, J * P)

    gu, sgu = w["L0_ffn_expert_gate_up"], w["L0_ffn_shared_gate_up"]
    down = hidden(w["L0_ffn_expert_down"].transpose(0, 2, 1), w["L0_ffn_shared_down"].T)
    owner = np.minimum(np.arange(NCH * P) // INTER, E)
    owner[HID:] = -1
    rows = np.where(np.arange(P) < 64, np.arange(P) % 32, P)
    select = (owner[None, :] == rows[:, None]).astype(np.float32)
    d.update({
        "wemb": rows_in(w["L0_cond2_W_emb"]), "bemb": cols(w["L0_cond2_b_emb"]),
        "gnorm": cols(w["L0_cond2_g_norm"]), "wqkv": rows_in(w["L0_cond2_W_qkv"]),
        "gqk": np.broadcast_to(np.concatenate([np.tile(w["L0_cond2_g_q"], H2),
                                               np.tile(w["L0_cond2_g_k"], H2)]), (P, 2 * D)),
        "wout": rows_in(w["L0_cond2_W_out"]),
        "parity": (np.arange(P)[:, None] // DH2 % 2 == np.arange(2)).astype(np.float32),
        "gw": rows_in(np.concatenate([w["L0_ffn_gate_w"], w["L0_ffn_shared_gate_vec"]]).T),
        "wf": np.concatenate([in_chunks(hidden(gu[:, :INTER], sgu[:SHARED])),
                              in_chunks(hidden(gu[:, INTER:], sgu[SHARED:])),
                              down.reshape(NCH, P, D),
                              select.reshape(P, NCH, P).transpose(1, 0, 2)], 2),
    })
    return {k: np.ascontiguousarray(a) for k, a in d.items()}


def kernel(**inputs):
    import concourse.bacc as bacc
    from concourse.bass_utils import run_bass_kernel_spmd

    arrays = laid_out(**{k: np.asarray(v) for k, v in inputs.items()})
    nc = bacc.Bacc("TRN2", target_bir_lowering=False, num_devices=1)
    dram = {n: nc.dram_tensor(f"in_{n}", a.shape, F32, kind="ExternalInput").ap()
            for n, a in arrays.items()}
    out = nc.dram_tensor("out", [NT, D], F32, kind="ExternalOutput").ap()
    program(nc, dram, out)
    result = run_bass_kernel_spmd(nc, [{f"in_{n}": a for n, a in arrays.items()}], core_ids=[0])
    return result.results[0]["out"].reshape(B, T, D)
```

```python
from contextlib import ExitStack

import numpy as np

import concourse.bass as bass
from concourse import mybir

P = 128
F32 = mybir.dt.float32
F32R = mybir.dt.float32r
BF16 = mybir.dt.bfloat16
ACT = mybir.ActivationFunctionType
ALU = mybir.AluOpType
AX = mybir.AxisListType

B, T, D = 4, 256, 256
J = D // P
NT = B * T
TILES = NT // P
HALF = 512
H2, DH2 = 16, 16
TC = T // P
E, TOPK, INTER, SHARED = 16, 4, 176, 704
HID = E * INTER + SHARED
NCH = -(-HID // P)
H1, DH1 = 16, 128
QB = T // H1
LEADING = 2 * QB
BLOCKS = 1
U = BLOCKS * QB


class Count:

    def __init__(self, sem):
        self.sem, self.n = sem, 0

    def inc(self, instruction, by=1):
        instruction.then_inc(self.sem, by)
        self.n += by
        return self.n


def cut(place, shapes):
    views, start = [], 0
    for shape in shapes:
        n = int(np.prod(shape[1:]))
        view = place[:, start:start + n]
        views.append(view.rearrange("p (a n) -> p a n", a=shape[1]) if len(shape) == 3 else view)
        start += n
    return views


def ahead(nc, stack, tag, shapes, sems, place=None):
    tensors = cut(place, shapes.values()) if place is not None else [
        stack.enter_context(nc.sbuf_tensor(f"{n}_{tag}", s, F32)) for n, s in shapes.items()]
    held = dict(zip(shapes, tensors))
    for name in sems:
        held[name] = stack.enter_context(nc.semaphore(f"{name}_{tag}"))
    return held


def gru_block(nc, dram, wq, gruT, QT, load_ahead):
    with ExitStack() as ctx:
        def sb(name, shape, dt=F32):
            return ctx.enter_context(nc.sbuf_tensor(name, shape, dt))

        def sem(name):
            return ctx.enter_context(nc.semaphore(name))

        xT, wih, whh, *whh_rest = cut(QT[:].rearrange("p h b t c -> p (h b t c)"),
                                      [[P, J, NT]] + 4 * [[P, J, 3 * D]])
        whh_part = sb("whh_part", [P, 3, J, 3 * D], BF16)
        bias_ih = sb("bias_ih", [P, 6])
        bias_hh = sb("bias_hh", [P, 6])
        bias_g = sb("bias_g", [P, 4])
        ident = sb("ident_f", [P, P])
        identb = sb("ident_b", [P, P], BF16)
        condT = sb("condT", [P, J, B])
        gates = [sb(f"gates{q}", [P, T, 24]) for q in range(3)]
        bhn = sb("bhn", [P, 3, 8])
        hs = sb("hs", [P, 2, 3, 16])
        r_scan = sb("r_scan", [P, 32])
        t_scan = sb("t_scan", [P, 32])
        u_scan = sb("u_scan", [P, 16])
        nv_scan = sb("nv_scan", [P, 16])
        r_sum = sb("r_sum", [P, 8])
        z_sum = sb("z_sum", [P, 8])
        z_gate = sb("z_gate", [P, 8])
        bank = [ctx.enter_context(nc.psum_tensor(f"gb{i}", [P, HALF], F32)) for i in range(7)]
        R, Z, N = bank[4:7]

        loaded = {n: sem(f"ld_{n}") for n in ("x0", "x1", "wih", "whh", "small", "wq")}
        gi_psum, gi_sbuf, bias_ready = sem("gi_psum"), sem("gi_sbuf"), sem("bias_ready")
        whh_split, whh_ready = sem("whh_split"), sem("whh_ready")
        gates_split, split_dve = sem("gates_split"), sem("split_dve")
        r_psum, z_psum, scan_in = sem("r_psum"), sem("z_psum"), sem("scan_in")
        r_sum_ready, z_sum_ready, z_ready = sem("r_sum_ready"), sem("z_sum_ready"), sem("z_ready")
        npre_ready, hin_ready = sem("npre_ready"), sem("hin_ready")
        q_psum, q_read = sem("q_psum"), sem("q_read")
        h_new, h_rest, h_ready, h_stored = sem("h_new"), sem("h_rest"), sem("h_ready"), sem("h_stored")

        def high(ap):
            return ap.bitcast(BF16)[:, 1::2]

        def part(par, q):
            return hs[:, par, q, 1::2]

        def part_high(par, q):
            return hs[:, par, q, :].bitcast(BF16)[:, 3::4]


        block = ctx.enter_context(nc.Block())

        @block.sync
        def _(sp):
            sp.dma_start(xT[:, :, 0:HALF], dram["xT"][:, :, 0:HALF]).then_inc(loaded["x0"], 16)
            sp.dma_start(wih, dram["wih"]).then_inc(loaded["wih"], 16)
            sp.dma_start(xT[:, :, HALF:NT], dram["xT"][:, :, HALF:NT]).then_inc(loaded["x1"], 16)
            sp.dma_start(whh, dram["whh"]).then_inc(loaded["whh"], 16)
            for dst, name in ((bias_ih, "bias_ih"), (bias_hh, "bias_hh"), (condT, "condT"),
                              (ident, "ident")):
                sp.dma_start(dst[:], dram[name]).then_inc(loaded["small"], 16)
            sp.dma_start(wq, dram["wq"]).then_inc(loaded["wq"], 16)
            load_ahead(sp)

        @block.tensor
        def _(pe):
            pe.wait_ge(loaded["x0"], 16)
            pe.wait_ge(loaded["wih"], 16)
            for n in range(12):
                m, half = n % 6, n // 6
                if n == 6:
                    pe.wait_ge(loaded["x1"], 16)
                if n >= 4:
                    pe.wait_ge(gi_sbuf, n - 3)
                for j in range(J):
                    mm = pe.matmul(bank[n % 4][:], wih[:, j, m * P:(m + 1) * P],
                                   xT[:, j, half * HALF:(half + 1) * HALF],
                                   start=(j == 0), stop=(j == J - 1))
                mm.then_inc(gi_psum, 1)
            pe.wait_ge(split_dve, 1)
            pe.wait_ge(whh_ready, 3)
            pe.wait_ge(h_stored, 1)
            pe.wait_ge(loaded["wq"], 16)

            def queries(place, c, n):
                pe.wait_ge(q_read, n + 1)
                for j in range(J):
                    src = gruT[:, j, :, bass.ds(place * QB, QB)]
                    mm = pe.matmul(bank[(c + 1) % 2][:, 0:B * QB].rearrange("p (b t) -> p b t", b=B),
                                   wq[:, c, j * P:(j + 1) * P], src,
                                   start=(j == 0), stop=(j == J - 1))
                mm.then_inc(q_psum, 1)

            with pe.Fori(0, T // U) as i:
                for k in range(U):
                    t, cur = i * U + k, k % 2
                    if k % QB == 1:
                        pe.wait_ge(h_stored, t)
                    blk = i * BLOCKS + k // QB
                    queries(blk + (k % QB > 0), (k - 1) % H1, blk * H1 + k % QB)
                    pe.wait_ge(z_sum_ready, t + 1)
                    for q in range(3):
                        for dst, c0 in ((R, 0), (Z, 8)):
                            g = gates[q][:, bass.ds(t, 1), c0:c0 + 8].rearrange("p a b -> p (a b)")
                            pe.matmul(dst[:, 0:24:3], identb[:], high(g), start=(q == 0),
                                      stop=False, skip_group_check=True)
                    pe.wait_ge(npre_ready, t + 1)
                    for q in range(3):
                        g = gates[q][:, bass.ds(t, 1), 16:24].rearrange("p a b -> p (a b)")
                        pe.matmul(N[:, 3:32:4], identb[:], high(g), start=(q == 0), stop=False,
                                  skip_group_check=True)
                        pe.matmul(N[:, 0:32:4], identb[:], high(bhn[:, q, :]), start=False,
                                  stop=False, skip_group_check=True)
                    pe.wait_ge(h_ready, t + 1)
                    for dst, width, m0, done in ((R, 3, 0, r_psum), (Z, 3, 2, z_psum),
                                                 (N, 4, 4, scan_in)):
                        for mi in range(J):
                            out = dst[:, mi * B * width:(mi + 1) * B * width] \
                                .rearrange("p (b q) -> p b q", q=width)[:, :, 0:3]
                            for q in range(3):
                                for j in range(J):
                                    w = whh_part[:, q, j, (m0 + mi) * P:(m0 + mi + 1) * P]
                                    h = hs[:, cur, :, 8 * j:8 * j + 8].bitcast(BF16)[:, :, 3::4] \
                                        .rearrange("p q b -> p b q")
                                    mm = pe.matmul(out, w, h, start=False, stop=False,
                                                   skip_group_check=True)
                        mm.then_inc(done, 1)

        @block.scalar
        def _(act):
            act.wait_ge(bias_ready, 1)
            for n in range(12):
                m, half = n % 6, n // 6
                gate, mi = m // 2, m % 2
                act.wait_ge(gi_psum, n + 1)
                c0 = gate * 8 + mi * B + half * 2
                out = gates[0][:, :, c0:c0 + 2].rearrange("p t b -> p b t")
                bias = bias_g[:, m:m + 1] if gate < 2 else bias_ih[:, m:m + 1]
                nc.scalar.activation(out, bank[n % 4][:].rearrange("p (b t) -> p b t", b=2),
                                     ACT.Identity, bias=bias).then_inc(gi_sbuf, 1)

            def query(place, c, n):
                act.wait_ge(q_psum, n + 1)
                dst = QT[:, bass.ds(place, 1)].rearrange("p o b t c -> p (o b) t c")
                nc.scalar.activation(dst[:, :, :, c],
                                     bank[(c + 1) % 2][:, 0:B * QB].rearrange("p (b t) -> p b t", b=B),
                                     ACT.Identity, bias=wq[:, c, J * P:J * P + 1]) \
                                         .then_inc(q_read, 1)

            with act.Fori(0, T // U) as i:
                for k in range(U):
                    t = i * U + k
                    act.wait_ge(r_sum_ready, t + 1)
                    nc.scalar.activation(r_scan[:, 3::4], r_sum[:], ACT.Sigmoid) \
                        .then_inc(scan_in, 1)
                    act.wait_ge(z_sum_ready, t + 2)
                    nc.scalar.activation(z_gate[:], z_sum[:], ACT.Sigmoid).then_inc(z_ready, 1)
                    nc.scalar.activation(u_scan[:, 1::2], z_sum[:], ACT.Sigmoid, scale=-1.0)
                    act.wait_ge(npre_ready, t + 2)
                    nc.scalar.activation(nv_scan[:, 0::2], t_scan[:, 3::4],
                                         ACT.Tanh).then_inc(hin_ready, 1)
                    blk = i * BLOCKS + k // QB
                    query(blk + (k % QB > 0), (k - 1) % H1, blk * H1 + k % QB)
        @block.vector
        def _(dve):
            dve.wait_ge(loaded["small"], 64)
            nc.vector.tensor_tensor(bias_g[:], bias_ih[:, 0:4], bias_hh[:, 0:4],
                                    ALU.add).then_inc(bias_ready, 1)
            nc.vector.memset(r_scan[:], 0.0).then_inc(bias_ready, 1)
            nc.vector.memset(u_scan[:], 0.0).then_inc(bias_ready, 1)
            nc.vector.memset(hs[:], 0.0).then_inc(bias_ready, 1)
            dve.wait_ge(bias_ready, 4)
            nc.vector.memset(r_scan[:, 1::4], 1.0).then_inc(bias_ready, 1)
            nc.vector.memset(r_scan[:, 2::4], 1.0).then_inc(bias_ready, 1)
            nc.vector.tensor_copy(identb[:], ident[:]).then_inc(bias_ready, 1)
            nc.vector.memset(bhn[:], 0.0).then_inc(bias_ready, 1)
            dve.wait_ge(bias_ready, 8)
            for mi in range(J):
                nc.vector.tensor_scalar(bhn[:, 0, mi * B:(mi + 1) * B], bhn[:, 0, mi * B:(mi + 1) * B],
                                        bias_hh[:, 4 + mi:5 + mi], None,
                                        ALU.add).then_inc(bias_ready, 1)
            nc.vector.tensor_copy(part(0, 0), condT[:].rearrange("p j b -> p (j b)")) \
                .then_inc(bias_ready, 1)
            dve.wait_ge(bias_ready, 11)
            dve.wait_ge(loaded["whh"], 16)
            src = whh.rearrange("p j n -> p (j n)")
            for q in range(2):
                rest = whh_rest[q].rearrange("p j n -> p (j n)")
                nc.vector.tensor_tensor(rest, src, high(src), ALU.subtract).then_inc(whh_split, 1)
                dve.wait_ge(whh_split, q + 1)
                nc.vector.tensor_tensor(bhn[:, q + 1, :], bhn[:, q, :], high(bhn[:, q, :]),
                                        ALU.subtract).then_inc(bias_ready, 1)
                nc.vector.tensor_tensor(part(0, q + 1), part(0, q), part_high(0, q),
                                        ALU.subtract).then_inc(bias_ready, 1)
                dve.wait_ge(bias_ready, 13 + 2 * q)
                src = rest
            for n in range(12):
                dve.wait_ge(gi_sbuf, n + 1)
                m, half = n % 6, n // 6
                c0 = m // 2 * 8 + m % 2 * B + half * 2
                for q in range(2):
                    a = gates[q][:, :, c0:c0 + 2]
                    nc.vector.tensor_tensor(gates[q + 1][:, :, c0:c0 + 2], a,
                                            a.bitcast(BF16)[:, :, 1::2],
                                            ALU.subtract).then_inc(gates_split, 1)
                    dve.wait_ge(gates_split, 2 * n + q + 1)
            nc.vector.memset(bias_g[:], 0.0).then_inc(q_read, 2)
            nc.vector.memset(t_scan[:], 0.0).then_inc(npre_ready, 1)
            nc.vector.memset(r_sum[:], 0.0).then_inc(z_sum_ready, 1)
            nc.vector.memset(z_sum[:], 0.0).then_inc(h_ready, 1)
            nc.vector.memset(nv_scan[:], 0.0).then_inc(split_dve, 1)
            with dve.Fori(0, T // U) as i:
                for k in range(U):
                    t, cur = i * U + k, k % 2
                    nxt = 1 - cur
                    dve.wait_ge(r_psum, t + 1)
                    nc.vector.tensor_reduce(r_sum[:], R[:, 0:24].rearrange("p (m q) -> p m q", q=3),
                                            AX.X, ALU.add).then_inc(r_sum_ready, 1)
                    dve.wait_ge(z_psum, t + 1)
                    nc.vector.tensor_reduce(z_sum[:], Z[:, 0:24].rearrange("p (m q) -> p m q", q=3),
                                            AX.X, ALU.add).then_inc(z_sum_ready, 1)
                    dve.wait_ge(scan_in, 2 * t + 2)
                    nc.vector.tensor_tensor_scan(t_scan[:], r_scan[:], N[:, 0:32], 0.0, ALU.mult,
                                                 ALU.add).then_inc(npre_ready, 1)
                    dve.wait_ge(z_ready, t + 1)
                    nc.vector.tensor_tensor(nv_scan[:, 1::2], z_gate[:], part(cur, 0),
                                            ALU.mult).then_inc(hin_ready, 1)
                    dve.wait_ge(h_stored, t + 1)
                    dve.wait_ge(hin_ready, 2 * t + 2)
                    nc.vector.tensor_tensor_scan(hs[:, nxt, 0, :], u_scan[:], nv_scan[:], 0.0,
                                                 ALU.mult, ALU.add).then_inc(h_new, 1)
                    dve.wait_ge(h_new, t + 1)
                    nc.vector.tensor_tensor(part(nxt, 1), part(nxt, 0), part_high(nxt, 0),
                                            ALU.subtract).then_inc(h_rest, 1)
                    dve.wait_ge(h_rest, t + 1)
                    nc.vector.tensor_tensor(part(nxt, 2), part(nxt, 1), part_high(nxt, 1),
                                            ALU.subtract).then_inc(h_ready, 1)

        @block.gpsimd
        def _(pool):
            nc.gpsimd.memset(gruT[:, :, :, 0:LEADING], 0.0).then_inc(h_stored, 1)
            pool.wait_ge(loaded["whh"], 16)
            for q, src in enumerate((whh, *whh_rest)):
                if q:
                    pool.wait_ge(whh_split, q)
                nc.gpsimd.tensor_copy(whh_part[:, q].rearrange("p j n -> p (j n)"),
                                      high(src.rearrange("p j n -> p (j n)"))) \
                                          .then_inc(whh_ready, 1)
            with pool.Fori(0, T // U) as i:
                for k in range(U):
                    t, nxt = i * U + k, 1 - k % 2
                    pool.wait_ge(h_new, t + 1)
                    nc.gpsimd.tensor_copy(
                        gruT[:, :, :, bass.ds(t + LEADING, 1)].rearrange("p j b o -> p (j b o)"),
                        part(nxt, 0)).then_inc(h_stored, 1)


def attention_buffers(nc, stack):
    return ahead(nc, stack, "attn", {
        "mask": [P, 3 * P], "ident": [P, P], "bo": [1, D], "wkv": [P, 2, 2 * J * P + 1],
        "wo": [P, 2, D + 1]},
        ("const_in", "x_in", "wkv_in0", "wkv_in1", "wo_in0", "wo_in1"))


def attention_loads(sp, dram, a, x1):
    for dst, name in ((a["mask"], "mask"), (a["ident"], "ident"), (a["bo"], "bo")):
        sp.dma_start(dst[:], dram[name]).then_inc(a["const_in"], 16)
    sp.dma_start(a["wkv"][:, 0], dram["wkv"][0]).then_inc(a["wkv_in0"], 16)
    sp.dma_start(a["wo"][:, 0], dram["wo"][0]).then_inc(a["wo_in0"], 16)
    sp.dma_start(a["wkv"][:, 1], dram["wkv"][1]).then_inc(a["wkv_in1"], 16)
    sp.dma_start(x1[:], dram["xr"]).then_inc(a["x_in"], 16)


def attention_block(nc, dram, held, wq, gruT, QT, x1, load_ahead):
    scale = float(DH1) ** -0.5
    units = H1 * B
    with ExitStack() as ctx:
        def sb(name, shape, dt=F32):
            return ctx.enter_context(nc.sbuf_tensor(name, shape, dt))

        def sem(name):
            return ctx.enter_context(nc.semaphore(name))

        mask, ident, bo, wkv, wo = held["mask"], held["ident"], held["bo"], held["wkv"], held["wo"]
        qh = sb("qh", [P, 2, B, T])
        kh = sb("kh", [P, 2, B, T])
        vh = sb("vh", [P, 2, B, TC * DH1])
        logits = sb("logits", [P, 2, 3 * P])
        probs = sb("probs", [P, 2, 3 * P])
        probsT = sb("probsT", [P, 3 * P])
        g_hi = sb("g_hi", [P, J, B, T], F32R)
        g_lo = sb("g_lo", [P, J, B, T], F32R)
        wk_hi = sb("wk_hi", [P, 2, J * P], F32R)
        wk_lo = sb("wk_lo", [P, 2, J * P], F32R)
        wo_hi = sb("wo_hi", [P, 2, D], F32R)
        wo_lo = sb("wo_lo", [P, 2, D], F32R)
        oT_hi = sb("oT_hi", [P, T], F32R)
        oT_lo = sb("oT_lo", [P, T], F32R)
        zeros = sb("zeros", [P, D])
        waiter_p = sb("waiter_p", [1, 1])
        ones = sb("ones", [1, P])
        waiter = sb("waiter", [P, 1])
        waiter_o = sb("waiter_o", [P, 1])
        rmax = sb("rmax", [P, 2, TC])
        nmax = sb("nmax", [P, 2, TC])
        rsum = sb("rsum", [P, 2, TC])
        rinv = sb("rinv", [P, 2, TC])
        acc = [ctx.enter_context(nc.psum_tensor(f"acc{i}", [P, HALF], F32)) for i in range(B)]
        S = [ctx.enter_context(nc.psum_tensor(f"S{i}", [P, HALF], F32)) for i in range(2)]
        TB = ctx.enter_context(nc.psum_tensor("TB", [P, HALF], F32))
        OB = ctx.enter_context(nc.psum_tensor("OB", [P, HALF], F32))

        const_in, x_in = held["const_in"], held["x_in"]
        wkv_in, wo_in = (held["wkv_in0"], held["wkv_in1"]), (held["wo_in0"], held["wo_in1"])
        q_psum, q_read = sem("q_psum_a"), sem("q_read_a")
        ones_ready, zeros_ready, g_hi_ready, g_lo_ready = (sem(n) for n in (
            "ones_ready", "zeros_ready_a", "g_hi_ready", "g_lo_ready"))
        wk_hi_written, wk_split, wo_hi_written, wo_split = (sem(n) for n in (
            "wk_hi_written", "wk_split", "wo_hi_written", "wo_split"))
        qh_ready, s_psum, k_psum, v_psum, t_psum, o_psum, op_done = (sem(n) for n in (
            "qh_ready", "s_psum", "k_psum", "v_psum", "t_psum", "o_psum", "op_done"))
        k_ready, v_ready, pT_ready, oT_hi_ready, oT_ready = (sem(n) for n in (
            "k_ready", "v_ready", "pT_ready", "oT_hi_ready", "oT_ready"))
        max_ready, nmax_ready, exp_done, rinv_ready, p_ready, x1_ready = (sem(n) for n in (
            "max_ready", "nmax_ready", "exp_done", "rinv_ready", "p_ready", "x1_ready"))

        left_after = [range(b * (H1 + 1) // B, (b + 1) * (H1 + 1) // B) for b in range(B)]

        block = ctx.enter_context(nc.Block())

        def heads(eng, head):
            with eng.Fori(0, H1 // 2 - 1) as i:
                for hh in range(2):
                    head(i, i * 2 + hh, hh, False)
            head(H1 // 2 - 1, H1 - 2, 0, False)
            head(H1 // 2 - 1, H1 - 1, 1, True)

        @block.sync
        def _(sp):
            sp.wait_ge(q_read, H1 + 1)
            load_ahead(sp)

            def loads(i, h, par, last):
                if last:
                    return
                sp.wait_ge(op_done, 4 * h + 2)
                sp.dma_start(wo[:, 1 - par], dram["wo"][bass.ds(h + 1, 1)]
                             .rearrange("o p n -> (o p) n")).then_inc(wo_in[1 - par], 16)
                if isinstance(h, int) and h + 2 >= H1:
                    return
                sp.wait_ge(k_ready, 4 * h + 4)
                sp.wait_ge(v_psum, 4 * h + 4)
                sp.dma_start(wkv[:, par], dram["wkv"][bass.ds(h + 2, 1)]
                             .rearrange("o p n -> (o p) n")).then_inc(wkv_in[par], 16)
            heads(sp, loads)

        @block.tensor
        def _(pe):
            def k_unit(par, b, bank):
                for j in range(J):
                    mm = pe.matmul(bank[:, 0:T], wkv[:, par, j * P:(j + 1) * P], gruT[:, j, b, LEADING:],
                                   start=(j == 0), stop=(j == J - 1))
                mm.then_inc(k_psum, 1)

            def k_unit_parts(par, b, bank):
                n = 0
                for j in range(J):
                    cols = slice(j * P, (j + 1) * P)
                    for w, g in ((wk_hi, g_hi), (wk_hi, g_lo), (wk_lo, g_hi)):
                        mm = pe.matmul(bank[:, 0:T], w[:, par, cols], g[:, j, b, :],
                                       start=(n == 0), stop=(n == 3 * J - 1))
                        n += 1
                mm.then_inc(k_psum, 1)

            def v_unit(par, b, bank):
                for sc in range(TC):
                    for j in range(J):
                        mm = pe.matmul(bank[:, sc * DH1:(sc + 1) * DH1],
                                       gruT[:, j, b, LEADING + sc * P:LEADING + (sc + 1) * P],
                                       wkv[:, par, (J + j) * P:(J + j + 1) * P],
                                       start=(j == 0), stop=(j == J - 1))
                mm.then_inc(v_psum, 1)

            def score_unit(par, b, bank):
                for tc in range(TC):
                    mm = pe.matmul(bank[:, tc * P:(2 * tc + 1) * P],
                                   qh[:, par, b, tc * P:(tc + 1) * P],
                                   kh[:, par, b, 0:(tc + 1) * P], start=True, stop=True)
                mm.then_inc(s_psum, 1)

            def out_unit(par, b):
                for tc in range(TC):
                    for o, w in ((oT_hi, wo_hi), (oT_hi, wo_lo), (oT_lo, wo_hi)):
                        mm = pe.matmul(acc[b][:, tc * D:(tc + 1) * D], o[:, tc * P:(tc + 1) * P],
                                       w[:, par, :], start=False, stop=False, skip_group_check=True)
                mm.then_inc(op_done, 1)

            def left_query(n):
                place, c = H1 + (n > 0), (n - 1) % H1
                if n >= B:
                    pe.wait_ge(q_read, n - B + 1)
                for j in range(J):
                    mm = pe.matmul(acc[n % B][:, 0:B * QB].rearrange("p (b t) -> p b t", b=B),
                                   wq[:, c, j * P:(j + 1) * P],
                                   gruT[:, j, :, place * QB:(place + 1) * QB],
                                   start=(j == 0), stop=(j == J - 1))
                mm.then_inc(q_psum, 1)

            pe.wait_ge(wkv_in[0], 16)
            for b in range(B):
                if b >= 2:
                    pe.wait_ge(k_ready, b - 1)
                k_unit(0, b, (OB, S[1])[b % 2])
                if b >= 2:
                    pe.wait_ge(v_ready, b - 1)
                v_unit(0, b, (TB, S[0])[b % 2])
                for n in left_after[b]:
                    left_query(n)
            pe.wait_ge(k_ready, B)
            pe.wait_ge(v_ready, B)
            pe.wait_ge(qh_ready, 1)
            score_unit(0, 0, S[0])
            pe.wait_ge(q_read, H1 + 1)
            pe.wait_ge(const_in, 48)
            pe.wait_ge(ones_ready, 1)
            for b in range(B):
                for tc in range(TC):
                    mm = pe.matmul(acc[b][:, tc * D:(tc + 1) * D], ones[:], bo[:], start=(tc == 0),
                                   stop=False, skip_group_check=True)
            mm.then_inc(op_done, 1)
            pe.wait_ge(g_lo_ready, B)
            pe.wait_ge(zeros_ready, 5)

            def head(i, h, par, last):
                for b in range(B):
                    u = h * 4 + b
                    if not (last and b == B - 1):
                        if last:
                            pe.wait_ge(k_ready, units)
                            pe.wait_ge(exp_done, u)
                        else:
                            pe.wait_ge(k_ready, u + 4)
                        if b == B - 1:
                            pe.wait_ge(qh_ready, h + 2)
                        score_unit(par if b < B - 1 else 1 - par, (b + 1) % B, S[(b + 1) % 2])
                    pe.wait_ge(p_ready, u + 1)
                    pe.wait_ge(v_ready, units if last else u + 4)
                    for n in range(3):
                        mm = pe.transpose(TB[:, n * P:(n + 1) * P],
                                          probs[:, b % 2, n * P:(n + 1) * P], ident[:])
                    mm.then_inc(t_psum, 1)
                    if not last:
                        if b == 0:
                            pe.wait_ge(wkv_in[1 - par], 16 * (i + par) + 16)
                            pe.wait_ge(wk_split, h + 1)
                        k_unit_parts(1 - par, b, S[b % 2])
                    if b == 1:
                        pe.wait_ge(wo_split, h + 1)
                    pe.wait_ge(oT_ready, u + 1)
                    out_unit(par if b else 1 - par, (b - 1) % B)
                    pe.wait_ge(pT_ready, u + 1)
                    pe.matmul(OB[:, 0:P], vh[:, par, b, 0:DH1], probsT[:, 0:P],
                              start=True, stop=False, skip_group_check=True)
                    pe.matmul(OB[:, P:T], vh[:, par, b, 0:DH1], probsT[:, P:2 * P],
                              start=False, stop=False, skip_group_check=True)
                    pe.matmul(OB[:, P:T], vh[:, par, b, DH1:2 * DH1], probsT[:, 2 * P:3 * P],
                              start=False, stop=True, skip_group_check=True).then_inc(o_psum, 1)
                    if not last:
                        v_unit(1 - par, b, TB)
            heads(pe, head)
            pe.wait_ge(oT_ready, units + 1)
            out_unit(1, B - 1)

        @block.scalar
        def _(act):
            def key(par, b, bank, n):
                act.wait_ge(k_psum, n + 1)
                nc.scalar.activation(kh[:, par, b, :], bank[:, 0:T], ACT.Identity,
                                     bias=wkv[:, par, 2 * J * P:2 * J * P + 1]).then_inc(k_ready, 1)

            def exps(n, par):
                act.wait_ge(nmax_ready, n + 1)
                for tc in range(TC):
                    c = slice(tc * P, (2 * tc + 1) * P)
                    a = nc.scalar.activation(probs[:, par, c], logits[:, par, c], ACT.Exp,
                                             bias=nmax[:, par, tc:tc + 1],
                                             accum_out=rsum[:, par, tc:tc + 1])
                a.then_inc(exp_done, 1)

            for b in range(B):
                nc.scalar.activation(g_hi[:, :, b, :], gruT[:, :, b, LEADING:],
                                     ACT.Copy).then_inc(g_hi_ready, 1)
            for b in range(B):
                key(0, b, (OB, S[1])[b % 2], b)
                for n in left_after[b]:
                    place, c = H1 + (n > 0), (n - 1) % H1
                    act.wait_ge(q_psum, n + 1)
                    nc.scalar.activation(QT[:, place, :, :, c],
                                         acc[n % B][:, 0:B * QB].rearrange("p (b t) -> p b t", b=B),
                                         ACT.Identity,
                                         bias=wq[:, c, J * P:J * P + 1]).then_inc(q_read, 1)
            exps(0, 0)

            def head(i, h, par, last):
                for b in range(B):
                    u = h * 4 + b
                    if not (last and b == B - 1):
                        if isinstance(h, int) or b > 0:
                            act.wait_ge(t_psum, u)
                        exps(u + 1, (b + 1) % 2)
                    if not last:
                        key(1 - par, b, S[b % 2], u + 4)
                    if b == 0:
                        act.wait_ge(wo_in[par], 16 * i + 16)
                    act.wait_ge(op_done, u + 2)
                    act.wait_ge(o_psum, u + 1)
                    nc.scalar.activation(oT_hi[:], OB[:, 0:T], ACT.Identity,
                                         bias=wo[:, par, D:D + 1]).then_inc(oT_hi_ready, 1)
            heads(act, head)

        @block.vector
        def _(dve):
            nc.vector.memset(ones[:], 1.0).then_inc(ones_ready, 1)
            nc.vector.memset(waiter[:], 0.0).then_inc(oT_ready, 1)
            nc.vector.memset(zeros[:], 0.0).then_inc(zeros_ready, 1)
            dve.wait_ge(zeros_ready, 1)
            for dst in (wo_hi[:, 1, :], wo_lo[:, 1, :], oT_hi[:], oT_lo[:]):
                nc.vector.tensor_copy(dst, zeros[:]).then_inc(zeros_ready, 1)
            for b in range(B):
                dve.wait_ge(g_hi_ready, b + 1)
                nc.vector.tensor_tensor(g_lo[:, :, b, :], gruT[:, :, b, LEADING:],
                                        g_hi[:, :, b, :].bitcast(F32),
                                        ALU.subtract).then_inc(g_lo_ready, 1)

            def value(par, b, n, bank):
                dve.wait_ge(v_psum, n + 1)
                nc.vector.tensor_copy(vh[:, par, b, :], bank[:, 0:TC * DH1]).then_inc(v_ready, 1)

            def maxima(n, par, bank):
                dve.wait_ge(s_psum, n + 1)
                nc.vector.memset(waiter[:], 0.0)
                for tc in range(TC):
                    c = slice(tc * P, (2 * tc + 1) * P)
                    a = nc.vector.tensor_tensor_reduce(
                        out=logits[:, par, c], in0=bank[:, c], in1=mask[:, c], scale=scale,
                        scalar=-3.0e38, op0=ALU.add, op1=ALU.max, accum_out=rmax[:, par, tc:tc + 1])
                a.then_inc(max_ready, 1)
                dve.wait_ge(max_ready, n + 1)
                nc.vector.tensor_scalar(nmax[:, par, :], rmax[:, par, :], -1.0, None,
                                        ALU.mult).then_inc(nmax_ready, 1)

            def inverse(n, par):
                dve.wait_ge(exp_done, n + 1)
                nc.vector.reciprocal(rinv[:, par, :], rsum[:, par, :]).then_inc(rinv_ready, 1)

            for b in range(B):
                value(0, b, b, (TB, S[0])[b % 2])
            maxima(0, 0, S[0])
            inverse(0, 0)

            def head(i, h, par, last):
                for b in range(B):
                    u = h * 4 + b
                    nxt = (b + 1) % 2
                    if not (last and b == B - 1):
                        maxima(u + 1, nxt, S[nxt])
                    dve.wait_ge(t_psum, u + 1)
                    nc.vector.tensor_copy(probsT[:], TB[:, 0:3 * P]).then_inc(pT_ready, 1)
                    if not (last and b == B - 1):
                        inverse(u + 1, nxt)
                    dve.wait_ge(oT_hi_ready, u + 1)
                    nc.vector.memset(waiter_o[:], 0.0)
                    nc.vector.scalar_tensor_tensor(out=oT_lo[:], in0=OB[:, 0:T],
                                                   scalar=wo[:, par, D:D + 1],
                                                   in1=oT_hi[:].bitcast(F32), op0=ALU.add,
                                                   op1=ALU.subtract).then_inc(oT_ready, 1)
                    if not last:
                        value(1 - par, b, u + 4, TB)
            heads(dve, head)
            dve.wait_ge(x_in, 16)
            dve.wait_ge(op_done, units + 2)
            for b in range(B):
                nc.vector.tensor_tensor(x1[:, 2 * b:2 * b + 2, :].rearrange("p a d -> p (a d)"),
                                        acc[b][:], x1[:, 2 * b:2 * b + 2, :]
                                        .rearrange("p a d -> p (a d)"), ALU.add) \
                                            .then_inc(x1_ready, 1)

        @block.gpsimd
        def _(pool):
            def query(h, par):
                if isinstance(h, int):
                    src = QT[:, h + 2].rearrange("p b r c -> p b (r c)")
                else:
                    src = QT[:, bass.ds(h + 2, 1)].rearrange("p o b r c -> p (o b) (r c)")
                nc.gpsimd.tensor_copy(qh[:, par], src).then_inc(qh_ready, 1)

            def weights(n, par):
                pool.wait_ge(rinv_ready, n + 1)
                for tc in range(TC):
                    c = slice(tc * P, (2 * tc + 1) * P)
                    a = nc.gpsimd.tensor_tensor(
                        probs[:, par, c], probs[:, par, c],
                        rinv[:, par, tc:tc + 1].to_broadcast([P, (tc + 1) * P]), ALU.mult)
                a.then_inc(p_ready, 1)
            def split(raw, hi, lo, loaded, count, written, n, done):
                pool.wait_ge(loaded, count)
                nc.gpsimd.tensor_tensor(waiter_p[:], raw[0:1, 0:1], raw[0:1, 0:1], ALU.add)
                nc.gpsimd.tensor_copy(hi, raw).then_inc(written, 1)
                pool.wait_ge(written, n)
                nc.gpsimd.tensor_tensor(lo, raw, hi.bitcast(F32), ALU.subtract).then_inc(done, 1)

            def split_key(par, count, n):
                split(wkv[:, par, 0:J * P], wk_hi[:, par, :], wk_lo[:, par, :], wkv_in[par], count,
                      wk_hi_written, n, wk_split)

            def split_out(par, count, n):
                split(wo[:, par, 0:D], wo_hi[:, par, :], wo_lo[:, par, :], wo_in[par], count,
                      wo_hi_written, n, wo_split)

            query(0, 0)
            split_out(0, 16, 1)
            split_key(1, 16, 1)
            weights(0, 0)

            def head(i, h, par, last):
                for b in range(B):
                    u = h * 4 + b
                    if b == 0 and not last:
                        pool.wait_ge(s_psum, u + 1)
                        query(h + 1, 1 - par)
                    if b == 2 and not isinstance(h, int):
                        split_key(par, 16 * i + 32, h + 2)
                    if b == 3 and not last:
                        split_out(1 - par, 16 * (i + par) + 16, h + 2)
                    if not (last and b == B - 1):
                        weights(u + 1, (b + 1) % 2)
            heads(pool, head)


ADALN_LOADS = ("wemb", "bemb", "gnorm", "condT", "wqkv", "gqk", "wout", "ident", "parity")


def adaln_buffers(nc, stack, place):
    return ahead(nc, stack, "adaln", {
        "wemb": [P, J, 2 * D], "bemb": [P, 4], "gnorm": [P, J], "condT": [P, J, B],
        "wqkv": [P, J, 3 * D], "gqk": [P, 2 * D], "wout": [P, J, D], "ident": [P, P],
        "parity": [P, 2]}, ("w_in",), place)


def adaln_loads(sp, dram, a):
    for name in ADALN_LOADS:
        sp.dma_start(a[name][:], dram[name]).then_inc(a["w_in"], 16)


def adaln_block(nc, dram, held, x1, yT, load_ahead):
    eps, scale = 1e-6, float(DH2) ** -0.5
    PAIRS = TILES * H2 // 2
    RUN = 2 * TC + 1
    LEAD, PPT = 3, H2 // 2
    with ExitStack() as ctx:
        def sb(name, shape, dt=F32):
            return ctx.enter_context(nc.sbuf_tensor(name, shape, dt))

        def sem(name):
            return ctx.enter_context(nc.semaphore(name))

        wemb, bemb, gnorm, condT = held["wemb"], held["bemb"], held["gnorm"], held["condT"]
        wqkv, gqk, wout = held["wqkv"], held["gqk"], held["wout"]
        ident, parity = held["ident"], held["parity"]
        emb = sb("emb", [P, 4, B])
        gain = sb("gain", [P, J, B])
        epst = sb("epst", [P, 1])
        ss = sb("ss", [P, TILES])
        rms = sb("rms", [P, TILES])
        rstd = sb("rstd", [P, TILES])
        xn = sb("xn", [P, TILES, D])
        xnT = sb("xnT", [P, J, NT])
        qk = sb("qk", [P, TILES, 2 * D])
        sq = sb("sq", [P, 2, 2 * D])
        ss2 = sb("ss2", [P, TILES, 32])
        rms2 = sb("rms2", [P, TILES, 32])
        rstd2 = sb("rstd2", [P, TILES, 32])
        v = sb("v", [P, TILES, H2 // 2, 2, 2, DH2])
        qT_hi, qT_lo = (sb(f"qT_{part}", [P, J, NT], F32R) for part in ("hi", "lo"))
        kT_hi, kT_lo = (sb(f"kT_{part}", [P, J, B, 2, T], F32R) for part in ("hi", "lo"))
        mx = sb("mx", [P, 4, 2])
        nmx = sb("nmx", [P, 4, 2])
        rsum = sb("rsum2", [P, TILES, H2])
        rinv = sb("rinv2", [P, TILES, H2])
        probs = sb("probs2", [P, 4, 2, T])
        pT = sb("pT", [P, 4, HALF])
        oT = sb("oT2", [P, J, NT])
        bk = [ctx.enter_context(nc.psum_tensor(f"cb{i}", [P, HALF], F32)) for i in range(8)]

        w_in = held["w_in"]
        emb_psum, emb_act, gain_ready = (sem(n) for n in ("emb_psum", "emb_act", "gain_ready"))
        ss_ready, rms_ready, rstd_ready, xn_ready = (sem(n) for n in (
            "ss_ready", "rms_ready", "rstd_ready", "xn_ready"))
        xt_psum, xt_done, qk_psum, qk_done, v_psum, v_done = (sem(n) for n in (
            "xt_psum", "xt_done", "qk_psum2", "qk_done", "v_psum2", "v_done"))
        sq_ready, ss2_ready, rms2_ready, rstd2_ready, qn_dve, qn_pool, qn_part = (sem(n) for n in (
            "sq_ready", "ss2_ready", "rms2_ready", "rstd2_ready", "qn_dve", "qn_pool", "qn_part"))
        qn_part_pool = sem("qn_part_pool")
        t_psum, tq_done, tk_done = sem("t_psum2"), sem("tq_done"), sem("tk_done")
        tq_hi, tk_hi = sem("tq_hi"), sem("tk_hi")
        sc_psum, mx_ready, nmx_ready, exp_done = (sem(n) for n in (
            "sc_psum", "mx_ready", "nmx_ready", "exp_done2"))
        tr_psum, pt_dve, pt_act, pv_done = (sem(n) for n in (
            "tr_psum", "pt_dve", "pt_act", "pv_done"))
        v_zero, rinv_ready, norm_done, ot_done, y_psum, y_done = (sem(n) for n in (
            "v_zero", "rinv_ready2", "norm_done", "ot_done2", "y_psum", "y_done"))
        block = ctx.enter_context(nc.Block())

        def tile_cols(i):
            return slice(i * P, (i + 1) * P)

        @block.sync
        def _(sp):
            load_ahead(sp)

        @block.tensor
        def _(pe):
            pe.wait_ge(w_in, 16 * len(ADALN_LOADS))
            for m in range(4):
                for j in range(J):
                    mm = pe.matmul(bk[7][:, m * B:(m + 1) * B], wemb[:, j, m * P:(m + 1) * P],
                                   condT[:, j, :], start=(j == 0), stop=(j == J - 1))
            mm.then_inc(emb_psum, 1)
            for n in range(B * J):
                b, j = n // J, n % J
                if n >= 4:
                    pe.wait_ge(xt_done, n - 3)
                for tc in range(TC):
                    i = b * TC + tc
                    pe.wait_ge(xn_ready, i + 1)
                    mm = pe.transpose(bk[n % 4][:, tile_cols(tc)], xn[:, i, j * P:(j + 1) * P],
                                      ident[:])
                mm.then_inc(xt_psum, 1)
            pe.wait_ge(emb_act, 4)
            for step in range(TILES + RUN):
                if step >= RUN and (step - RUN) % TC == 0:
                    b = (step - RUN) // TC
                    pe.wait_ge(xt_done, B * J)
                    pe.wait_ge(qn_dve, b + 1)
                    pe.wait_ge(qn_pool, b + 1)
                    for n in range(2 * J):
                        which, j = n // J, n % J
                        if b >= 1:
                            pe.wait_ge((tq_done, tk_done)[which], J * (b - 1) + j + 1)
                        c0 = which * D + j * P
                        for tc in range(TC):
                            mm = pe.transpose(bk[n][:, tile_cols(tc)],
                                              qk[:, b * TC + tc, c0:c0 + P], ident[:])
                        mm.then_inc(t_psum, 1)
                if step >= TILES:
                    continue
                i = step
                pe.wait_ge(xt_done, J * (i // TC + 1))
                if i >= 2:
                    pe.wait_ge(qk_done, i - 1)
                    pe.wait_ge(v_done, i - 1)
                for j in range(J):
                    mm = pe.matmul(bk[4 + i % 2][:], xnT[:, j, tile_cols(i)], wqkv[:, j, 0:2 * D],
                                   start=(j == 0), stop=(j == J - 1))
                mm.then_inc(qk_psum, 1)
                for j in range(J):
                    mm = pe.matmul(bk[6 + i % 2][:, 0:D], xnT[:, j, tile_cols(i)],
                                   wqkv[:, j, 2 * D:3 * D], start=(j == 0), stop=(j == J - 1))
                mm.then_inc(v_psum, 1)
            pe.wait_ge(tq_done, J * B)
            pe.wait_ge(tk_done, J * B)

            def scores(n):
                i, j, p = n // PPT, n // 4 % J, n % 4
                rows = slice(32 * p, 32 * p + 32)
                if n >= 4:
                    pe.wait_ge(exp_done, n - 3)
                for n, (q, k) in enumerate(((qT_hi, kT_hi), (qT_hi, kT_lo), (qT_lo, kT_hi))):
                    mm = pe.matmul(bk[p][:], q[rows, j, tile_cols(i)],
                                   k[rows, j, i // TC].rearrange("p e t -> p (e t)"),
                                   start=(n == 0), stop=(n == 2), tile_position=(32 * p, 0))
                mm.then_inc(sc_psum, 1)

            def pv_pair(n):
                i, g, p = n // PPT, n // 4, n % 4
                pe.wait_ge((pt_dve, pt_act)[n % 2], n // 2 + 1)
                if p == 0 and g >= 2:
                    pe.wait_ge(ot_done, g - 1)
                for k in range(2 * TC):
                    e, sc = k // TC, k % TC
                    mm = pe.matmul(bk[6 + g % 2][32 * p:32 * p + 32, 0:P],
                                   v[:, (i // TC) * TC + sc, n % PPT, e].rearrange("p z d -> p (z d)"),
                                   pT[:, n % 4, k * P:(k + 1) * P], start=(k == 0),
                                   stop=(k == 2 * TC - 1), tile_position=(0, 32 * p))
                mm.then_inc(pv_done, 1)

            for n in range(LEAD):
                scores(n)
            pe.wait_ge(v_done, TILES)
            for n in range(PAIRS):
                if n % 2 == 0:
                    for m in range(n + LEAD, min(n + LEAD + 2, PAIRS)):
                        scores(m)
                pe.wait_ge(norm_done, n + 1)
                if n >= 2:
                    pe.wait_ge((pt_dve, pt_act)[n % 2], n // 2)
                for k in range(2 * TC):
                    mm = pe.transpose(bk[4 + n % 2][:, k * P:(k + 1) * P],
                                      probs[:, n % 4, k // TC, k % TC * P:(k % TC + 1) * P], ident[:])
                mm.then_inc(tr_psum, 1)
                if n >= 2:
                    pv_pair(n - 2)
            pv_pair(PAIRS - 2)
            pv_pair(PAIRS - 1)
            for n in range(4):
                m, half = n % 2, n // 2
                pe.wait_ge(ot_done, PAIRS // 8 * (half + 1))
                for j in range(J):
                    mm = pe.matmul(bk[4 + n][:], wout[:, j, m * P:(m + 1) * P],
                                   oT[:, j, half * HALF:(half + 1) * HALF],
                                   start=(j == 0), stop=(j == J - 1))
                mm.then_inc(y_psum, 1)

        def transposed(eng, n):
            eng.wait_ge(tr_psum, n + 1)
            if n >= 4:
                eng.wait_ge(pv_done, n - 3)
            if n % 2:
                nc.scalar.activation(pT[:, n % 4, :], bk[4 + n % 2][:], ACT.Copy) \
                    .then_inc(pt_act, 1)
            else:
                nc.vector.tensor_copy(pT[:, n % 4, :], bk[4 + n % 2][:]).then_inc(pt_dve, 1)

        @block.scalar
        def _(act):
            act.wait_ge(emb_psum, 1)
            for m in range(4):
                nc.scalar.activation(emb[:, m, :], bk[7][:, m * B:(m + 1) * B], ACT.Identity,
                                     bias=bemb[:, m:m + 1]).then_inc(emb_act, 1)
            act.wait_ge(ss_ready, TILES + 1)
            nc.scalar.activation(rms[:], ss[:], ACT.Sqrt, bias=epst[:],
                                 scale=1.0 / D).then_inc(rms_ready, 1)
            act.wait_ge(gain_ready, 2)
            for n in range(B * J):
                b, j = n // J, n % J
                act.wait_ge(xt_psum, n + 1)
                nc.scalar.activation(xnT[:, j, b * T:(b + 1) * T], bk[n % 4][:, 0:T], ACT.Identity,
                                     bias=emb[:, J + j, b:b + 1],
                                     scale=gain[:, j, b:b + 1]).then_inc(xt_done, 1)
            for step in range(TILES + RUN):
                if step >= RUN and (step - RUN) % TC == 0:
                    b = (step - RUN) // TC
                    for j in range(J):
                        act.wait_ge(t_psum, 2 * J * b + j + 1)
                        nc.scalar.activation(qT_hi[:, j, b * T:(b + 1) * T], bk[j][:, 0:T],
                                             ACT.Copy).then_inc(tq_hi, 1)
                    for j in range(J):
                        act.wait_ge(t_psum, 2 * J * b + J + j + 1)
                        for e in range(2):
                            a = nc.scalar.activation(kT_hi[:, j, b, e, :], bk[J + j][:, 0:T],
                                                     ACT.Identity, scale=parity[:, e:e + 1])
                        a.then_inc(tk_hi, 1)
                if step < TILES:
                    act.wait_ge(qk_psum, step + 1)
                    nc.scalar.activation(qk[:, step, :], bk[4 + step % 2][:],
                                         ACT.Copy).then_inc(qk_done, 1)
                if step % TC == 0 and 0 < step <= TILES:
                    rows = slice(step - TC, step)
                    act.wait_ge(ss2_ready, step)
                    nc.scalar.activation(rms2[:, rows, :], ss2[:, rows, :], ACT.Sqrt, bias=epst[:],
                                         scale=1.0 / DH2).then_inc(rms2_ready, 1)
            for n in range(PAIRS + LEAD):
                if n >= LEAD and (n - LEAD) % 2:
                    transposed(act, n - LEAD)
                if n >= PAIRS:
                    continue
                act.wait_ge(nmx_ready, n + 1)
                if n >= 4:
                    act.wait_ge(tr_psum, n - 3)
                for e in range(2):
                    h = n % PPT * 2 + e
                    a = nc.scalar.activation(probs[:, n % 4, e, :], bk[n % 4][:, e * T:(e + 1) * T],
                                             ACT.Exp, bias=nmx[:, n % 4, e:e + 1], scale=scale,
                                             accum_out=rsum[:, n // PPT, h:h + 1])
                a.then_inc(exp_done, 1)

        @block.vector
        def _(dve):
            nc.vector.memset(epst[:], eps).then_inc(ss_ready, 1)
            for i in range(TILES):
                nc.vector.tensor_tensor_reduce(out=xn[:, i, :], in0=x1[:, i, :], in1=x1[:, i, :],
                                               scale=1.0, scalar=0.0, op0=ALU.mult, op1=ALU.add,
                                               accum_out=ss[:, i:i + 1]).then_inc(ss_ready, 1)
            dve.wait_ge(emb_act, 4)
            nc.vector.tensor_scalar(gain[:].rearrange("p j b -> p (j b)"),
                                    emb[:, 0:J, :].rearrange("p j b -> p (j b)"), 1.0, None,
                                    ALU.add).then_inc(gain_ready, 1)
            dve.wait_ge(gain_ready, 1)
            for j in range(J):
                a = nc.vector.tensor_scalar(gain[:, j, :], gain[:, j, :], gnorm[:, j:j + 1], None,
                                            ALU.mult)
            a.then_inc(gain_ready, 1)
            dve.wait_ge(rms_ready, 1)
            nc.vector.reciprocal(rstd[:], rms[:]).then_inc(rstd_ready, 1)
            dve.wait_ge(rstd_ready, 1)
            for i in range(TILES):
                nc.vector.tensor_scalar(xn[:, i, :], x1[:, i, :], rstd[:, i:i + 1], None,
                                        ALU.mult).then_inc(xn_ready, 1)
            dve.wait_ge(v_zero, 1)
            for step in range(TILES + RUN):
                if step >= RUN and (step - RUN) % TC == 0:
                    b = (step - RUN) // TC
                    for j in range(J):
                        cols = slice(b * T, (b + 1) * T)
                        dve.wait_ge(tq_hi, J * b + j + 1)
                        nc.vector.tensor_tensor(qT_lo[:, j, cols], bk[j][:, 0:T],
                                                qT_hi[:, j, cols].bitcast(F32),
                                                ALU.subtract).then_inc(tq_done, 1)
                    for j in range(J):
                        dve.wait_ge(tk_hi, J * b + j + 1)
                        for e in range(2):
                            a = nc.vector.scalar_tensor_tensor(
                                out=kT_lo[:, j, b, e, :], in0=bk[J + j][:, 0:T],
                                scalar=parity[:, e:e + 1], in1=kT_hi[:, j, b, e, :].bitcast(F32),
                                op0=ALU.mult, op1=ALU.subtract)
                        a.then_inc(tk_done, 1)
                i = step
                if step < TILES:
                    dve.wait_ge(v_psum, i + 1)
                    src = bk[6 + i % 2][:, 0:D].rearrange("p (n z d) -> p n z d", z=2, d=DH2)
                    for e in range(2):
                        a = nc.vector.tensor_copy(v[:, i, :, e, e, :], src[:, :, e, :])
                    a.then_inc(v_done, 1)
                normalised = step % TC == 0 and 0 < step <= TILES
                if normalised:
                    b, rows = step // TC - 1, slice(step - TC, step)
                    dve.wait_ge(rms2_ready, b + 1)
                    nc.vector.reciprocal(rstd2[:, rows, :], rms2[:, rows, :]) \
                        .then_inc(rstd2_ready, 1)
                if step < TILES:
                    dve.wait_ge(sq_ready, i + 1)
                    nc.vector.tensor_reduce(ss2[:, i, :],
                                            sq[:, i % 2].rearrange("p (h d) -> p h d", d=DH2),
                                            AX.X, ALU.add).then_inc(ss2_ready, 1)
                if normalised:
                    dve.wait_ge(rstd2_ready, b + 1)
                    i = b * TC
                    q3 = qk[:, i].rearrange("p (h d) -> p h d", d=DH2)
                    nc.vector.tensor_tensor(q3, q3, rstd2[:, i, :].unsqueeze(2)
                                            .to_broadcast([P, 32, DH2]),
                                            ALU.mult).then_inc(qn_part, 1)
                    dve.wait_ge(qn_part, b + 1)
                    nc.vector.tensor_tensor(qk[:, i], qk[:, i], gqk[:], ALU.mult) \
                        .then_inc(qn_dve, 1)

            def maxima(n):
                dve.wait_ge(sc_psum, n + 1)
                nc.vector.tensor_reduce(mx[:, n % 4, :], bk[n % 4][:].rearrange("p (e t) -> p e t", e=2),
                                        AX.X, ALU.max).then_inc(mx_ready, 1)
                dve.wait_ge(mx_ready, n + 1)
                nc.vector.tensor_scalar(nmx[:, n % 4, :], mx[:, n % 4, :], -scale, None,
                                        ALU.mult).then_inc(nmx_ready, 1)

            def out_rows(g):
                dve.wait_ge(pv_done, 4 * (g + 1))
                nc.vector.tensor_copy(oT[:, g % J, tile_cols(g // J)],
                                      bk[6 + g % 2][:, 0:P]).then_inc(ot_done, 1)

            def inverse(n):
                dve.wait_ge(exp_done, n + 1)
                heads = slice(n % PPT * 2, n % PPT * 2 + 2)
                nc.vector.reciprocal(rinv[:, n // PPT, heads],
                                     rsum[:, n // PPT, heads]).then_inc(rinv_ready, 1)

            for n in range(LEAD):
                maxima(n)
                if n:
                    inverse(n - 1)
            for n in range(PAIRS + 1):
                if n % 2 == 1:
                    transposed(dve, n - 1)
                if n + LEAD < PAIRS:
                    maxima(n + LEAD)
                if n + LEAD - 1 < PAIRS:
                    inverse(n + LEAD - 1)
                if n % 4 == 2 and n > 4:
                    out_rows(n // 4 - 1)
            out_rows(PAIRS // 4 - 1)
            for n in range(4):
                m, half = n % 2, n // 2
                dve.wait_ge(y_psum, n + 1)
                nc.vector.tensor_tensor(yT[:, m, half * HALF:(half + 1) * HALF], bk[4 + n][:],
                                        oT[:, m, half * HALF:(half + 1) * HALF],
                                        ALU.add).then_inc(y_done, 1)

        @block.gpsimd
        def _(pool):
            nc.gpsimd.memset(v[:], 0.0).then_inc(v_zero, 1)
            for step in range(TILES + 1):
                i = step
                if step < TILES:
                    pool.wait_ge(qk_done, i + 1)
                    if i >= 2:
                        pool.wait_ge(ss2_ready, i - 1)
                    nc.gpsimd.tensor_tensor(sq[:, i % 2], qk[:, i], qk[:, i],
                                            ALU.mult).then_inc(sq_ready, 1)
                if step % TC == 0 and step > 0:
                    b, i = step // TC - 1, step - 1
                    pool.wait_ge(rstd2_ready, b + 1)
                    q3 = qk[:, i].rearrange("p (h d) -> p h d", d=DH2)
                    nc.gpsimd.tensor_tensor(q3, q3, rstd2[:, i, :].unsqueeze(2)
                                            .to_broadcast([P, 32, DH2]),
                                            ALU.mult).then_inc(qn_part_pool, 1)
                    pool.wait_ge(qn_part_pool, b + 1)
                    nc.gpsimd.tensor_tensor(qk[:, i], qk[:, i], gqk[:], ALU.mult) \
                        .then_inc(qn_pool, 1)
            for n in range(PAIRS):
                pool.wait_ge(rinv_ready, n + 1)
                heads = slice(n % PPT * 2, n % PPT * 2 + 2)
                nc.gpsimd.tensor_tensor(probs[:, n % 4], probs[:, n % 4],
                                        rinv[:, n // PPT, heads].unsqueeze(2).to_broadcast([P, 2, T]),
                                        ALU.mult).then_inc(norm_done, 1)


def ffn_buffers(nc, stack):
    return ahead(nc, stack, "ffn", {"gw": [P, J, E + 1], "ident": [P, P], "wf": [P, 2, 7 * P]},
                 ("w_in", "wf_in0", "wf_in1"))


def ffn_loads(sp, dram, a):
    sp.dma_start(a["gw"][:], dram["gw"]).then_inc(a["w_in"], 16)
    sp.dma_start(a["ident"][:], dram["ident"]).then_inc(a["w_in"], 16)
    sp.dma_start(a["wf"][:, 0], dram["wf"][0]).then_inc(a["wf_in0"], 16)
    sp.dma_start(a["wf"][:, 1], dram["wf"][1]).then_inc(a["wf_in1"], 16)


def ffn_block(nc, dram, held, x1, yT, out):
    R17 = E + 1
    PAD = 4
    LO = 32
    with ExitStack() as ctx:
        def sb(name, shape, dt=F32):
            return ctx.enter_context(nc.sbuf_tensor(name, shape, dt))

        def sem(name):
            return ctx.enter_context(nc.semaphore(name))

        gw, ident = held["gw"], held["ident"]
        wf = held["wf"]
        w_hi = sb("w_hi", [P, 2, 6 * P], F32R)
        w_lo = sb("w_lo", [P, 2, 6 * P], F32R)
        select = sb("select", [2 * LO, 2, P], F32R)
        y_hi = sb("y_hi", [P, J, NT], F32R)
        y_lo = sb("y_lo", [P, J, NT], F32R)
        lg = sb("lg", [P, TILES, R17])
        mx = sb("mxr", [P, TILES])
        ex = sb("ex", [P, TILES, E])
        pr = sb("pr", [P, TILES, E + PAD])
        den = sb("den", [P, TILES])
        rden = sb("rden", [P, TILES])
        top = sb("top", [P, TILES, 8])
        rep = sb("rep", [P, TILES, E + PAD])
        cw = sb("cw", [P, TILES, R17])
        es = sb("es", [P, TILES])
        cw_hi = sb("cw_hi", [P, TILES, R17], F32R)
        cw_parts = sb("cw_parts", [P, TILES, 2 * LO])
        cwT = sb("cwT", [2 * LO, NT], F32R)
        act_g = sb("act_g", [P, 2, HALF])
        prod = sb("prod", [P, 2, HALF])
        hT = sb("hT", [P, 2, HALF])
        h_hi = sb("h_hi", [P, 2, HALF], F32R)
        h_lo = sb("h_lo", [P, 2, HALF], F32R)
        outT = sb("outT", [P, J, NT])
        waiter = sb("waiter_f", [1, 1])
        fin = sb("fin", [P, TILES, D])
        acc = [ctx.enter_context(nc.psum_tensor(f"fa{i}", [P, HALF], F32)) for i in range(4)]
        GB, UB, CB, XB = [ctx.enter_context(nc.psum_tensor(f"fb{i}", [P, HALF], F32))
                          for i in range(4)]
        w_in, wf_in = held["w_in"], (held["wf_in0"], held["wf_in1"])
        y_hi_ready, y_lo_ready = sem("y_hi_ready"), sem("y_lo_ready")
        lg_psum, chain, exps, cw_ready, ct_psum, ct_done, es_done = (sem(n) for n in (
            "lg_psum", "chain", "exps", "cw_ready", "ct_psum", "ct_done", "es_done"))
        gu_ready, zeros_ready, d_ready, d_done = (sem(n) for n in (
            "gu_ready", "zeros_ready", "d_ready", "d_done"))
        hi_written, d_hi_written = sem("hi_written"), sem("d_hi_written")
        g_psum, u_psum, c_psum = (sem(n) for n in ("g_psum", "u_psum", "c_psum"))
        g_act, prod_ready, h_made, hi_ready, lo_ready = (sem(n) for n in (
            "g_act", "prod_ready", "h_made", "hi_ready", "lo_ready"))
        out_read = [sem(f"out_read{hf}") for hf in range(2)]
        t_psum, fin_ready, stored = (sem(n) for n in (
            "t_psum3", "fin_ready", "stored"))
        block = ctx.enter_context(nc.Block())
        halves = [slice(0, HALF), slice(HALF, NT)]

        @block.sync
        def _(sp):
            with sp.Fori(0, NCH // 2 - 1) as i:
                for par in range(2):
                    sp.wait_ge(d_ready, i * 2 + par + 1)
                    sp.dma_start(wf[:, par], dram["wf"][bass.ds(i * 2 + 2 + par, 1)]
                                 .rearrange("o p n -> (o p) n")).then_inc(wf_in[par], 16)
            out_rows = out.rearrange("(i p) d -> p i d", p=P)
            for a in range(4):
                sp.wait_ge(fin_ready, a + 1)
                sp.dma_start(out_rows[:, 2 * a:2 * a + 2, :],
                             fin[:, 2 * a:2 * a + 2, :]).then_inc(stored, 16)
            sp.wait_ge(stored, 64)

        @block.tensor
        def _(pe):
            pe.wait_ge(w_in, 32)
            for i in range(TILES):
                for j in range(J):
                    mm = pe.matmul(XB[:, i * R17:(i + 1) * R17], yT[:, j, i * P:(i + 1) * P],
                                   gw[:, j, :], start=(j == 0), stop=(j == J - 1))
            mm.then_inc(lg_psum, 1)
            pe.wait_ge(cw_ready, 2)
            for i in range(TILES):
                mm = pe.matmul((GB, UB)[i // 4][0:2 * LO, (i % 4) * P:(i % 4 + 1) * P],
                               cw_parts[:, i, :], ident[:], start=True, stop=True)
            mm.then_inc(ct_psum, 1)
            pe.wait_ge(zeros_ready, 3)
            pe.wait_ge(lo_ready, 1)
            for a in range(4):
                mm = pe.matmul(acc[a][:], w_hi[:, 1, 4 * P:5 * P], h_hi[:, 1, :], start=True,
                               stop=False, skip_group_check=True)
            mm.then_inc(d_done, 1)
            pe.wait_ge(ct_done, 2)
            pe.wait_ge(y_lo_ready, 2)

            def product(dst, par, c0, hf, ready):
                n = 0
                for j in range(J):
                    cols = slice((c0 + j) * P, (c0 + j + 1) * P)
                    for w, y in ((w_hi, y_hi), (w_hi, y_lo), (w_lo, y_hi)):
                        mm = pe.matmul(dst[:], w[:, par, cols], y[:, j, halves[hf]],
                                       start=(n == 0), stop=(n == 3 * J - 1))
                        n += 1
                return mm.then_inc(ready, 1)

            def summed(par, hf):
                for m in range(J):
                    cols = slice((4 + m) * P, (5 + m) * P)
                    for w, h in ((w_hi, h_hi), (w_lo, h_hi), (w_hi, h_lo)):
                        mm = pe.matmul(acc[2 * m + hf][:], w[:, par, cols], h[:, hf, :],
                                       start=False, stop=False, skip_group_check=True)
                mm.then_inc(d_done, 1)

            with pe.Fori(0, NCH // 2) as i:
                for k in range(4):
                    par, hf, u = k // 2, k % 2, i * 4 + k
                    if hf == 0:
                        pe.wait_ge(gu_ready, i * 2 + par + 1)
                    pe.wait_ge(g_act, u + 1)
                    product(GB, par, 0, hf, g_psum)
                    pe.wait_ge(prod_ready, u + 1)
                    product(UB, par, J, hf, u_psum)
                    pe.wait_ge(h_made, u + 1)
                    pe.matmul(CB[:], select[:, par, :], cwT[:, halves[hf]],
                              start=True, stop=True).then_inc(c_psum, 1)
                    pe.wait_ge(lo_ready, u + 1)
                    if hf == 1:
                        pe.wait_ge(d_ready, i * 2 + par + 1)
                    summed((k - 1) % 4 // 2, (k - 1) % 2)
            pe.wait_ge(lo_ready, 2 * NCH + 1)
            summed(1, 1)
            for n in range(4):
                pe.wait_ge(out_read[n // 2], J)
                for k in range(4):
                    i, m = 2 * n + k // 2, k % 2
                    mm = pe.transpose((GB, UB, CB, XB)[n][:, k * P:(k + 1) * P],
                                      outT[:, m, i * P:(i + 1) * P], ident[:])
                mm.then_inc(t_psum, 1)

        @block.scalar
        def _(act):
            for hf in range(2):
                nc.scalar.activation(y_hi[:, :, halves[hf]], yT[:, :, halves[hf]],
                                     ACT.Copy).then_inc(y_hi_ready, 1)
            act.wait_ge(chain, 4)
            nc.scalar.activation(ex[:].rearrange("p i e -> p (i e)"),
                                 ex[:].rearrange("p i e -> p (i e)"), ACT.Exp).then_inc(exps, 1)
            nc.scalar.activation(es[:], lg[:, :, E], ACT.Exp, scale=-1.0).then_inc(es_done, 1)
            with act.Fori(0, NCH // 2) as i:
                for k in range(4):
                    u = i * 4 + k
                    act.wait_ge(g_psum, u + 1)
                    act.wait_ge(prod_ready, u + 1)
                    nc.scalar.activation(act_g[:, k % 2, :], GB[:], ACT.Silu).then_inc(g_act, 1)
                    act.wait_ge(h_made, u + 2)
                    act.wait_ge(d_done, u + 2)
                    nc.scalar.activation(h_hi[:, k % 2, :], hT[:, k % 2, :],
                                         ACT.Copy).then_inc(hi_ready, 1)
            act.wait_ge(d_done, 2 * NCH + 3)
            for m in range(J):
                nc.scalar.activation(outT[:, m, 0:HALF], acc[2 * m][:],
                                     ACT.Copy).then_inc(out_read[0], 1)

        @block.vector
        def _(dve):
            def link(a, n):
                a.then_inc(chain, 1)
                dve.wait_ge(chain, n)
            nc.vector.memset(mx[:], 0.0).then_inc(chain, 1)
            nc.vector.memset(den[:], 0.0).then_inc(prod_ready, 1)
            nc.vector.memset(rden[:], 0.0).then_inc(d_done, 1)
            dve.wait_ge(lg_psum, 1)
            link(nc.vector.tensor_copy(lg[:].rearrange("p i e -> p (i e)"),
                                       XB[:, 0:TILES * R17]), 2)
            link(nc.vector.tensor_reduce(mx[:], lg[:, :, 0:E], AX.X, ALU.max), 3)
            link(nc.vector.tensor_tensor(ex[:], lg[:, :, 0:E],
                                         mx[:].unsqueeze(2).to_broadcast([P, TILES, E]),
                                         ALU.subtract), 4)
            link(nc.vector.memset(pr[:], -1.0), 5)
            dve.wait_ge(exps, 1)
            link(nc.vector.tensor_reduce(den[:], ex[:], AX.X, ALU.add), 6)
            link(nc.vector.reciprocal(rden[:], den[:]), 7)
            link(nc.vector.tensor_tensor(pr[:, :, 0:E], ex[:],
                                         rden[:].unsqueeze(2).to_broadcast([P, TILES, E]),
                                         ALU.mult), 8)
            for i in range(TILES):
                a = nc.vector.max(top[:, i, :], pr[:, i, 0:E])
            link(a, 9)
            link(nc.vector.memset(top[:, :, TOPK:8], -1.0), 10)
            for i in range(TILES):
                a = nc.vector.match_replace(rep[:, i, :], top[:, i, :], pr[:, i, :], -2.0)
            link(a, 11)
            link(nc.vector.tensor_reduce(den[:], top[:, :, 0:TOPK], AX.X, ALU.add), 12)
            link(nc.vector.reciprocal(rden[:], den[:]), 13)
            link(nc.vector.scalar_tensor_tensor(out=cw[:, :, 0:E], in0=rep[:, :, 0:E], scalar=0.0,
                                                in1=pr[:, :, 0:E], op0=ALU.is_lt, op1=ALU.mult), 14)
            nc.vector.tensor_tensor(cw[:, :, 0:E], cw[:, :, 0:E],
                                    rden[:].unsqueeze(2).to_broadcast([P, TILES, E]),
                                    ALU.mult).then_inc(cw_ready, 1)
            dve.wait_ge(es_done, 1)
            link(nc.vector.tensor_scalar(es[:], es[:], 1.0, None, ALU.add), 15)
            link(nc.vector.reciprocal(cw[:, :, E], es[:]), 16)
            dve.wait_ge(cw_ready, 1)
            link(nc.vector.tensor_copy(cw_hi[:], cw[:]), 17)
            dve.wait_ge(g_act, 1)
            nc.vector.tensor_copy(cw_parts[:, :, 0:R17], cw_hi[:].bitcast(F32)).then_inc(chain, 1)
            nc.vector.tensor_tensor(cw_parts[:, :, LO:LO + R17], cw[:], cw_hi[:].bitcast(F32),
                                    ALU.subtract).then_inc(cw_ready, 1)
            for hf in range(2):
                dve.wait_ge(y_hi_ready, hf + 1)
                nc.vector.tensor_tensor(y_lo[:, :, halves[hf]], yT[:, :, halves[hf]],
                                        y_hi[:, :, halves[hf]].bitcast(F32),
                                        ALU.subtract).then_inc(y_lo_ready, 1)
            dve.wait_ge(ct_psum, 1)
            nc.vector.tensor_copy(cwT[:, 0:HALF], GB[0:2 * LO, :]).then_inc(ct_done, 1)
            nc.vector.tensor_copy(cwT[:, HALF:NT], UB[0:2 * LO, :]).then_inc(ct_done, 1)
            with dve.Fori(0, NCH // 2) as i:
                for k in range(4):
                    u = i * 4 + k
                    dve.wait_ge(g_act, u + 2)
                    dve.wait_ge(u_psum, u + 1)
                    nc.vector.tensor_tensor(prod[:, k % 2, :], UB[:], act_g[:, k % 2, :],
                                            ALU.mult).then_inc(prod_ready, 1)
                    dve.wait_ge(prod_ready, u + 2)
                    dve.wait_ge(c_psum, u + 1)
                    nc.vector.tensor_tensor(hT[:, k % 2, :], CB[:], prod[:, k % 2, :],
                                            ALU.mult).then_inc(h_made, 1)
                    dve.wait_ge(hi_ready, u + 1)
                    nc.vector.tensor_tensor(h_lo[:, k % 2, :], hT[:, k % 2, :],
                                            h_hi[:, k % 2, :].bitcast(F32),
                                            ALU.subtract).then_inc(lo_ready, 1)
            dve.wait_ge(d_done, 2 * NCH + 3)
            for m in range(J):
                nc.vector.tensor_copy(outT[:, m, HALF:NT], acc[2 * m + 1][:]) \
                    .then_inc(out_read[1], 1)
            for n in range(4):
                dve.wait_ge(t_psum, n + 1)
                nc.vector.tensor_tensor(fin[:, 2 * n:2 * n + 2, :].rearrange("p i d -> p (i d)"),
                                        (GB, UB, CB, XB)[n][:],
                                        x1[:, 2 * n:2 * n + 2, :].rearrange("p i d -> p (i d)"),
                                        ALU.add).then_inc(fin_ready, 1)

        @block.gpsimd
        def _(pool):
            nc.gpsimd.memset(cw_parts[:], 0.0).then_inc(g_act, 1)
            nc.gpsimd.memset(hT[:, 1, :], 0.0).then_inc(h_made, 1)
            pool.wait_ge(h_made, 1)
            nc.gpsimd.tensor_copy(h_hi[:, 1, :], hT[:, 1, :]).then_inc(zeros_ready, 1)
            nc.gpsimd.tensor_copy(h_lo[:, 1, :], hT[:, 1, :]).then_inc(lo_ready, 1)
            nc.gpsimd.tensor_copy(w_hi[:, 1, 4 * P:6 * P], hT[:, 1, 0:D]).then_inc(zeros_ready, 1)
            nc.gpsimd.tensor_copy(w_lo[:, 1, 4 * P:6 * P], hT[:, 1, 0:D]).then_inc(zeros_ready, 1)
            with pool.Fori(0, NCH // 2) as i:
                for par in range(2):
                    c = i * 2 + par
                    pool.wait_ge(wf_in[par], 16 * i + 16)
                    pool.wait_ge(d_done, c * 2 + 1)
                    nc.gpsimd.tensor_tensor(waiter[:], wf[0:1, par, 0:1], wf[0:1, par, 0:1], ALU.add)
                    for cols, written, ready in ((slice(0, 4 * P), hi_written, gu_ready),
                                                 (slice(4 * P, 6 * P), d_hi_written, d_ready)):
                        nc.gpsimd.tensor_copy(w_hi[:, par, cols], wf[:, par, cols]) \
                            .then_inc(written, 1)
                        if ready is gu_ready:
                            nc.gpsimd.tensor_copy(select[:, par, :], wf[0:2 * LO, par, 6 * P:7 * P])
                        pool.wait_ge(written, c + 1)
                        nc.gpsimd.tensor_tensor(w_lo[:, par, cols], wf[:, par, cols],
                                                w_hi[:, par, cols].bitcast(F32),
                                                ALU.subtract).then_inc(ready, 1)


def program(nc, dram, out):
    with ExitStack() as late:
        def sb(stack, name, shape):
            return stack.enter_context(nc.sbuf_tensor(name, shape, F32))

        x1 = sb(late, "x1", [P, TILES, D])
        shared = sb(late, "shared", [P, H1 * (J * P + 1)])
        wq = shared[:].rearrange("p (h n) -> p h n", h=H1)
        adaln = adaln_buffers(nc, late, shared)
        with ExitStack() as early:
            gruT = sb(early, "gruT", [P, J, B, LEADING + T])
            QT = sb(early, "QT", [P, 2 + H1, B, QB, H1])
            attn = attention_buffers(nc, early)
            gru_block(nc, dram, wq, gruT, QT, lambda sp: attention_loads(sp, dram, attn, x1))
            attention_block(nc, dram, attn, wq, gruT, QT, x1,
                            lambda sp: adaln_loads(sp, dram, adaln))
        yT = sb(late, "yT", [P, J, NT])
        ffn = ffn_buffers(nc, late)
        adaln_block(nc, dram, adaln, x1, yT, lambda sp: ffn_loads(sp, dram, ffn))
        ffn_block(nc, dram, ffn, x1, yT, out)


def laid_out(x, cond_2048, L0_cond_W_ih, L0_cond_W_hh, L0_cond_b_ih, L0_cond_b_hh, **w):
    def rows_in(a):
        return np.ascontiguousarray(a.reshape(J, P, -1).transpose(1, 0, 2))

    def cols(a):
        return np.ascontiguousarray(a.reshape(-1, P).T)

    def heads_of(w):
        return w.reshape(J, P, H1, DH1).transpose(2, 1, 0, 3).reshape(H1, P, J * DH1)

    tri = np.where(np.tri(P, dtype=bool), 0.0, -1e30).astype(np.float32)
    d = {
        "wq": np.concatenate([heads_of(w["L0_attn_Wq"]), w["L0_attn_bq"].reshape(H1, P, 1)], 2)
        .transpose(1, 0, 2),
        "wkv": np.concatenate([heads_of(w["L0_attn_Wk"]), heads_of(w["L0_attn_Wv"]),
                               w["L0_attn_bk"].reshape(H1, P, 1)], 2),
        "wo": np.concatenate([w["L0_attn_Wo"].reshape(H1, P, D),
                              w["L0_attn_bv"].reshape(H1, P, 1)], 2),
        "bo": w["L0_attn_bo"].reshape(1, D),
        "mask": np.concatenate([tri, np.zeros((P, P), np.float32), tri], 1),
        "xr": np.ascontiguousarray(x.reshape(TILES, P, D).transpose(1, 0, 2)),
        "xT": rows_in(x.reshape(NT, D).T),
        "wih": rows_in(L0_cond_W_ih), "whh": rows_in(L0_cond_W_hh),
        "bias_ih": cols(L0_cond_b_ih), "bias_hh": cols(L0_cond_b_hh),
        "condT": rows_in(cond_2048.T), "ident": np.eye(P, dtype=np.float32),
    }
    def hidden(gu, shared):
        a = np.concatenate([gu.reshape(E * INTER, D), shared])
        return np.concatenate([a, np.zeros((NCH * P - HID, D), a.dtype)])

    def in_chunks(a):
        return a.reshape(NCH, P, J, P).transpose(0, 3, 2, 1).reshape(NCH, P, J * P)

    gu, sgu = w["L0_ffn_expert_gate_up"], w["L0_ffn_shared_gate_up"]
    down = hidden(w["L0_ffn_expert_down"].transpose(0, 2, 1), w["L0_ffn_shared_down"].T)
    owner = np.minimum(np.arange(NCH * P) // INTER, E)
    owner[HID:] = -1
    rows = np.where(np.arange(P) < 64, np.arange(P) % 32, P)
    select = (owner[None, :] == rows[:, None]).astype(np.float32)
    d.update({
        "wemb": rows_in(w["L0_cond2_W_emb"]), "bemb": cols(w["L0_cond2_b_emb"]),
        "gnorm": cols(w["L0_cond2_g_norm"]), "wqkv": rows_in(w["L0_cond2_W_qkv"]),
        "gqk": np.broadcast_to(np.concatenate([np.tile(w["L0_cond2_g_q"], H2),
                                               np.tile(w["L0_cond2_g_k"], H2)]), (P, 2 * D)),
        "wout": rows_in(w["L0_cond2_W_out"]),
        "parity": (np.arange(P)[:, None] // DH2 % 2 == np.arange(2)).astype(np.float32),
        "gw": rows_in(np.concatenate([w["L0_ffn_gate_w"], w["L0_ffn_shared_gate_vec"]]).T),
        "wf": np.concatenate([in_chunks(hidden(gu[:, :INTER], sgu[:SHARED])),
                              in_chunks(hidden(gu[:, INTER:], sgu[SHARED:])),
                              down.reshape(NCH, P, D),
                              select.reshape(P, NCH, P).transpose(1, 0, 2)], 2),
    })
    return {k: np.ascontiguousarray(a) for k, a in d.items()}


def kernel(**inputs):
    import concourse.bacc as bacc
    from concourse.bass_utils import run_bass_kernel_spmd

    arrays = laid_out(**{k: np.asarray(v) for k, v in inputs.items()})
    nc = bacc.Bacc("TRN2", target_bir_lowering=False, num_devices=1)
    dram = {n: nc.dram_tensor(f"in_{n}", a.shape, F32, kind="ExternalInput").ap()
            for n, a in arrays.items()}
    out = nc.dram_tensor("out", [NT, D], F32, kind="ExternalOutput").ap()
    program(nc, dram, out)
    result = run_bass_kernel_spmd(nc, [{f"in_{n}": a for n, a in arrays.items()}], core_ids=[0])
    return result.results[0]["out"].reshape(B, T, D)
```
